# Optimizing a Trainium2 kernel written in Bass

```python
import numpy as np
import jax
import jax.numpy as jnp

def _softmax(x, axis=-1):
    return jax.nn.softmax(x, axis=axis)
def _gelu(x):
    return jax.nn.gelu(x, approximate=True)
def _silu(x):
    return jax.nn.silu(x)
def _sigmoid(x):
    return jax.nn.sigmoid(x)
def _layernorm(x, axis=-1, eps=1e-5):
    m = jnp.mean(x, axis=axis, keepdims=True)
    v = jnp.var(x, axis=axis, keepdims=True)
    return (x - m) / jnp.sqrt(v + eps)
def _scatter_add(tgt, idx, src, axis=0):
    return tgt.at[idx].add(src)
def _segment_sum(src, seg, n):
    return jax.ops.segment_sum(src, seg, n)

kernel_name = 'mk_conv_preact_d2_conv_nchw384_152d0d'

def setup_inputs(seed: int = 0):
    np.random.seed(seed)
    _w = jnp.asarray
    def _rec_inputs():
        import jax
        import jax.numpy as jnp
        _gk = jax.random.key(seed)
        x = -0.0002221 + 1 * jax.random.normal(jax.random.fold_in(_gk, 1), (4, 384, 128, 128), jnp.float32)
        return x
    x = _rec_inputs()
    def _L0_conv_setup():
        import jax, jax.numpy as jnp
        import numpy as np
        from jax import lax
        EPS_LN = 1e-05
        EPS_NORM = 1e-12

        def _layernorm_c(x, w, b):
            mu = jnp.mean(x, axis=1, keepdims=True)
            var = jnp.mean(jnp.square(x - mu), axis=1, keepdims=True)
            return (x - mu) / jnp.sqrt(var + EPS_LN) * w[None, :, None, None] + b[None, :, None, None]

        def _conv1x1(x, w):
            return jnp.einsum('oc,bchw->bohw', w, x)

        def _dwconv3x3(x, w):
            C = x.shape[1]
            return lax.conv_general_dilated(x, w, window_strides=(1, 1), padding=((1, 1), (1, 1)), dimension_numbers=('NCHW', 'OIHW', 'NCHW'), feature_group_count=C)
        key = jax.random.key(seed)
        ks = jax.random.split(key, 8)
        B, C, H, W = (4, 384, 128, 128)
        n_heads = 8
        s = 1.0 / np.sqrt(C)
        inp = {'x': jax.random.normal(ks[0], (B, C, H, W), jnp.float32), 'wq': jax.random.normal(ks[1], (C, C), jnp.float32) * s, 'wk': jax.random.normal(ks[2], (C, C), jnp.float32) * s, 'wv': jax.random.normal(ks[3], (C, C), jnp.float32) * s, 'dwq': jax.random.normal(ks[4], (C, 1, 3, 3), jnp.float32) * (1.0 / 3.0), 'dwk': jax.random.normal(ks[5], (C, 1, 3, 3), jnp.float32) * (1.0 / 3.0), 'dwv': jax.random.normal(ks[6], (C, 1, 3, 3), jnp.float32) * (1.0 / 3.0), 'scale': jnp.ones((n_heads, 1, 1), jnp.float32), 'ln1_w': jnp.ones((C,), jnp.float32), 'ln1_b': jnp.zeros((C,), jnp.float32), 'ln2_w': jnp.ones((C,), jnp.float32), 'ln2_b': jnp.zeros((C,), jnp.float32)}
        return inp
    _L0_conv_all = _L0_conv_setup()
    _L0_conv_in = {k: v for k, v in _L0_conv_all.items() if k in ('wq', 'wk', 'wv', 'dwq', 'dwk', 'dwv', 'scale', 'ln1_w', 'ln1_b', 'ln2_w', 'ln2_b', )}
    del _L0_conv_all

    def _L1_conv_setup():
        import jax, jax.numpy as jnp
        import numpy as np
        B, C, H, W, K = (32, 384, 56, 56, 7)
        EPS = 1e-06
        key = jax.random.key(seed)
        ks = jax.random.split(key, 8)
        return {'x': jax.random.normal(ks[0], (B, C, H, W), dtype=jnp.float32), 'w_avg': jax.random.normal(ks[1], (C, C), dtype=jnp.float32) * 0.05, 'b_avg': jax.random.normal(ks[2], (C,), dtype=jnp.float32) * 0.05, 'w_max': jax.random.normal(ks[3], (C, C), dtype=jnp.float32) * 0.05, 'b_max': jax.random.normal(ks[4], (C,), dtype=jnp.float32) * 0.05, 'w_mix': jax.random.normal(ks[5], (C, K * K), dtype=jnp.float32) * 0.05, 'gamma': jax.random.normal(ks[6], (C, 1, 1), dtype=jnp.float32), 'beta': jax.random.normal(ks[7], (C, 1, 1), dtype=jnp.float32)}
    _L1_conv_all = _L1_conv_setup()
    _L1_conv_in = {k: v for k, v in _L1_conv_all.items() if k in ('w_avg', 'b_avg', 'w_max', 'b_max', 'w_mix', 'gamma', 'beta', )}
    del _L1_conv_all

    return {
        "x": x,
        "L0_conv_wq": _L0_conv_in["wq"],
        "L0_conv_wk": _L0_conv_in["wk"],
        "L0_conv_wv": _L0_conv_in["wv"],
        "L0_conv_dwq": _L0_conv_in["dwq"],
        "L0_conv_dwk": _L0_conv_in["dwk"],
        "L0_conv_dwv": _L0_conv_in["dwv"],
        "L0_conv_scale": _L0_conv_in["scale"],
        "L0_conv_ln1_w": _L0_conv_in["ln1_w"],
        "L0_conv_ln1_b": _L0_conv_in["ln1_b"],
        "L0_conv_ln2_w": _L0_conv_in["ln2_w"],
        "L0_conv_ln2_b": _L0_conv_in["ln2_b"],
        "L1_conv_w_avg": _L1_conv_in["w_avg"],
        "L1_conv_b_avg": _L1_conv_in["b_avg"],
        "L1_conv_w_max": _L1_conv_in["w_max"],
        "L1_conv_b_max": _L1_conv_in["b_max"],
        "L1_conv_w_mix": _L1_conv_in["w_mix"],
        "L1_conv_gamma": _L1_conv_in["gamma"],
        "L1_conv_beta": _L1_conv_in["beta"],
    }

def reference(x, L0_conv_wq, L0_conv_wk, L0_conv_wv, L0_conv_dwq, L0_conv_dwk, L0_conv_dwv, L0_conv_scale, L0_conv_ln1_w, L0_conv_ln1_b, L0_conv_ln2_w, L0_conv_ln2_b, L1_conv_w_avg, L1_conv_b_avg, L1_conv_w_max, L1_conv_b_max, L1_conv_w_mix, L1_conv_gamma, L1_conv_beta):
    import jax
    import jax.numpy as jnp
    def _L0_conv_ref(x, wq, wk, wv, dwq, dwk, dwv, scale, ln1_w, ln1_b, ln2_w, ln2_b):
        import jax, jax.numpy as jnp
        import numpy as np
        from jax import lax
        EPS_LN = 1e-05
        EPS_NORM = 1e-12

        def _layernorm_c(x, w, b):
            mu = jnp.mean(x, axis=1, keepdims=True)
            var = jnp.mean(jnp.square(x - mu), axis=1, keepdims=True)
            return (x - mu) / jnp.sqrt(var + EPS_LN) * w[None, :, None, None] + b[None, :, None, None]

        def _conv1x1(x, w):
            return jnp.einsum('oc,bchw->bohw', w, x)

        def _dwconv3x3(x, w):
            C = x.shape[1]
            return lax.conv_general_dilated(x, w, window_strides=(1, 1), padding=((1, 1), (1, 1)), dimension_numbers=('NCHW', 'OIHW', 'NCHW'), feature_group_count=C)
        B, C, H, W = x.shape
        n_heads = scale.shape[0]
        d = C // n_heads
        L = H * W
        x_norm = _layernorm_c(x, ln1_w, ln1_b)
        q = _dwconv3x3(_conv1x1(x_norm, wq), dwq)
        k = _dwconv3x3(_conv1x1(x_norm, wk), dwk)
        v = _dwconv3x3(_conv1x1(x_norm, wv), dwv)
        q = q.reshape(B, n_heads, d, L)
        k = k.reshape(B, n_heads, d, L)
        v = v.reshape(B, n_heads, d, L)
        q = q / jnp.maximum(jnp.linalg.norm(q, axis=-1, keepdims=True), EPS_NORM)
        k = k / jnp.maximum(jnp.linalg.norm(k, axis=-1, keepdims=True), EPS_NORM)
        attn = jnp.einsum('bndl,bnel->bnde', q, k) * scale[None]
        attn = jax.nn.softmax(attn, axis=-1)
        out = jnp.einsum('bnde,bnel->bndl', attn, v)
        out = out.reshape(B, C, H, W)
        return _layernorm_c(out, ln2_w, ln2_b)

    def _L1_conv_ref(x, w_avg, b_avg, w_max, b_max, w_mix, gamma, beta):
        import jax, jax.numpy as jnp
        import numpy as np
        B, C, H, W, K = (32, 384, 56, 56, 7)
        EPS = 1e-06
        b, c, h, w = x.shape
        k = int(np.sqrt(w_mix.shape[1]))
        pad = k // 2
        x_avg = x.mean(axis=(2, 3))
        x_max = x.max(axis=(2, 3))
        x_w = jax.nn.gelu(x_avg @ w_avg.T + b_avg + x_max @ w_max.T + b_max, approximate=False)
        x_w = x_w[:, :, None] * w_mix[None, :, :]
        xr = x_w.reshape(b, c, k, k)
        Gx = jnp.sqrt(jnp.sum(xr * xr, axis=(2, 3), keepdims=True))
        Nx = Gx / (Gx.mean(axis=1, keepdims=True) + EPS)
        kern = gamma[None] * (xr * Nx) + beta[None]
        x_flat = x.reshape(1, b * c, h, w)
        w_flat = kern.reshape(b * c, 1, k, k)
        out = jax.lax.conv_general_dilated(x_flat, w_flat, window_strides=(1, 1), padding=[(pad, pad), (pad, pad)], feature_group_count=b * c, dimension_numbers=('NCHW', 'OIHW', 'NCHW'))
        return out.reshape(b, c, h, w)

    def _gn(v, G=32, eps=1e-5):
        B_, C_, H_, W_ = v.shape
        g = v.reshape(B_, G, C_ // G, H_, W_)
        m = jnp.mean(g, axis=(2, 3, 4), keepdims=True)
        s = jnp.var(g, axis=(2, 3, 4), keepdims=True)
        return ((g - m) / jnp.sqrt(s + eps)).reshape(v.shape)

    def _ln_c(v, eps=1e-6):
        m = jnp.mean(v, axis=1, keepdims=True)
        s = jnp.var(v, axis=1, keepdims=True)
        return (v - m) / jnp.sqrt(s + eps)

    def _ln_t(v, eps=1e-5):
        m = jnp.mean(v, axis=-1, keepdims=True)
        s = jnp.var(v, axis=-1, keepdims=True)
        return (v - m) / jnp.sqrt(s + eps)

    def _to_tokens(v):
        B_, C_, H_, W_ = v.shape
        return v.reshape(B_, C_, H_ * W_).transpose(0, 2, 1)
    def _from_tokens(t, like):
        B_, C_, H_, W_ = like.shape
        return t.transpose(0, 2, 1).reshape(B_, C_, H_, W_)

    x = x + _L0_conv_ref(_gn(x), L0_conv_wq, L0_conv_wk, L0_conv_wv, L0_conv_dwq, L0_conv_dwk, L0_conv_dwv, L0_conv_scale, L0_conv_ln1_w, L0_conv_ln1_b, L0_conv_ln2_w, L0_conv_ln2_b)
    x = x + _L1_conv_ref(_gn(x), L1_conv_w_avg, L1_conv_b_avg, L1_conv_w_max, L1_conv_b_max, L1_conv_w_mix, L1_conv_gamma, L1_conv_beta)
    return x


_drawn_inputs = setup_inputs


def setup_inputs(seed=0):
    import zlib

    import numpy as np

    out = dict(_drawn_inputs(seed))
    spreads = {'L0_conv_scale': (1.0, 0.6),
     'L0_conv_ln1_w': (1.0, 0.2),
     'L0_conv_ln1_b': (0.0, 0.1),
     'L0_conv_ln2_w': (1.0, 0.2),
     'L0_conv_ln2_b': (0.0, 0.1)}
    factors = {'L0_conv_wk': 2.82,
     'L0_conv_dwq': 2.711,
     'L0_conv_dwk': 2.724,
     'L1_conv_w_avg': 4.679,
     'L1_conv_b_avg': 7.706,
     'L1_conv_b_max': 6.314}
    for name, (base, spread) in spreads.items():
        noise = np.random.default_rng([zlib.crc32(name.encode()), seed]).standard_normal(out[name].shape)
        drawn = base * np.exp(spread * noise) if base else spread * noise
        out[name] = jnp.asarray(drawn.astype(out[name].dtype))
    for name, factor in factors.items():
        out[name] = (out[name] * factor).astype(out[name].dtype)
    return out
```

```python
from contextlib import ExitStack

import numpy as np

import concourse.bass as bass
from concourse import mybir

F32 = mybir.dt.float32
ALU = mybir.AluOpType
ACT = mybir.ActivationFunctionType
AX = mybir.AxisListType

P = 128
B, C, H, W = 4, 384, 128, 128
HW = H * W
G = C // P
GN_SIZE = C // 32
HEADS = 8
HEAD = C // HEADS
EPS_GN = 1e-5
EPS_LN = 1e-5
EPS_NORM = 1e-12
EPS_NX = 1e-6

RB = 8
NB = H // RB
PX = RB * W
TILE = 512
HALVES = PX // TILE
ROWS_T = TILE // W
M9 = 3 * G
U_TILES = M9 * HALVES
TAPS = [(dy, dx) for dy in range(3) for dx in range(3) if (dy, dx) != (1, 1)]
OPS = 3 * len(TAPS)
WIN = [((P * a) // HEAD * HEAD, -(-(P * (a + 1)) // HEAD) * HEAD) for a in range(G)]
WOFF = [sum(hi - lo for lo, hi in WIN[:a]) for a in range(G)]
WCOLS = sum(hi - lo for lo, hi in WIN)

T2 = HW // TILE
LOADS2 = T2 // HALVES

K7 = 7
PAD = K7 // 2
FOLD = -(-P // K7)
BAND = FOLD * K7
CG = 4
NCG = C // CG
XP = W + 2 * PAD
GN_COLS = 4096
GN_LOADS = HW // GN_COLS

CH_NAMES = ["ln1_w", "ln1_b", "ln2_w", "ln2_b", "scale", "b_avg", "b_max", "gamma", "beta"]


def build(nc, x, w_qkv, dw_qkv, chans, w_avg, w_max, w_mix_ch, w_mix_ky,
          ident_in, member_in, headmask_in, band_in, sel_in, out):
    ctx = ExitStack()
    with ctx:
        def sb(name, shape):
            return ctx.enter_context(nc.sbuf_tensor(name, shape, F32))

        def sem(name):
            return ctx.enter_context(nc.semaphore(name))

        v_dram = nc.dram_tensor("v_scratch", (B, C, HW), F32, kind="Internal").ap()
        x1_dram = nc.dram_tensor("x1_scratch", (B, C, HW), F32, kind="Internal").ap()

        ps = ctx.enter_context(nc.psum_tensor("ps", [P, 8, 512], F32))

        ident = sb("ident", [P, P])
        ones = sb("ones", [P, P])
        mean_c = sb("mean_c", [P, P])
        zero1 = sb("zero1", [P, 1])
        eps_gn = sb("eps_gn", [P, 1])
        member = sb("member", [P, G, C])
        ch = sb("ch", [P, len(CH_NAMES), G])
        par = {n: ch[:, i, :] for i, n in enumerate(CH_NAMES)}
        dw = sb("dw", [P, M9, 9])
        bias_u = sb("bias_u", [P, M9])
        gn_st = sb("gn_st", [P, G, B, 2])
        gn_tmp = sb("gn_tmp", [P, G, B])
        gn_mean = sb("gn_mean", [P, G, B])
        gn_r = sb("gn_r", [P, G, B])
        gn_nb = sb("gn_nb", [P, G, B])
        ch_mean = sb("ch_mean", [P, G, B])
        ch_max = sb("ch_max", [P, G, B])
        aggr = sb("aggr", [P, G, 2])
        mu2 = sb("mu2", [P, RB])
        var = sb("var", [P, RB])
        std = sb("std", [P, RB])
        rstd = sb("rstd", [P, RB])
        norms = sb("norms", [P, 2, G, NB])
        norm = sb("norm", [P, 2, G])
        rnorm = sb("rnorm", [P, 2, G])
        rqs = sb("rqs", [P, G])
        smx = sb("smx", [P, G])
        ssum = sb("ssum", [P, G])
        rsum = sb("rsum", [P, G])
        std2 = sb("std2", [P, 4, ROWS_T])
        rstd2 = sb("rstd2", [P, 4, ROWS_T])
        diag = sb("diag", [P, G, P])
        scores = sb("scores", [P, WCOLS])
        hmask = sb("hmask", [P, WCOLS])
        cur = sb("cur", [P, 2, G])
        at = sb("at", [P, G, C])

        arena = sb("arena", [P, 47300])

        def carve(start, *dims):
            n = int(np.prod(dims))
            v = arena[:, start:start + n]
            names = "abcd"[:len(dims)]
            if len(dims) > 1:
                v = v.rearrange(f"p ({' '.join(names)}) -> p {' '.join(names)}",
                                **{k: d for k, d in zip(names, dims)})
            return v, start + n

        o = 0
        xin, o = carve(o, 2, G, PX)
        o_ysq = o
        ysq, o = carve(o, G, PX)
        o_ubuf = o
        ubuf, o = carve(o, M9, RB + 3, W + 2)
        o_acc = o
        accs, o = carve(o, 2, 2 * G, (RB + 1) * W)
        accv, o = carve(o, G, (RB + 1) * W)
        o_end_acc = o
        wc, o = carve(o, G, M9 * P)
        o_qkT = o
        qkT, o = carve(o, 2, 2, C)
        junk, o = carve(o, 2, (RB + 1) * W)
        end_l0 = o
        assert o <= 47300, o
        wraw, _ = carve(o_acc, G, M9 * P)
        gnbn, _ = carve(o_acc + G * M9 * P, G, B, HW // 512, 6)
        gnx, o = carve(0, 2, GN_COLS)
        assert o <= o_ubuf
        a_full, o = carve(o_qkT, G, C)
        a_cent, o = carve(o, G, C)
        rk_row, o = carve(o, C)
        assert o <= end_l0
        o = o_acc
        vin, o = carve(o, 2, G, PX)
        ow, o = carve(o, 4, G, TILE)
        osq, o = carve(o, 2, G, TILE)
        assert o <= o_end_acc, (o, o_end_acc)
        bn2, o2 = carve(o_ysq, G, T2, 6)
        mx2, o2 = carve(o2, G, T2)
        o = 0
        wfold, o = carve(o, C, K7 + 1, K7)
        chb, o = carve(o, 4, C, B)
        band, o = carve(o, BAND)
        toep, o = carve(o, 2, K7 + 1, BAND)
        o_tmp = o
        xg, o = carve(o, 2, B, CG, W)
        og, o = carve(o, 2, B, CG, W)
        ypad, o = carve(o, 2, B, XP)
        zpad, o = carve(o, 2, B, XP)
        s2, o = carve(o, B, XP)
        s4, o = carve(o, B, XP)
        s6, o = carve(o, B, W)
        box, o = carve(o, 2, B, W)
        assert o <= 47300, o
        wT, o_l1 = carve(o_tmp, 2, G, C)
        selk, o_l1 = carve(o_l1, K7, P)
        wky, o_l1 = carve(o_l1, C * K7)
        d4, o_l1 = carve(o_l1, 2, P, B)
        wmx, o_l1 = carve(o_l1, G, K7 * K7)
        wsq, o_l1 = carve(o_l1, G, K7 * K7)
        assert o_l1 <= o, o_l1
        l1v = sb("l1v", [P, 16, G, B])
        l1s = sb("l1s", [P, 4, G])
        mrow = sb("mrow", [P, 2, B])

        par_in = sem("par_in")
        const_set = sem("const_set")
        passed = sem("passed")
        gn_in = [sem(f"gn_in{i}") for i in range(2)]
        gn_used = sem("gn_used")
        chain = sem("chain")
        wraw_scaled = sem("wraw_scaled")
        wmean_ready = sem("wmean_ready")
        wc_ready = sem("wc_ready")
        gst_ready = sem("gst_ready")
        gsum_ready = sem("gsum_ready")
        gvar_ready = sem("gvar_ready")
        gstd_ready = sem("gstd_ready")
        gn_ready = sem("gn_ready")
        cur_set = sem("cur_set")
        x_in = [sem(f"x_in{i}") for i in range(2)]
        y_ready = sem("y_ready")
        stat_ready = sem("stat_ready")
        mu2_ready = sem("mu2_ready")
        var_ready = sem("var_ready")
        std_ready = sem("std_ready")
        rstd_ready = sem("rstd_ready")
        bc_ready = sem("bc_ready")
        xn_ready = sem("xn_ready")
        u_ready = sem("u_ready")
        u_evicted = sem("u_evicted")
        halo_ready = sem("halo_ready")
        centre_ready = sem("centre_ready")
        tap_done = sem("tap_done")
        v_stored = [sem(f"v_stored{g}") for g in range(G)]
        qkT_ready = sem("qkT_ready")
        qkT_evicted = sem("qkT_evicted")
        gram_done = sem("gram_done")
        sq_done = sem("sq_done")
        nsum_ready = sem("nsum_ready")
        nroot_ready = sem("nroot_ready")
        diag_ready = sem("diag_ready")
        rk_ready = sem("rk_ready")
        rk_copied = sem("rk_copied")
        smx_ready = sem("smx_ready")
        exp_done = sem("exp_done")
        a_zero = sem("a_zero")
        a_ready = sem("a_ready")
        cm_ready = sem("cm_ready")
        ac_ready = sem("ac_ready")
        at_ready = sem("at_ready")
        at_copied = sem("at_copied")
        small = sem("small")
        x2_in = [sem(f"x2_in{i}") for i in range(2)]
        v2_in = [sem(f"v2_in{i}") for i in range(2)]
        o_ready = sem("o_ready")
        osq_ready = sem("osq_ready")
        o_evicted = sem("o_evicted")
        ostat_ready = sem("ostat_ready")
        ostd_ready = sem("ostd_ready")
        orstd_ready = sem("orstd_ready")
        obc_ready = sem("obc_ready")
        on_done = sem("on_done")
        x1_ready = sem("x1_ready")
        bn_done = sem("bn_done")
        x1_stored = [sem(f"x1_stored{i}") for i in range(2)]
        batch_done = sem("batch_done")
        l1_in = sem("l1_in")
        wf_ready = sem("wf_ready")
        wf_copied = sem("wf_copied")
        beta_ready = sem("beta_ready")
        beta_set = sem("beta_set")
        pool_ready = sem("pool_ready")
        gate_ready = sem("gate_ready")
        gate_in = sem("gate_in")
        gelu_done = sem("gelu_done")
        wnorm_done = sem("wnorm_done")
        gx2_ready = sem("gx2_ready")
        gx_ready = sem("gx_ready")
        gxm_ready = sem("gxm_ready")
        d4_ready = sem("d4_ready")
        chb_ready = sem("chb_ready")
        chb_set = sem("chb_set")
        l1_ready = sem("l1_ready")
        pads_zero = sem("pads_zero")
        xg_in = [sem(f"xg_in{i}") for i in range(2)]
        yz_ready = sem("yz_ready")
        toep_ready = sem("toep_ready")
        box_step = sem("box_step")
        box_ready = sem("box_ready")
        conv_ready = sem("conv_ready")
        og_ready = sem("og_ready")
        og_stored = [sem(f"og_stored{i}") for i in range(2)]

        wqk = wc.rearrange("p k (m c) -> p k m c", c=P)
        xr = x.rearrange("b (g p) h w -> b p g (h w)", p=P)
        xg_n = x.rearrange("b (g p) h w -> (b g) p (h w)", p=P)
        vr = v_dram.rearrange("b (g p) n -> b p g n", p=P)
        x1r = x1_dram.rearrange("b (g p) n -> b p g n", p=P)
        x1y = x1_dram.rearrange("b c (y w) -> y b c w", w=W)
        outy = out.rearrange("b c y w -> y b c w")

        def of_image(ap, b):
            return ap[bass.ds(b, 1)].rearrange("a p g n -> (a p) g n")

        def rows_of(i):
            return (1 if i == 0 else 0), (RB + 1 if i == NB - 1 else RB)

        def blocks(eng, b, body):
            body(b * NB, 0, 0, b * (NB // 2))
            with eng.Fori(0, (NB - 2) // 2) as k:
                body(b * NB + k * 2 + 1, None, 1, b * (NB // 2) + k, k * 2 + 1)
                body(b * NB + k * 2 + 2, None, 0, b * (NB // 2) + k + 1, k * 2 + 2)
            body(b * NB + (NB - 1), NB - 1, 1, b * (NB // 2) + (NB // 2 - 1))

        pooled = (l1v[:, 0], l1v[:, 1])
        gxv = l1v[:, 6]
        SMALL = 9

        block = ctx.enter_context(nc.Block())

        @block.sync
        def _(sp):
            for dst, src in ((ident, ident_in), (member, member_in), (ch, chans), (dw, dw_qkv),
                             (wraw, w_qkv), (hmask, headmask_in)):
                sp.dma_start(dst[:], src).then_inc(par_in, 16)
            with sp.Fori(0, B * G) as n:
                for q in range(GN_LOADS):
                    sp.wait_ge(gn_used, n * GN_LOADS + (q + 1))
                    sp.sem_inc(passed, 1)
                    sp.dma_start(gnx[:, q % 2, :],
                                 xg_n[bass.ds(n, 1), :, q * GN_COLS:(q + 1) * GN_COLS].rearrange("a p n -> (a p) n")
                                 ).then_inc(gn_in[q % 2], 16)
            sp.wait_ge(gn_used, B * G * GN_LOADS + 2)
            sp.wait_ge(wc_ready, 2)
            with sp.Fori(0, B) as b:
                xb, vb, x1b = of_image(xr, b), of_image(vr, b), of_image(x1r, b)
                for i in range(2):
                    sp.dma_start(xin[:, i], xb[:, :, i * PX:(i + 1) * PX]).then_inc(x_in[i], 16)

                def first(n, i, odd, seen, idx=None):
                    r0, r1 = rows_of(i)
                    for g in range(G):
                        sp.wait_ge(tap_done, n * (G * OPS) + OPS * (g + 1))
                        sp.sem_inc(passed, 1)
                        if i is None:
                            dst = vb[:, g:g + 1, bass.ds(idx * PX - W, RB * W)]
                        else:
                            dst = vb[:, g:g + 1, i * PX - W + r0 * W:i * PX - W + r1 * W]
                        sp.dma_start(dst.rearrange("p a n -> p (a n)"), accv[:, g, r0 * W:r1 * W]
                                     ).then_inc(v_stored[g], 16)
                        if g == 0 and i is None:
                            load(n, odd, idx)
                        elif g == 0 and i == 0:
                            sp.wait_ge(u_ready, n * U_TILES + U_TILES)
                            sp.sem_inc(passed, 1)
                            sp.dma_start(xin[:, 0], xb[:, :, 2 * PX:3 * PX]).then_inc(x_in[0], 16)

                def load(n, odd, idx):
                    sp.wait_ge(u_ready, n * U_TILES + U_TILES)
                    sp.sem_inc(passed, 1)
                    sp.dma_start(xin[:, odd], xb[:, :, bass.ds(idx * PX + 2 * PX, PX)]).then_inc(x_in[odd], 16)

                def first_no_load(n, i, odd, seen, idx):
                    r0, r1 = rows_of(i)
                    for g in range(G):
                        sp.wait_ge(tap_done, n * (G * OPS) + OPS * (g + 1))
                        sp.sem_inc(passed, 1)
                        sp.dma_start(vb[:, g:g + 1, idx * PX - W + r0 * W:idx * PX - W + r1 * W].rearrange("p a n -> p (a n)"),
                                     accv[:, g, r0 * W:r1 * W]).then_inc(v_stored[g], 16)

                first(b * NB, 0, 0, None)
                with sp.Fori(0, (NB - 4) // 2) as k:
                    first(b * NB + k * 2 + 1, None, 1, None, k * 2 + 1)
                    first(b * NB + k * 2 + 2, None, 0, None, k * 2 + 2)
                first(b * NB + (NB - 3), None, 1, None, NB - 3)
                first_no_load(b * NB + (NB - 2), None, 0, None, NB - 2)
                first_no_load(b * NB + (NB - 1), NB - 1, 1, None, NB - 1)

                def load2(slot, cols):
                    sp.dma_start(xin[:, slot], xb[:, :, cols]).then_inc(x2_in[slot], 16)
                    sp.dma_start(vin[:, slot], vb[:, :, cols]).then_inc(v2_in[slot], 16)

                sp.wait_ge(u_ready, b * (NB * U_TILES) + NB * U_TILES)
                sp.sem_inc(passed, 1)
                sp.wait_ge(gram_done, b * H + (H + 2))
                sp.sem_inc(passed, 1)
                sp.wait_ge(sq_done, b * (2 * G * NB) + (2 * G * NB + 2))
                sp.sem_inc(passed, 1)
                for g in range(G):
                    sp.wait_ge(v_stored[g], b * (16 * NB) + 16 * (NB + 1))
                    sp.sem_inc(passed, 1)
                for s in range(2):
                    load2(s, slice(s * PX, (s + 1) * PX))

                def second(k, last):
                    for s in range(2):
                        sp.wait_ge(x1_ready, b * (3 * T2) + k * (12) + (6 * (s + 1)))
                        sp.sem_inc(passed, 1)
                        cols = bass.ds(k * (2 * PX) + s * PX, PX)
                        sp.dma_start(x1b[:, :, cols], xin[:, s]).then_inc(x1_stored[s], 16)
                        if last:
                            continue
                        sp.wait_ge(bn_done, b * T2 + k * 4 + (2 * (s + 1)))
                        sp.sem_inc(passed, 1)
                        sp.wait_ge(x1_stored[s], b * (16 * LOADS2 // 2) + k * 16 + 16)
                        sp.sem_inc(passed, 1)
                        load2(s, bass.ds(k * (2 * PX) + (s + 2) * PX, PX))

                with sp.Fori(0, LOADS2 // 2 - 1) as k:
                    second(k, False)
                second(LOADS2 // 2 - 1, True)
                sp.wait_ge(batch_done, b + 1)
                sp.sem_inc(passed, 1)
                for s in range(2):
                    sp.wait_ge(x1_stored[s], b * (8 * LOADS2) + 8 * LOADS2)
                    sp.sem_inc(passed, 1)

            for dst, src in ((wT[:, 0], w_avg), (wT[:, 1], w_max), (wmx, w_mix_ch), (band, band_in)):
                sp.dma_start(dst, src).then_inc(l1_in, 16)
            sp.dma_start(selk[0:K7], sel_in).then_inc(l1_in, 16)
            sp.dma_start(wky[0:K7], w_mix_ky).then_inc(l1_in, 16)
            sp.wait_ge(l1_ready, 2)

            def load_x1(s, cols):
                for b in range(B):
                    sp.dma_start(xg[:, s, b], x1y[:, b, cols, :]).then_inc(xg_in[s], 16)

            for s in range(2):
                load_x1(s, slice(s * CG, (s + 1) * CG))

            def groups(k, last):
                for s in range(2):
                    sp.wait_ge(og_ready, k * (2 * CG) + CG * (s + 1) + 2)
                    sp.sem_inc(passed, 1)
                    for b in range(B):
                        sp.dma_start(outy[:, b, bass.ds(k * (2 * CG) + s * CG, CG), :], og[:, s, b]).then_inc(og_stored[s], 16)
                    if not last:
                        load_x1(s, bass.ds(k * (2 * CG) + (s + 2) * CG, CG))

            with sp.Fori(0, NCG // 2 - 1) as k:
                groups(k, False)
            groups(NCG // 2 - 1, True)
            for s in range(2):
                sp.wait_ge(og_stored[s], 16 * B * (NCG // 2 + 1))

        @block.gpsimd
        def _(pool):
            nc.gpsimd.memset(ones[:], 1.0).then_inc(const_set, 1)
            nc.gpsimd.memset(mean_c[:], 1.0 / C).then_inc(const_set, 1)
            nc.gpsimd.memset(zero1[:], 0.0).then_inc(const_set, 1)
            nc.gpsimd.memset(eps_gn[:], EPS_GN).then_inc(const_set, 1)
            nc.gpsimd.memset(ubuf, 0.0).then_inc(const_set, 1)
            pool.wait_ge(const_set, 5)
            for g in range(G):
                pool.sem_inc(halo_ready, 1)

            def halo(n, i, odd, seen, idx=None):
                for g in range(G):
                    pool.wait_ge(tap_done, n * (G * OPS) + OPS * (g + 1))
                    pool.sem_inc(passed, 1)
                    rows = ubuf[:, 3 * g:3 * g + 3]
                    if i == NB - 1:
                        nc.gpsimd.memset(rows[:, :, 0:2, 1:W + 1], 0.0).then_inc(halo_ready, 1)
                    else:
                        nc.gpsimd.tensor_copy(rows[:, :, 0:2, 1:W + 1], rows[:, :, RB:RB + 2, 1:W + 1]).then_inc(halo_ready, 1)

            with pool.Fori(0, B) as b:
                blocks(pool, b, halo)
            pool.wait_ge(l1_ready, 2)
            nc.gpsimd.memset(ypad, 0.0).then_inc(pads_zero, 1)
            nc.gpsimd.memset(zpad, 0.0).then_inc(pads_zero, 1)

        @block.scalar
        def _(act):
            A = nc.scalar.activation
            act.sem_inc(u_evicted, 3)
            act.sem_inc(sq_done, 2)
            act.sem_inc(qkT_evicted, 1)
            act.sem_inc(o_evicted, 2)
            act.sem_inc(ostd_ready, 1)
            act.sem_inc(wf_copied, 2)
            act.sem_inc(chb_set, 2)
            act.wait_ge(const_set, 5)

            def group_root(step):
                act.wait_ge(gvar_ready, step)
                A(gn_r[:], gn_tmp[:], ACT.Sqrt, bias=eps_gn[:, 0:1]).then_inc(gstd_ready, 1)

            group_root(1)

            def make_y(n, odd, seen):
                act.wait_ge(x_in[odd], seen * 16 + 16)
                for g in range(G):
                    A(ysq[:, g], xin[:, odd, g], ACT.Square, bias=cur[:, 1, g:g + 1], scale=cur[:, 0, g:g + 1])
                for g in range(G):
                    ins = A(xin[:, odd, g], xin[:, odd, g], ACT.Identity, bias=cur[:, 1, g:g + 1], scale=cur[:, 0, g:g + 1])
                ins.then_inc(y_ready, 1)

            def mean_squared(n):
                act.wait_ge(stat_ready, n + 1)
                A(mu2[:], ps[:, 3, 0:RB], ACT.Square, bias=zero1[:, 0:1]).then_inc(mu2_ready, 1)

            def root(n):
                act.wait_ge(var_ready, n + 1)
                A(std[:], var[:], ACT.Sqrt, bias=eps_gn[:, 0:1]).then_inc(std_ready, 1)

            def evict_u(n, g, i, odd):
                r0, r1 = rows_of(i)
                act.wait_ge(halo_ready, n * G + (g + 1))
                for q in range(3):
                    m = 3 * g + q
                    for j in range(HALVES):
                        t = m * HALVES + j
                        act.wait_ge(u_ready, n * U_TILES + (t + 1))
                        A(ubuf[:, m, 2 + ROWS_T * j:2 + ROWS_T * (j + 1), 1:W + 1],
                          ps[:, t % 3, :].rearrange("p (r w) -> p r w", w=W),
                          ACT.Identity, bias=bias_u[:, m:m + 1]).then_inc(u_evicted, 1)
                    act.wait_ge(u_evicted, n * U_TILES + (m + 1) * HALVES + 3)
                    if q == 2:
                        act.wait_ge(v_stored[g], n * 16 + 16)
                        dst = accv[:, g]
                    else:
                        dst = accs[:, odd, 2 * g + q]
                    A(dst[:, r0 * W:r1 * W].rearrange("p (r w) -> p r w", w=W), ubuf[:, m, r0 + 1:r1 + 1, 1:W + 1],
                      ACT.Copy, scale=dw[:, m, 4:5]).then_inc(centre_ready, 1)

            def squares_and_turns(n, i, odd, idx):
                r0, r1 = rows_of(i)
                act.wait_ge(tap_done, n * (G * OPS) + G * OPS)
                act.sem_inc(passed, 1)
                for c in range(2 * G):
                    g, q = c // 2, c % 2
                    col = norms[:, q, g, bass.ds(idx, 1)] if i is None else norms[:, q, g, i:i + 1]
                    act.wait_ge(sq_done, n * (2 * G) + (c + 1))
                    act.sem_inc(passed, 1)
                    A(junk[:, c % 2, r0 * W:r1 * W], accs[:, odd, c, r0 * W:r1 * W], ACT.Square, bias=zero1[:, 0:1],
                      accum_out=col).then_inc(sq_done, 1)
                for r in range(r0, r1):
                    act.wait_ge(qkT_ready, n * RB + r)
                    act.wait_ge(gram_done, n * RB + r)
                    A(qkT[:, r % 2, 0], ps[:, 5, 0:C], ACT.Copy)
                    A(qkT[:, r % 2, 1], ps[:, 6, 0:C], ACT.Copy).then_inc(qkT_evicted, 1)

            with act.Fori(0, B) as b:
                act.wait_ge(cur_set, b + 1)
                make_y(b * NB, 0, b * (NB // 2))
                mean_squared(b * NB)
                root(b * NB)

                def first(n, i, odd, seen, idx=None):
                    evict_u(n, 0, i, odd)
                    if i != NB - 1:
                        make_y(n + 1, 1 - odd, seen + (1 if odd else 0))
                        mean_squared(n + 1)
                    evict_u(n, 1, i, odd)
                    if i == 0:
                        pass
                    elif i is None:
                        before(n, odd, idx)
                    else:
                        squares_and_turns(n - 1, None, 1 - odd, NB - 2)
                    if i != NB - 1:
                        root(n + 1)
                    evict_u(n, 2, i, odd)

                def before(n, odd, idx):
                    squares_and_turns(n - 1, PREV[0], 1 - odd, idx - 1)

                PREV = [0]
                first(b * NB, 0, 0, b * (NB // 2))
                first(b * NB + 1, None, 1, b * (NB // 2), 1)
                PREV[0] = None
                with act.Fori(0, (NB - 4) // 2) as k:
                    first(b * NB + k * 2 + 2, None, 0, b * (NB // 2) + k + 1, k * 2 + 2)
                    first(b * NB + k * 2 + 3, None, 1, b * (NB // 2) + k + 1, k * 2 + 3)
                first(b * NB + (NB - 2), None, 0, b * (NB // 2) + (NB // 2 - 1), NB - 2)
                first(b * NB + (NB - 1), NB - 1, 1, b * (NB // 2) + (NB // 2 - 1))
                squares_and_turns(b * NB + (NB - 1), NB - 1, 1, NB - 1)

                act.wait_ge(nsum_ready, b + 1)
                A(norm[:], norm[:], ACT.Sqrt, bias=zero1[:, 0:1]).then_inc(nroot_ready, 1)
                act.wait_ge(rk_ready, b + 1)
                A(rk_row, ps[:, 0, 0:C], ACT.Copy).then_inc(rk_copied, 1)
                act.wait_ge(smx_ready, b + 1)
                for a in range(G):
                    cols = slice(WOFF[a], WOFF[a] + WIN[a][1] - WIN[a][0])
                    A(scores[:, cols], scores[:, cols], ACT.Exp, bias=smx[:, a:a + 1], accum_out=ssum[:, a:a + 1]
                      ).then_inc(exp_done, 1)
                act.wait_ge(at_ready, b + 1)
                A(at[:], ps[:, 2:5, 0:C], ACT.Copy).then_inc(at_copied, 1)

                with act.Fori(0, T2 // 4) as k:
                    for j in range(4):
                        T = b * T2 + k * 4 + j
                        s = 3 * (j % 2)
                        act.wait_ge(o_ready, T + 1)
                        A(osq[:, j % 2], ps[:, s:s + 3, :], ACT.Square, bias=zero1[:, 0:1]).then_inc(osq_ready, 1)
                        act.wait_ge(on_done, T + 1)
                        for a in range(G):
                            ins = A(ow[:, j, a], ps[:, s + a, :], ACT.Copy, scale=par["ln2_w"][:, a:a + 1])
                        ins.then_inc(o_evicted, 1)
                        act.wait_ge(ostat_ready, T + 1)
                        A(std2[:, j], ps[:, 6, 0:ROWS_T], ACT.Sqrt, bias=eps_gn[:, 0:1]).then_inc(ostd_ready, 1)
                act.wait_ge(batch_done, b + 1)

            group_root(2)
            act.wait_ge(l1_in, 16 * 6)
            for g in range(G):
                ins = A(wsq[:, g], wmx[:, g], ACT.Square, bias=zero1[:, 0:1], accum_out=l1s[:, 0, g:g + 1])
            ins.then_inc(wnorm_done, 1)
            act.wait_ge(halo_ready, G * (B * NB + 1))
            for r in range(K7):
                for q in range(6):
                    t = r * 6 + q
                    act.wait_ge(wf_ready, t + 1)
                    A(wfold[:, 64 * q:64 * (q + 1), 0:K7, r], ps[:, t % 2, 0:64 * K7].rearrange("p (c k) -> p c k", k=K7),
                      ACT.Copy).then_inc(wf_copied, 1)
            act.wait_ge(beta_ready, 1)
            for r in range(K7):
                ins = A(wfold[:, :, K7, r], ps[:, 2, 0:C], ACT.Copy)
            ins.then_inc(beta_set, 1)
            act.wait_ge(gate_in, 1)
            A(l1v[:, 4], l1v[:, 3], ACT.Gelu, bias=zero1[:, 0:1]).then_inc(gelu_done, 1)
            act.wait_ge(gx2_ready, 1)
            A(l1v[:, 6], l1v[:, 5], ACT.Sqrt, bias=zero1[:, 0:1]).then_inc(gx_ready, 1)
            for t in range(4 * G):
                act.wait_ge(chb_ready, t + 1)
                v, g = t // G, t % G
                A(chb[:, v, P * g:P * (g + 1), :], ps[:, 6 + t % 2, :].rearrange("p (c b) -> p c b", b=B), ACT.Copy
                  ).then_inc(chb_set, 1)
            act.wait_ge(chb_set, 4 * G + 2)
            act.sem_inc(l1_ready, 1)
            act.wait_ge(pads_zero, 2)
            with act.Fori(0, NCG // 2) as k:
                for s in range(2):
                    for c in range(CG):
                        K = k * (2 * CG) + (CG * s + c)
                        if c == 0:
                            act.wait_ge(xg_in[s], k * (16 * B) + 16 * B)
                        act.wait_ge(box_ready, K + 1)
                        act.wait_ge(conv_ready, K + 1)
                        act.sem_inc(passed, 1)
                        for b in range(B):
                            A(ypad[:, c % 2, b, PAD:PAD + W], xg[:, s, b, c, :], ACT.Identity,
                              bias=chb[:, 1, bass.ds(K, 1), b], scale=chb[:, 0, bass.ds(K, 1), b])
                        for b in range(B):
                            ins = A(zpad[:, c % 2, b, PAD:PAD + W], xg[:, s, b, c, :], ACT.Identity,
                                    bias=chb[:, 3, bass.ds(K, 1), b], scale=chb[:, 2, bass.ds(K, 1), b])
                        ins.then_inc(yz_ready, 1)

        @block.tensor
        def _(pe):
            mm = pe.matmul
            pe.wait_ge(const_set, 5)
            pe.wait_ge(wraw_scaled, 1)
            for m in range(G):
                for k in range(G):
                    mm(ps[:, m, 0:C], mean_c[:], wc[:, k, C * m:C * (m + 1)], start=(k == 0), stop=(k == G - 1))
            for m in range(M9):
                for k in range(G):
                    ins = mm(ps[:, 3, m:m + 1], wraw[:, k, P * m:P * (m + 1)], par["ln1_b"][:, k:k + 1],
                             start=(k == 0), stop=(k == G - 1), skip_group_check=True)
            ins.then_inc(wmean_ready, 1)

            def group_sums(step):
                pe.wait_ge(gst_ready, step)
                for m in range(G):
                    for k in range(G):
                        ins = mm(ps[:, 4, 8 * m:8 * m + 8], member[:, k, P * m:P * (m + 1)],
                                 gn_st[:, k].rearrange("p b s -> p (b s)"), start=(k == 0), stop=(k == G - 1),
                                 skip_group_check=True)
                ins.then_inc(gsum_ready, 1)

            group_sums(1)

            def stats(n, odd):
                pe.wait_ge(y_ready, n + 1)
                pe.wait_ge(xn_ready, n * 2 + 2)
                for v, src in enumerate((xin[:, odd], ysq)):
                    for r in range(RB):
                        for k in range(G):
                            ins = mm(ps[:, 3, v * RB + r:v * RB + r + 1], src[:, k, W * r:W * (r + 1)], mean_c[:, 0:1],
                                     start=(k == 0), stop=(k == G - 1), skip_group_check=True)
                ins.then_inc(stat_ready, 1)

            def spread(n):
                pe.wait_ge(rstd_ready, n + 1)
                for j in range(HALVES):
                    for r in range(ROWS_T):
                        c = ROWS_T * j + r
                        ins = mm(ps[:, 3 + j, W * r:W * (r + 1)], rstd[:, c:c + 1].broadcast_to([P, P]), ident[:],
                                 start=True, stop=True)
                    ins.then_inc(bc_ready, 1)

            def make_u(n, g, odd):
                if g == 0:
                    pe.wait_ge(xn_ready, n * 2 + 4)
                for q in range(3):
                    m = 3 * g + q
                    for j in range(HALVES):
                        t = m * HALVES + j
                        pe.wait_ge(u_evicted, n * U_TILES + (t + 1))
                        for k in range(G):
                            ins = mm(ps[:, t % 3, :], wc[:, k, P * m:P * (m + 1)], xin[:, odd, k, TILE * j:TILE * (j + 1)],
                                     start=(k == 0), stop=(k == G - 1))
                        ins.then_inc(u_ready, 1)

            def turn(n, r, odd):
                pe.wait_ge(qkT_evicted, n * RB + r)
                for q in range(2):
                    for g in range(G):
                        ins = pe.transpose(ps[:, 5 + q, P * g:P * (g + 1)], accs[:, odd, 2 * g + q, W * r:W * (r + 1)], ident[:])
                ins.then_inc(qkT_ready, 1)

            def gram_row(n, r, start, stop):
                pe.wait_ge(qkT_evicted, n * RB + r + 1)
                for a in range(G):
                    lo, hi = WIN[a]
                    ins = mm(ps[:, 7, WOFF[a]:WOFF[a] + hi - lo], qkT[:, r % 2, 0, P * a:P * (a + 1)],
                             qkT[:, r % 2, 1, lo:hi], start=(start and a == 0), stop=stop, skip_group_check=True)
                ins.then_inc(gram_done, 1)

            def gram(n, i, odd):
                r0, r1 = rows_of(i)
                pe.wait_ge(tap_done, n * (G * OPS) + G * OPS)
                turn(n, r0, odd)
                for r in range(r0, r1):
                    gram_first = (i == 0 and r == r0)
                    gram_row(n, r, gram_first, i == NB - 1 and r == r1 - 1)
                    if r + 1 < r1:
                        turn(n, r + 1, odd)

            with pe.Fori(0, B) as b:
                pe.wait_ge(cur_set, b + 1)
                stats(b * NB, 0)
                spread(b * NB)

                def first(n, i, odd, prev):
                    make_u(n, 0, odd)
                    if i != NB - 1:
                        stats(n + 1, 1 - odd)
                    make_u(n, 1, odd)
                    if i != 0:
                        gram(n - 1, prev, 1 - odd)
                    if i != NB - 1:
                        spread(n + 1)
                    make_u(n, 2, odd)

                first(b * NB, 0, 0, None)
                first(b * NB + 1, None, 1, 0)
                with pe.Fori(0, (NB - 4) // 2) as k:
                    first(b * NB + k * 2 + 2, None, 0, None)
                    first(b * NB + k * 2 + 3, None, 1, None)
                first(b * NB + (NB - 2), None, 0, None)
                first(b * NB + (NB - 1), NB - 1, 1, None)
                gram(b * NB + (NB - 1), NB - 1, 1)

                pe.wait_ge(diag_ready, b + 1)
                mm(ps[:, 0, 0:C], ones[:], diag[:].rearrange("p g c -> p (g c)"), start=True, stop=True).then_inc(rk_ready, 1)
                pe.wait_ge(a_ready, b + 1)
                for a in range(G):
                    ins = mm(ps[:, 1, 0:C], mean_c[:], a_full[:, a], start=(a == 0), stop=(a == G - 1))
                ins.then_inc(cm_ready, 1)
                pe.wait_ge(ac_ready, b + 1)
                for k in range(G):
                    for a in range(G):
                        ins = pe.transpose(ps[:, 2 + k, P * a:P * (a + 1)], a_cent[:, a, P * k:P * (k + 1)], ident[:])
                ins.then_inc(at_ready, 1)
                pe.wait_ge(at_copied, b + 1)

                def make_o(T, j, loaded):
                    s = 3 * (j % 2)
                    if j % 2 == 0:
                        pe.wait_ge(v2_in[j // 2], loaded)
                    pe.wait_ge(o_evicted, T + 1)
                    for a in range(G):
                        for k in range(G):
                            ins = mm(ps[:, s + a, :], at[:, k, P * a:P * (a + 1)],
                                     vin[:, j // 2, k, TILE * (j % 2):TILE * (j % 2 + 1)], start=(k == 0), stop=(k == G - 1))
                    ins.then_inc(o_ready, 1)

                def finish_o(T, j):
                    pe.wait_ge(osq_ready, T + 1)
                    pe.wait_ge(ostd_ready, T + 1)
                    for r in range(ROWS_T):
                        for k in range(G):
                            ins = mm(ps[:, 6, r:r + 1], osq[:, j % 2, k, W * r:W * (r + 1)], mean_c[:, 0:1],
                                     start=(k == 0), stop=(k == G - 1), skip_group_check=True)
                    ins.then_inc(ostat_ready, 1)
                    pe.wait_ge(orstd_ready, T + 1)
                    pe.wait_ge(on_done, T + 4)
                    for r in range(ROWS_T):
                        ins = mm(ps[:, 7, W * r:W * (r + 1)], rstd2[:, j, r:r + 1].broadcast_to([P, P]), ident[:],
                                 start=True, stop=True)
                    ins.then_inc(obc_ready, 1)

                def second(k, last):
                    for j in range(4):
                        T = b * T2 + k * 4 + j
                        if not (last and j == 3):
                            nxt = (j + 1) % 4
                            make_o(T + 1, nxt, b * (8 * LOADS2) + k * 16 + (16 if nxt else 32))
                        finish_o(T, j)

                make_o(b * T2, 0, b * (8 * LOADS2) + 16)
                with pe.Fori(0, T2 // 4 - 1) as k:
                    second(k, False)
                second(T2 // 4 - 1, True)

            group_sums(2)
            pe.wait_ge(l1_in, 16 * 6)
            pe.wait_ge(batch_done, B)
            for r in range(K7):
                for q in range(6):
                    t = r * 6 + q
                    pe.wait_ge(wf_copied, t + 1)
                    mm(ps[:, t % 2, 0:64 * K7], selk[0:K7, r, :], wky[0:K7, 64 * K7 * q:64 * K7 * (q + 1)],
                       start=True, stop=True).then_inc(wf_ready, 1)
            pe.wait_ge(diag_ready, B + 1)
            mm(ps[:, 2, 0:C], ones[:], diag[:].rearrange("p g c -> p (g c)"), start=True, stop=True).then_inc(beta_ready, 1)
            pe.wait_ge(pool_ready, 1)
            for m in range(G):
                for k in range(G):
                    for v in range(2):
                        ins = mm(ps[:, 3, B * m:B * (m + 1)], wT[:, v, k, P * m:P * (m + 1)], pooled[v][:, k, :],
                                 start=(k == 0 and v == 0), stop=(k == G - 1 and v == 1), skip_group_check=True)
            ins.then_inc(gate_ready, 1)
            pe.wait_ge(gx_ready, 1)
            for k in range(G):
                ins = mm(ps[:, 5, 0:B], mean_c[:], gxv[:, k, :], start=(k == 0), stop=(k == G - 1))
            ins.then_inc(gxm_ready, 1)
            for t in range(4 * G):
                pe.wait_ge(d4_ready, t + 1)
                pe.wait_ge(chb_set, t + 1)
                mm(ps[:, 6 + t % 2, :], ones[:], d4[:, t % 2].rearrange("p c b -> p (c b)"), start=True, stop=True
                   ).then_inc(chb_ready, 1)
            pe.sem_inc(conv_ready, 2)
            with pe.Fori(0, NCG // 2) as k:
                for s in range(2):
                    for c in range(CG):
                        K = k * (2 * CG) + (CG * s + c)
                        pe.wait_ge(yz_ready, K + 1)
                        pe.wait_ge(toep_ready, K + 1)
                        pe.wait_ge(og_ready, K + 1)
                        for kx in range(K7):
                            mm(ps[:, c % 2, :].rearrange("p (b w) -> p b w", b=B), toep[:, c % 2, kx, 0:P],
                               zpad[:, c % 2, :, kx:kx + W], start=(kx == 0), stop=False)
                        pe.wait_ge(box_ready, K + 3)
                        mm(ps[:, c % 2, :].rearrange("p (b w) -> p b w", b=B), toep[:, c % 2, K7, 0:P], box[:, c % 2],
                           start=False, stop=True).then_inc(conv_ready, 1)

        @block.vector
        def _(dve):
            V = nc.vector
            count = [0]

            def then(ins):
                count[0] += 1
                ins.then_inc(chain, 1)
                dve.wait_ge(chain, count[0])

            dve.sem_inc(gn_used, 2)
            dve.sem_inc(xn_ready, 2)
            dve.sem_inc(gram_done, 2)
            dve.sem_inc(on_done, 4)
            for g in range(G):
                dve.sem_inc(v_stored[g], 16)
            dve.wait_ge(par_in, 16 * 6)
            for k in range(G):
                ins = V.tensor_scalar(wc[:, k], wraw[:, k], par["ln1_w"][:, k:k + 1], None, ALU.mult)
            ins.then_inc(wraw_scaled, 1)
            dve.wait_ge(wmean_ready, 1)
            dve.wait_ge(wraw_scaled, 1)
            for k in range(G):
                ins = V.tensor_tensor(wc[:, k].rearrange("p (a n) -> p a n", a=G), wc[:, k].rearrange("p (a n) -> p a n", a=G),
                                      ps[:, 0:3, 0:C], ALU.subtract)
            ins.then_inc(wc_ready, 1)
            V.tensor_copy(bias_u[:], ps[:, 3, 0:M9]).then_inc(wc_ready, 1)
            gnbn_n = gnbn.rearrange("p g b t s -> p (g b) t s")
            with dve.Fori(0, B) as b:
                for g in range(G):
                    for q in range(GN_LOADS):
                        dve.wait_ge(gn_in[q % 2], b * (8 * G * GN_LOADS) + 16 * ((g * GN_LOADS + q) // 2 + 1))
                        dve.sem_inc(passed, 1)
                        for t in range(GN_COLS // 512):
                            ins = V.bn_stats(gnbn[:, g, bass.ds(b, 1), q * (GN_COLS // 512) + t, :].rearrange("p a s -> p (a s)"),
                                             gnx[:, q % 2, 512 * t:512 * (t + 1)])
                        ins.then_inc(gn_used, 1)
            dve.wait_ge(gn_used, B * G * GN_LOADS + 2)
            for g in range(G):
                for b in range(B):
                    ins = V.bn_aggr(gn_st[:, g, b, :], gnbn[:, g, b].rearrange("p t s -> p (t s)"))
            then(ins)

            def group_norm(step, r, nb):
                dve.wait_ge(gsum_ready, step)
                gs = ps[:, 4, 0:8 * G].rearrange("p (g b s) -> p g b s", g=G, b=B)
                then(V.tensor_copy(gn_mean[:], gs[:, :, :, 0]))
                then(V.tensor_tensor(gn_tmp[:], gn_mean[:], gn_mean[:], ALU.mult))
                V.tensor_tensor(gn_tmp[:], gs[:, :, :, 1], gn_tmp[:], ALU.subtract).then_inc(gvar_ready, 1)
                dve.wait_ge(gstd_ready, step)
                then(V.reciprocal(r, gn_r[:]))
                then(V.scalar_tensor_tensor(out=nb, in0=gn_mean[:], scalar=-1.0, in1=r, op0=ALU.mult, op1=ALU.mult))

            then(V.tensor_tensor(gn_tmp[:], gn_st[:, :, :, 0], gn_st[:, :, :, 0], ALU.mult))
            V.tensor_tensor(gn_st[:, :, :, 1], gn_st[:, :, :, 1], gn_tmp[:], ALU.add).then_inc(gst_ready, 1)
            group_norm(1, gn_r[:], gn_nb[:])

            def variance(n):
                dve.wait_ge(mu2_ready, n + 1)
                V.tensor_tensor(var[:], ps[:, 3, RB:2 * RB], mu2[:], ALU.subtract).then_inc(var_ready, 1)

            def invert(n):
                dve.wait_ge(std_ready, n + 1)
                V.reciprocal(rstd[:], std[:]).then_inc(rstd_ready, 1)

            def normalise(n, odd):
                for j in range(HALVES):
                    dve.wait_ge(bc_ready, n * 2 + (j + 1))
                    px = xin[:, odd, :, TILE * j:TILE * (j + 1)]
                    V.tensor_tensor(px, px, ps[:, 3 + j:4 + j, :].broadcast_to([P, G, TILE]), ALU.mult).then_inc(xn_ready, 1)

            def taps(n, g, i, odd, between=None):
                r0, r1 = rows_of(i)
                dve.wait_ge(centre_ready, n * M9 + 3 * (g + 1))
                base = n * (G * OPS) + OPS * g
                for t, (dy, dx) in enumerate(TAPS):
                    if t == 3 and between:
                        between()
                    for q in range(3):
                        m = 3 * g + q
                        acc = accv[:, g] if q == 2 else accs[:, odd, 2 * g + q]
                        acc = acc[:, r0 * W:r1 * W].rearrange("p (r w) -> p r w", w=W)
                        if t:
                            dve.wait_ge(tap_done, base + (3 * t + q - 2))
                        V.scalar_tensor_tensor(out=acc, in0=ubuf[:, m, r0 + dy:r1 + dy, dx:dx + W],
                                               scalar=dw[:, m, 3 * dy + dx:3 * dy + dx + 1], in1=acc,
                                               op0=ALU.mult, op1=ALU.add).then_inc(tap_done, 1)

            with dve.Fori(0, B) as b:
                V.tensor_copy(cur[:, 0], gn_r[:, :, bass.ds(b, 1)].rearrange("p g a -> p (g a)"))
                V.tensor_copy(cur[:, 1], gn_nb[:, :, bass.ds(b, 1)].rearrange("p g a -> p (g a)")).then_inc(cur_set, 1)
                variance(b * NB)
                invert(b * NB)
                normalise(b * NB, 0)

                def first(n, i, odd, seen, idx=None):
                    more = i != NB - 1
                    taps(n, 0, i, odd)
                    if more:
                        variance(n + 1)
                    taps(n, 1, i, odd, (lambda: invert(n + 1)) if more else None)
                    if more:
                        normalise(n + 1, 1 - odd)
                    taps(n, 2, i, odd)

                blocks(dve, b, first)

                step = [0]

                def thus(ins):
                    step[0] += 1
                    ins.then_inc(small, 1)
                    dve.wait_ge(small, b * SMALL + step[0])

                dve.wait_ge(sq_done, b * (2 * G * NB) + (2 * G * NB + 2))
                V.tensor_reduce(norm[:], norms[:], AX.X, ALU.add).then_inc(nsum_ready, 1)
                dve.wait_ge(gram_done, b * H + (H + 2))
                thus(V.memset(a_full, 0.0))
                dve.wait_ge(nroot_ready, b + 1)
                thus(V.tensor_scalar(norm[:], norm[:], EPS_NORM, None, ALU.max))
                thus(V.reciprocal(rnorm[:], norm[:]))
                V.tensor_tensor(rqs[:], rnorm[:, 0], par["scale"], ALU.mult)
                for g in range(G):
                    ins = V.tensor_scalar(diag[:, g], ident[:], rnorm[:, 1, g:g + 1], None, ALU.mult)
                ins.then_inc(diag_ready, 1)
                dve.wait_ge(diag_ready, b + 1)
                dve.wait_ge(rk_copied, b + 1)
                for a in range(G):
                    cols = slice(WOFF[a], WOFF[a] + WIN[a][1] - WIN[a][0])
                    ins = V.scalar_tensor_tensor(out=scores[:, cols], in0=ps[:, 7, cols], scalar=rqs[:, a:a + 1],
                                                 in1=rk_row[:, WIN[a][0]:WIN[a][1]], op0=ALU.mult, op1=ALU.mult)
                thus(ins)
                thus(V.tensor_tensor(scores[:], scores[:], hmask[:], ALU.add))
                for a in range(G):
                    cols = slice(WOFF[a], WOFF[a] + WIN[a][1] - WIN[a][0])
                    ins = V.tensor_reduce(smx[:, a:a + 1], scores[:, cols], AX.X, ALU.max)
                thus(ins)
                V.tensor_scalar(smx[:], smx[:], -1.0, None, ALU.mult).then_inc(smx_ready, 1)
                dve.wait_ge(exp_done, b * 3 + 3)
                thus(V.reciprocal(rsum[:], ssum[:]))
                for a in range(G):
                    cols = slice(WOFF[a], WOFF[a] + WIN[a][1] - WIN[a][0])
                    ins = V.tensor_scalar(a_full[:, a, WIN[a][0]:WIN[a][1]], scores[:, cols], rsum[:, a:a + 1], None, ALU.mult)
                ins.then_inc(a_ready, 1)
                dve.wait_ge(a_ready, b + 1)
                dve.wait_ge(cm_ready, b + 1)
                V.tensor_tensor(a_cent, a_full, ps[:, 1:2, 0:C].broadcast_to([P, G, C]), ALU.subtract).then_inc(ac_ready, 1)

                with dve.Fori(0, T2 // 4) as k:
                    for j in range(4):
                        T = b * T2 + k * 4 + j
                        dve.wait_ge(ostd_ready, T + 2)
                        V.reciprocal(rstd2[:, j], std2[:, j]).then_inc(orstd_ready, 1)
                        dve.wait_ge(obc_ready, T + 1)
                        dve.wait_ge(o_evicted, T + 3)
                        V.tensor_tensor(ow[:, j], ow[:, j], ps[:, 7:8, :].broadcast_to([P, G, TILE]), ALU.mult
                                        ).then_inc(on_done, 1)
                        if j % 2 == 0:
                            dve.wait_ge(x2_in[j // 2], b * (8 * LOADS2) + k * 16 + 16)
                        dve.wait_ge(on_done, T + 5)
                        px = xin[:, j // 2, :, TILE * (j % 2):TILE * (j % 2 + 1)]
                        for a in range(G):
                            V.scalar_tensor_tensor(out=px[:, a], in0=px[:, a], scalar=par["ln2_b"][:, a:a + 1],
                                                   in1=ow[:, j, a], op0=ALU.add, op1=ALU.add).then_inc(x1_ready, 1)
                        dve.wait_ge(x1_ready, b * (3 * T2) + k * 12 + 3 * (j + 1))
                        dve.sem_inc(passed, 1)
                        for a in range(G):
                            V.bn_stats(bn2[:, a, bass.ds(k * 4 + j, 1), :].rearrange("p a s -> p (a s)"), px[:, a])
                        V.tensor_reduce(mx2[:, :, bass.ds(k * 4 + j, 1)], px, AX.X, ALU.max).then_inc(bn_done, 1)
                dve.wait_ge(bn_done, b * T2 + T2)
                dve.sem_inc(passed, 1)
                for a in range(G):
                    V.bn_aggr(aggr[:, a], bn2[:, a].rearrange("p t s -> p (t s)"))
                at_b = bass.ds(b, 1)
                thus(V.tensor_reduce(ch_max[:, :, at_b], mx2, AX.X, ALU.max))
                V.tensor_copy(ch_mean[:, :, at_b], aggr[:, :, 0:1])
                V.tensor_copy(gn_st[:, :, at_b, 0], aggr[:, :, 0:1])
                thus(V.tensor_tensor(gn_tmp[:, :, 0], aggr[:, :, 0], aggr[:, :, 0], ALU.mult))
                V.tensor_tensor(gn_st[:, :, at_b, 1], aggr[:, :, 1:2], gn_tmp[:, :, 0:1], ALU.add).then_inc(batch_done, 1)
                assert step[0] == SMALL, step[0]

            dve.wait_ge(batch_done, B)
            dve.sem_inc(gst_ready, 1)
            for g in range(G):
                ins = V.tensor_scalar(diag[:, g], ident[:], par["beta"][:, g:g + 1], None, ALU.mult)
            ins.then_inc(diag_ready, 1)
            r2, nb2, srv, snb = (l1v[:, i] for i in range(8, 12))
            group_norm(2, r2, nb2)
            then(V.tensor_tensor(pooled[0], ch_mean[:], r2, ALU.mult))
            then(V.tensor_tensor(pooled[0], pooled[0], nb2, ALU.add))
            then(V.tensor_tensor(pooled[1], ch_max[:], r2, ALU.mult))
            V.tensor_tensor(pooled[1], pooled[1], nb2, ALU.add).then_inc(pool_ready, 1)
            then(V.tensor_tensor(l1s[:, 1], par["b_avg"], par["b_max"], ALU.add))
            dve.wait_ge(gate_ready, 1)
            V.tensor_tensor(l1v[:, 3], ps[:, 3, 0:B * G].rearrange("p (g b) -> p g b", b=B),
                            l1s[:, 1].unsqueeze(2).broadcast_to([P, G, B]), ALU.add).then_inc(gate_in, 1)
            dve.wait_ge(gelu_done, 1)
            dve.wait_ge(wnorm_done, 1)
            xw = l1v[:, 4]
            then(V.tensor_tensor(l1v[:, 7], xw, xw, ALU.mult))
            V.tensor_tensor(l1v[:, 5], l1v[:, 7], l1s[:, 0].unsqueeze(2).broadcast_to([P, G, B]), ALU.mult).then_inc(gx2_ready, 1)
            dve.wait_ge(gxm_ready, 1)
            then(V.tensor_scalar(mrow[:, 0], ps[:, 5, 0:B], EPS_NX, None, ALU.add))
            then(V.reciprocal(mrow[:, 1], mrow[:, 0]))
            then(V.tensor_tensor(l1v[:, 7], l1v[:, 6], mrow[:, 1:2].broadcast_to([P, G, B]), ALU.mult))
            then(V.tensor_tensor(l1v[:, 7], l1v[:, 7], xw, ALU.mult))
            then(V.tensor_tensor(l1v[:, 7], l1v[:, 7], par["gamma"].unsqueeze(2).broadcast_to([P, G, B]), ALU.mult))
            then(V.tensor_tensor(srv, l1v[:, 7], r2, ALU.mult))
            then(V.tensor_tensor(snb, l1v[:, 7], nb2, ALU.mult))
            dve.wait_ge(l1_in, 16 * 6)
            for t in range(4 * G):
                v, g = t // G, t % G
                if t >= 2:
                    dve.wait_ge(chb_ready, t - 1)
                V.tensor_tensor(d4[:, t % 2], ident[:].unsqueeze(2).broadcast_to([P, P, B]),
                                (r2, nb2, srv, snb)[v][:, g:g + 1, :].broadcast_to([P, P, B]), ALU.mult).then_inc(d4_ready, 1)
            dve.wait_ge(beta_set, 1)
            dve.wait_ge(chb_ready, 4 * G)
            dve.wait_ge(wnorm_done, 1)
            dve.sem_inc(l1_ready, 1)
            dve.sem_inc(box_ready, 2)
            dve.sem_inc(og_ready, 2)
            for s in range(2):
                dve.sem_inc(og_stored[s], 16 * B)

            def add_x1(K, s, c, first_of_group, k):
                dve.wait_ge(conv_ready, K + 3)
                if first_of_group:
                    dve.wait_ge(og_stored[s], k * (16 * B) + 16 * B)
                V.tensor_tensor(og[:, s, :, c, :], ps[:, c % 2, :].rearrange("p (b w) -> p b w", b=B), xg[:, s, :, c, :],
                                ALU.add).then_inc(og_ready, 1)

            with dve.Fori(0, NCG // 2) as k:
                for s in range(2):
                    for c in range(CG):
                        K = k * (2 * CG) + (CG * s + c)
                        y = ypad[:, c % 2]
                        dve.wait_ge(yz_ready, K + 1)
                        V.tensor_tensor(s2[:, :, 0:XP - 1], y[:, :, 0:XP - 1], y[:, :, 1:XP], ALU.add).then_inc(box_step, 1)
                        dve.wait_ge(conv_ready, K + 1)
                        V.tensor_tensor(toep[:, c % 2].rearrange("p k (q r) -> p k q r", r=K7),
                                        wfold[:, bass.ds(K, 1)].rearrange("p a k r -> p (a k) r").unsqueeze(2).broadcast_to([P, K7 + 1, FOLD, K7]),
                                        band.rearrange("p (q r) -> p q r", r=K7).unsqueeze(1).broadcast_to([P, K7 + 1, FOLD, K7]),
                                        ALU.mult).then_inc(toep_ready, 1)
                        dve.wait_ge(box_step, K * 3 + 1)
                        V.tensor_tensor(s4[:, :, 0:XP - 3], s2[:, :, 0:XP - 3], s2[:, :, 2:XP - 1], ALU.add).then_inc(box_step, 1)
                        dve.wait_ge(box_step, K * 3 + 2)
                        V.tensor_tensor(s6, s4[:, :, 0:W], s2[:, :, 4:W + 4], ALU.add).then_inc(box_step, 1)
                        dve.wait_ge(box_step, K * 3 + 3)
                        V.tensor_tensor(box[:, c % 2], s6, y[:, :, 6:W + 6], ALU.add).then_inc(box_ready, 1)
                        add_x1(K, s, c, c == 0, k)


_IN = ["x", "w_qkv", "dw_qkv", "chans", "w_avg", "w_max", "w_mix_ch", "w_mix_ky",
       "ident", "member", "headmask", "band", "sel"]


def kernel(**inputs):
    import concourse.bacc as bacc
    from concourse.bass_utils import run_bass_kernel_spmd

    def split(a):
        a = np.asarray(a)
        return np.moveaxis(a.reshape((G, P) + a.shape[1:]), 0, 1)

    i = {k: np.asarray(v) for k, v in inputs.items()}
    w = np.stack([i[f"L0_conv_w{q}"].T.reshape(C, G, P) for q in "qkv"], axis=2)
    dwt = np.stack([i[f"L0_conv_dw{q}"].reshape(G, P, 9) for q in "qkv"], axis=1)
    vectors = [i["L0_conv_ln1_w"], i["L0_conv_ln1_b"], i["L0_conv_ln2_w"], i["L0_conv_ln2_b"],
               np.repeat(i["L0_conv_scale"].reshape(HEADS), HEAD), i["L1_conv_b_avg"], i["L1_conv_b_max"],
               i["L1_conv_gamma"].reshape(C), i["L1_conv_beta"].reshape(C)]
    w_mix = i["L1_conv_w_mix"]

    c = np.arange(C)
    member = np.where(c[:, None] // GN_SIZE == c[None, :] // GN_SIZE, 1.0 / GN_SIZE, 0.0)
    headmask = np.concatenate(
        [np.where((P * a + np.arange(P))[:, None] // HEAD == np.arange(*WIN[a])[None, :] // HEAD, 0.0, -1e30)
         for a in range(G)], axis=1)
    p, j, r = np.arange(P), np.arange(BAND), np.arange(K7)
    band = np.where(np.abs(p[:, None] - j[None, :]) <= PAD, 1.0, 0.0)
    sel = np.where(((p[None, :] - r[:, None] + PAD) % K7)[None] == r[:, None, None], 1.0, 0.0)

    arrays = {
        "x": i["x"], "w_qkv": split(w.reshape(C, M9 * P)),
        "dw_qkv": dwt.reshape(M9, P, 9).transpose(1, 0, 2),
        "chans": np.stack([split(v) for v in vectors], axis=1),
        "w_avg": split(i["L1_conv_w_avg"].T), "w_max": split(i["L1_conv_w_max"].T),
        "w_mix_ch": split(w_mix), "w_mix_ky": w_mix.reshape(C, K7, K7).transpose(1, 0, 2).reshape(K7, C * K7),
        "ident": np.eye(P), "member": split(member), "headmask": headmask, "band": band, "sel": sel,
    }
    nc = bacc.Bacc("TRN2", target_bir_lowering=False, num_devices=1)
    given, args = {}, []
    for name in _IN:
        a = arrays[name]
        if name in ("ident", "member", "headmask", "band", "sel"):
            a = a.astype(np.float32)
        a = np.ascontiguousarray(a)
        given[f"in_{name}"] = a
        args.append(nc.dram_tensor(f"in_{name}", a.shape, mybir.dt.from_np(a.dtype), kind="ExternalInput").ap())
    out = nc.dram_tensor("out_0", (B, C, H, W), F32, kind="ExternalOutput").ap()
    build(nc, *args, out)
    r = run_bass_kernel_spmd(nc, [given], core_ids=[0])
    return r.results[0]["out_0"]
```

```python
from contextlib import ExitStack

import numpy as np

import concourse.bass as bass
from concourse import mybir

F32 = mybir.dt.float32
F16 = mybir.dt.float16
ALU = mybir.AluOpType
ACT = mybir.ActivationFunctionType
AX = mybir.AxisListType

P = 128
B, C, H, W = 4, 384, 128, 128
HW = H * W
G = C // P
GN_SIZE = C // 32
HEADS = 8
HEAD = C // HEADS
EPS_GN = 1e-5
EPS_LN = 1e-5
EPS_NORM = 1e-12
EPS_NX = 1e-6

RB = 8
NB = H // RB
PX = RB * W
TILE = 512
HALVES = PX // TILE
ROWS_T = TILE // W
M9 = 3 * G
U_TILES = M9 * HALVES
TAPS = [(dy, dx) for dy in range(3) for dx in range(3) if (dy, dx) != (1, 1)]
OPS = 3 * len(TAPS)
STATS_AT = 3 * HALVES + 1
ROOT_AT = 6 * HALVES - 1
SQUARES_AT = 4 * HALVES - 2
SPREAD_AT = 7 * HALVES
GRAM_AT = U_TILES - RB - 2
WIN = [((P * a) // HEAD * HEAD, -(-(P * (a + 1)) // HEAD) * HEAD) for a in range(G)]
WOFF = [sum(hi - lo for lo, hi in WIN[:a]) for a in range(G)]
WCOLS = sum(hi - lo for lo, hi in WIN)

T2 = HW // TILE

K7 = 7
PAD = K7 // 2
FOLD = -(-P // K7)
BAND = FOLD * K7
CG = 4
NCG = C // CG
XP = W + 2 * PAD
MIN_W = 1e-30
MIN_S = 1e-12
GN_COLS = 4096
GN_LOADS = HW // GN_COLS

ARENA = 46720

CH_NAMES = ["ln1_w", "ln1_b", "ln2_w", "ln2_b", "scale", "b_avg", "b_max", "gamma", "beta"]


def build(nc, x, w_qkv, dw_qkv, chans, w_avg, w_max, w_mix_ch, w_mix_ky,
          ident_in, member_in, headmask_in, band_in, sel_in,
          to_row_in, from_row_in, out):
    ctx = ExitStack()
    with ctx:
        def sb(name, shape):
            return ctx.enter_context(nc.sbuf_tensor(name, shape, F32))

        def sem(name):
            return ctx.enter_context(nc.semaphore(name))

        v_dram = nc.dram_tensor("v_scratch", (B, C, HW), F32, kind="Internal").ap()
        x1_dram = nc.dram_tensor("x1_scratch", (B, C, HW), F32, kind="Internal").ap()

        ps = ctx.enter_context(nc.psum_tensor("ps", [P, 8, 512], F32))

        ident = sb("ident", [P, P])
        ones = sb("ones", [P, P])
        mean_c = sb("mean_c", [P, P])
        zero1 = sb("zero1", [P, 1])
        eps_gn = sb("eps_gn", [P, 1])
        member = sb("member", [P, G, C])
        ch = sb("ch", [P, len(CH_NAMES), G])
        par = {n: ch[:, i, :] for i, n in enumerate(CH_NAMES)}
        dw = sb("dw", [P, M9, 9])
        bias_u = sb("bias_u", [P, M9])
        gn_st = sb("gn_st", [P, G, B, 2])
        gn_tmp = sb("gn_tmp", [P, G, B])
        gn_mean = sb("gn_mean", [P, G, B])
        gn_r = sb("gn_r", [P, G, B])
        gn_nb = sb("gn_nb", [P, G, B])
        ch_mean = sb("ch_mean", [P, G, B])
        ch_max = sb("ch_max", [P, G, B])
        aggr = sb("aggr", [P, G, 2])
        mu2 = sb("mu2", [RB, W])
        var = sb("var", [RB, W])
        std = sb("std", [RB, W])
        rstd = sb("rstd", [RB, W])
        norms = sb("norms", [P, 2, G, NB])
        norm = sb("norm", [P, 2, G])
        rnorm = sb("rnorm", [P, 2, G])
        rqs = sb("rqs", [P, G])
        smx = sb("smx", [P, G])
        ssum = sb("ssum", [P, G])
        rsum = sb("rsum", [P, G])
        std2 = sb("std2", [ROWS_T, 4, W])
        rstd2 = sb("rstd2", [ROWS_T, 4, W])
        to_row = sb("to_row", [P, RB, RB])
        from_row = sb("from_row", [RB, RB, P])
        diag = sb("diag", [P, G, P])
        scores = sb("scores", [P, WCOLS])
        hmask = sb("hmask", [P, WCOLS])
        cur = sb("cur", [P, 2, G])

        arena = sb("arena", [P, ARENA])

        def carve(start, *dims):
            n = int(np.prod(dims))
            v = arena[:, start:start + n]
            names = "abcd"[:len(dims)]
            if len(dims) > 1:
                v = v.rearrange(f"p ({' '.join(names)}) -> p {' '.join(names)}",
                                **{k: d for k, d in zip(names, dims)})
            return v, start + n

        def carve16(start, *dims):
            words = -(-int(np.prod(dims)) // 2)
            v = arena[:, start:start + words].bitcast(F16)[:, 0:int(np.prod(dims))]
            names = "abcd"[:len(dims)]
            if len(dims) > 1:
                v = v.rearrange(f"p ({' '.join(names)}) -> p {' '.join(names)}",
                                **{k: d for k, d in zip(names, dims)})
            return v, start + words

        o = 0
        xin, o = carve(o, 2, G, PX)
        o_ysq = o
        ysq, o = carve(o, G, PX)
        o_ubuf = o
        ubuf, o = carve(o, M9, RB + 3, W + 2)
        o_acc = o
        accs, o = carve(o, 2, 2 * G, (RB + 1) * W)
        accv, o = carve(o, G, (RB + 1) * W)
        o_end_acc = o
        wc, o = carve(o, G, M9 * P)
        o_qkT = o
        qkT, o = carve(o, 2, 2, C)
        junk, o = carve(o, 2, (RB + 1) * W)
        end_l0 = o
        assert o <= ARENA, o
        wraw, _ = carve(o_acc, G, M9 * P)
        gnbn, _ = carve(o_acc + G * M9 * P, G, B, HW // 512, 6)
        gnx, o = carve(0, 2, GN_COLS)
        assert o <= o_ubuf
        a_full, o = carve(o_qkT, G, C)
        a_cent, o = carve(o, G, C)
        rk_row, o = carve(o, C)
        at, o = carve(o, G, C)
        assert o <= end_l0
        o = o_acc
        vin, o = carve(o, 4, G, TILE)
        x2, _ = carve(0, 4, G, TILE)
        ow, o = carve(o, 4, G, TILE)
        osq, o = carve(o, 2, G, TILE)
        assert o <= o_end_acc, (o, o_end_acc)
        bn2, o2 = carve(o_ysq, G, T2, 6)
        mx2, o2 = carve(o2, G, T2)
        o = 0
        wfold, o = carve16(o, C, 2 * K7, K7)
        chb, o = carve(o, 4, C, B)
        sig, o = carve(o, C)
        band, o = carve(o, BAND)
        band16, o = carve16(o, BAND)
        toep, o = carve16(o, 2, 2 * K7, BAND)
        o_tmp = o
        xg, o = carve(o, 2, B, CG, W)
        og, o = carve(o, 2, B, CG, W)
        ypad, o = carve(o, 2, B, XP)
        zfull, o = carve(o, 2, B, W)
        zhi, o = carve16(o, 2, B, XP)
        zlo, o = carve16(o, 2, B, XP)
        s2, o = carve(o, B, XP)
        s4, o = carve(o, B, XP)
        s6, o = carve(o, B, W)
        box, o = carve(o, 2, B, W)
        assert o <= ARENA, o
        wT, o_l1 = carve(o_tmp, 2, G, C)
        selk, o_l1 = carve(o_l1, K7, P)
        wky, o_l1 = carve(o_l1, C * K7)
        d4, o_l1 = carve(o_l1, 2, P, B)
        wmx, o_l1 = carve(o_l1, G, K7 * K7)
        wsq, o_l1 = carve(o_l1, G, K7 * K7)
        assert o_l1 <= o, o_l1
        l1v = sb("l1v", [P, 16, G, B])
        l1s = sb("l1s", [P, 10, G])
        mrow = sb("mrow", [P, 2, B])

        par_in = sem("par_in")
        const_set = sem("const_set")
        passed = sem("passed")
        gn_in = [sem(f"gn_in{i}") for i in range(2)]
        gn_used = sem("gn_used")
        chain = sem("chain")
        wraw_scaled = sem("wraw_scaled")
        wmean_ready = sem("wmean_ready")
        wc_ready = sem("wc_ready")
        gst_ready = sem("gst_ready")
        gsum_ready = sem("gsum_ready")
        gvar_ready = sem("gvar_ready")
        gstd_ready = sem("gstd_ready")
        gn_ready = sem("gn_ready")
        cur_set = sem("cur_set")
        x_in = [sem(f"x_in{i}") for i in range(2)]
        y_ready = sem("y_ready")
        stat_ready = sem("stat_ready")
        mu2_ready = sem("mu2_ready")
        var_ready = sem("var_ready")
        std_ready = sem("std_ready")
        rstd_ready = sem("rstd_ready")
        bc_ready = sem("bc_ready")
        xn_ready = sem("xn_ready")
        u_ready = sem("u_ready")
        u_evicted = sem("u_evicted")
        halo_ready = sem("halo_ready")
        centre_ready = sem("centre_ready")
        tap_done = sem("tap_done")
        v_stored = [sem(f"v_stored{g}") for g in range(G)]
        qkT_ready = sem("qkT_ready")
        qkT_evicted = sem("qkT_evicted")
        gram_done = sem("gram_done")
        sq_done = sem("sq_done")
        nsum_ready = sem("nsum_ready")
        nroot_ready = sem("nroot_ready")
        diag_ready = sem("diag_ready")
        rk_ready = sem("rk_ready")
        rk_copied = sem("rk_copied")
        smx_ready = sem("smx_ready")
        exp_done = sem("exp_done")
        a_zero = sem("a_zero")
        a_ready = sem("a_ready")
        cm_ready = sem("cm_ready")
        ac_ready = sem("ac_ready")
        at_ready = sem("at_ready")
        at_copied = sem("at_copied")
        small = sem("small")
        x2_in = [sem(f"x2_in{i}") for i in range(4)]
        v2_in = [sem(f"v2_in{i}") for i in range(4)]
        o_ready = sem("o_ready")
        osq_ready = sem("osq_ready")
        o_evicted = sem("o_evicted")
        ostat_ready = sem("ostat_ready")
        ostd_ready = sem("ostd_ready")
        orstd_ready = sem("orstd_ready")
        obc_ready = sem("obc_ready")
        on_done = sem("on_done")
        x1_ready = sem("x1_ready")
        bn_done = sem("bn_done")
        x1_stored = [sem(f"x1_stored{i}") for i in range(4)]
        batch_done = sem("batch_done")
        l1_in = sem("l1_in")
        wf_ready = sem("wf_ready")
        wf_copied = sem("wf_copied")
        wf_lo = sem("wf_lo")
        wdiv_ready = sem("wdiv_ready")
        wky_scaled = sem("wky_scaled")
        sig_ready = sem("sig_ready")
        sig_set = sem("sig_set")
        pool_ready = sem("pool_ready")
        gate_ready = sem("gate_ready")
        gate_in = sem("gate_in")
        gelu_done = sem("gelu_done")
        wnorm_done = sem("wnorm_done")
        gx2_ready = sem("gx2_ready")
        gx_ready = sem("gx_ready")
        gxm_ready = sem("gxm_ready")
        d4_ready = sem("d4_ready")
        chb_ready = sem("chb_ready")
        chb_set = sem("chb_set")
        l1_ready = sem("l1_ready")
        pads_zero = sem("pads_zero")
        xg_in = [sem(f"xg_in{i}") for i in range(2)]
        zfull_ready = sem("zfull_ready")
        yz_ready = sem("yz_ready")
        zlo_ready = sem("zlo_ready")
        toep_ready = sem("toep_ready")
        box_step = sem("box_step")
        box_ready = sem("box_ready")
        conv_ready = sem("conv_ready")
        og_ready = sem("og_ready")
        og_stored = [sem(f"og_stored{i}") for i in range(2)]

        wqk = wc.rearrange("p k (m c) -> p k m c", c=P)
        xr = x.rearrange("b (g p) h w -> b p g (h w)", p=P)
        xg_n = x.rearrange("b (g p) h w -> (b g) p (h w)", p=P)
        vr = v_dram.rearrange("b (g p) n -> b p g n", p=P)
        x1r = x1_dram.rearrange("b (g p) n -> b p g n", p=P)
        x1y = x1_dram.rearrange("b c (y w) -> y b c w", w=W)
        outy = out.rearrange("b c y w -> y b c w")

        def of_image(ap, b):
            return ap[bass.ds(b, 1)].rearrange("a p g n -> (a p) g n")

        def rows_of(i):
            return (1 if i == 0 else 0), (RB + 1 if i == NB - 1 else RB)

        def blocks(eng, b, body):
            body(b * NB, 0, 0, b * (NB // 2))
            with eng.Fori(0, (NB - 2) // 2) as k:
                body(b * NB + k * 2 + 1, None, 1, b * (NB // 2) + k, k * 2 + 1)
                body(b * NB + k * 2 + 2, None, 0, b * (NB // 2) + k + 1, k * 2 + 2)
            body(b * NB + (NB - 1), NB - 1, 1, b * (NB // 2) + (NB // 2 - 1))

        pooled = (l1v[:, 0], l1v[:, 1])
        gxv = l1v[:, 6]
        SMALL = 9

        block = ctx.enter_context(nc.Block())

        @block.sync
        def _(sp):
            for dst, src in ((ident, ident_in), (member, member_in), (ch, chans), (dw, dw_qkv),
                             (wraw, w_qkv), (hmask, headmask_in),
                             (to_row, to_row_in), (from_row, from_row_in)):
                sp.dma_start(dst[:], src).then_inc(par_in, 16)
            with sp.Fori(0, B * G) as n:
                for q in range(GN_LOADS):
                    sp.wait_ge(gn_used, n * GN_LOADS + (q + 1))
                    sp.sem_inc(passed, 1)
                    sp.dma_start(gnx[:, q % 2, :],
                                 xg_n[bass.ds(n, 1), :, q * GN_COLS:(q + 1) * GN_COLS].rearrange("a p n -> (a p) n")
                                 ).then_inc(gn_in[q % 2], 16)
            sp.wait_ge(gn_used, B * G * GN_LOADS + 2)
            sp.wait_ge(wc_ready, 2)
            with sp.Fori(0, B) as b:
                xb, vb, x1b = of_image(xr, b), of_image(vr, b), of_image(x1r, b)
                for i in range(2):
                    sp.dma_start(xin[:, i], xb[:, :, i * PX:(i + 1) * PX]).then_inc(x_in[i], 16)

                def first(n, i, odd, seen, idx=None):
                    r0, r1 = rows_of(i)
                    for g in range(G):
                        sp.wait_ge(tap_done, n * (G * OPS) + OPS * (g + 1))
                        sp.sem_inc(passed, 1)
                        if i is None:
                            dst = vb[:, g:g + 1, bass.ds(idx * PX - W, RB * W)]
                        else:
                            dst = vb[:, g:g + 1, i * PX - W + r0 * W:i * PX - W + r1 * W]
                        sp.dma_start(dst.rearrange("p a n -> p (a n)"), accv[:, g, r0 * W:r1 * W]
                                     ).then_inc(v_stored[g], 16)
                        if g == 0 and i is None:
                            load(n, odd, idx)
                        elif g == 0 and i == 0:
                            sp.wait_ge(u_ready, n * U_TILES + U_TILES)
                            sp.sem_inc(passed, 1)
                            sp.dma_start(xin[:, 0], xb[:, :, 2 * PX:3 * PX]).then_inc(x_in[0], 16)

                def load(n, odd, idx):
                    sp.wait_ge(u_ready, n * U_TILES + U_TILES)
                    sp.sem_inc(passed, 1)
                    sp.dma_start(xin[:, odd], xb[:, :, bass.ds(idx * PX + 2 * PX, PX)]).then_inc(x_in[odd], 16)

                def first_no_load(n, i, odd, seen, idx):
                    r0, r1 = rows_of(i)
                    for g in range(G):
                        sp.wait_ge(tap_done, n * (G * OPS) + OPS * (g + 1))
                        sp.sem_inc(passed, 1)
                        sp.dma_start(vb[:, g:g + 1, idx * PX - W + r0 * W:idx * PX - W + r1 * W].rearrange("p a n -> p (a n)"),
                                     accv[:, g, r0 * W:r1 * W]).then_inc(v_stored[g], 16)

                first(b * NB, 0, 0, None)
                with sp.Fori(0, (NB - 4) // 2) as k:
                    first(b * NB + k * 2 + 1, None, 1, None, k * 2 + 1)
                    first(b * NB + k * 2 + 2, None, 0, None, k * 2 + 2)
                first(b * NB + (NB - 3), None, 1, None, NB - 3)
                first_no_load(b * NB + (NB - 2), None, 0, None, NB - 2)
                first_no_load(b * NB + (NB - 1), NB - 1, 1, None, NB - 1)

                def load_x2(slot, cols):
                    sp.dma_start(x2[:, slot], xb[:, :, cols]).then_inc(x2_in[slot], 16)

                def load_v2(slot, cols):
                    sp.dma_start(vin[:, slot], vb[:, :, cols]).then_inc(v2_in[slot], 16)

                sp.wait_ge(u_ready, b * (NB * U_TILES) + NB * U_TILES)
                sp.sem_inc(passed, 1)
                for s in range(4):
                    load_x2(s, slice(s * TILE, (s + 1) * TILE))
                sp.wait_ge(gram_done, b * H + (H + 2))
                sp.sem_inc(passed, 1)
                sp.wait_ge(sq_done, b * (2 * G * NB) + (2 * G * NB + 2))
                sp.sem_inc(passed, 1)
                for g in range(G):
                    sp.wait_ge(v_stored[g], b * (16 * NB) + 16 * (NB + 1))
                    sp.sem_inc(passed, 1)
                for s in range(4):
                    load_v2(s, slice(s * TILE, (s + 1) * TILE))

                def second(k, last):
                    for s in range(4):
                        T = b * T2 + k * 4 + s
                        nxt = bass.ds(k * (4 * TILE) + (s + 4) * TILE, TILE)
                        if not last:
                            sp.wait_ge(o_ready, T + 1)
                            sp.sem_inc(passed, 1)
                            load_v2(s, nxt)
                        sp.wait_ge(x1_ready, T * 3 + 3)
                        sp.sem_inc(passed, 1)
                        sp.dma_start(x1b[:, :, bass.ds(k * (4 * TILE) + s * TILE, TILE)], x2[:, s]).then_inc(x1_stored[s], 16)
                        if last:
                            continue
                        sp.wait_ge(bn_done, T + 1)
                        sp.sem_inc(passed, 1)
                        sp.wait_ge(x1_stored[s], b * (4 * T2) + k * 16 + 16)
                        sp.sem_inc(passed, 1)
                        load_x2(s, nxt)

                with sp.Fori(0, T2 // 4 - 1) as k:
                    second(k, False)
                second(T2 // 4 - 1, True)
                sp.wait_ge(batch_done, b + 1)
                sp.sem_inc(passed, 1)
                for s in range(4):
                    sp.wait_ge(x1_stored[s], b * (4 * T2) + 4 * T2)
                    sp.sem_inc(passed, 1)

            for dst, src in ((wT[:, 0], w_avg), (wT[:, 1], w_max), (wmx, w_mix_ch), (band, band_in)):
                sp.dma_start(dst, src).then_inc(l1_in, 16)
            sp.dma_start(selk[0:K7], sel_in).then_inc(l1_in, 16)
            sp.dma_start(wky[0:K7], w_mix_ky).then_inc(l1_in, 16)
            sp.wait_ge(l1_ready, 2)

            def load_x1(s, cols):
                for b in range(B):
                    sp.dma_start(xg[:, s, b], x1y[:, b, cols, :]).then_inc(xg_in[s], 16)

            for s in range(2):
                load_x1(s, slice(s * CG, (s + 1) * CG))

            def groups(k, last):
                for s in range(2):
                    sp.wait_ge(og_ready, k * (2 * CG) + CG * (s + 1) + 2)
                    sp.sem_inc(passed, 1)
                    for b in range(B):
                        sp.dma_start(outy[:, b, bass.ds(k * (2 * CG) + s * CG, CG), :], og[:, s, b]).then_inc(og_stored[s], 16)
                    if not last:
                        load_x1(s, bass.ds(k * (2 * CG) + (s + 2) * CG, CG))

            with sp.Fori(0, NCG // 2 - 1) as k:
                groups(k, False)
            groups(NCG // 2 - 1, True)
            for s in range(2):
                sp.wait_ge(og_stored[s], 16 * B * (NCG // 2 + 1))

        @block.gpsimd
        def _(pool):
            nc.gpsimd.memset(ones[:], 1.0).then_inc(const_set, 1)
            nc.gpsimd.memset(mean_c[:], 1.0 / C).then_inc(const_set, 1)
            nc.gpsimd.memset(zero1[:], 0.0).then_inc(const_set, 1)
            nc.gpsimd.memset(eps_gn[:], EPS_GN).then_inc(const_set, 1)
            nc.gpsimd.memset(ubuf, 0.0).then_inc(const_set, 1)
            pool.wait_ge(const_set, 5)
            for g in range(G):
                pool.sem_inc(halo_ready, 1)

            def halo(n, i, odd, seen, idx=None):
                for g in range(G):
                    pool.wait_ge(tap_done, n * (G * OPS) + OPS * (g + 1))
                    pool.sem_inc(passed, 1)
                    rows = ubuf[:, 3 * g:3 * g + 3]
                    if i == NB - 1:
                        nc.gpsimd.memset(rows[:, :, 0:2, 1:W + 1], 0.0).then_inc(halo_ready, 1)
                    else:
                        nc.gpsimd.tensor_copy(rows[:, :, 0:2, 1:W + 1], rows[:, :, RB:RB + 2, 1:W + 1]).then_inc(halo_ready, 1)

            with pool.Fori(0, B) as b:
                blocks(pool, b, halo)
            pool.wait_ge(l1_ready, 2)
            nc.gpsimd.memset(ypad, 0.0).then_inc(pads_zero, 1)
            nc.gpsimd.memset(zhi, 0.0).then_inc(pads_zero, 1)
            nc.gpsimd.memset(zlo, 0.0).then_inc(pads_zero, 1)

        @block.scalar
        def _(act):
            A = nc.scalar.activation
            act.sem_inc(u_evicted, 3)
            act.sem_inc(sq_done, 2)
            act.sem_inc(qkT_evicted, 1)
            act.sem_inc(o_evicted, 2)
            act.sem_inc(ostd_ready, 1)
            act.sem_inc(chb_set, 2)
            act.wait_ge(const_set, 5)

            def group_root(step):
                act.wait_ge(gvar_ready, step)
                A(gn_r[:], gn_tmp[:], ACT.Sqrt, bias=eps_gn[:, 0:1]).then_inc(gstd_ready, 1)

            group_root(1)

            def make_y(n, odd, seen, parts=range(2 * G)):
                for part in parts:
                    if part == 0:
                        act.wait_ge(x_in[odd], seen * 16 + 16)
                    g = part % G
                    ins = A(ysq[:, g] if part < G else xin[:, odd, g], xin[:, odd, g],
                            ACT.Square if part < G else ACT.Identity, bias=cur[:, 1, g:g + 1], scale=cur[:, 0, g:g + 1])
                    if part == 2 * G - 1:
                        ins.then_inc(y_ready, 1)

            def mean_squared(n):
                act.wait_ge(stat_ready, n + 1)
                A(mu2[:], ps[0:RB, 3, 0:W], ACT.Square, bias=zero1[0:RB, 0:1]).then_inc(mu2_ready, 1)

            def root(n):
                act.wait_ge(var_ready, n + 1)
                A(std[:], var[:], ACT.Sqrt, bias=eps_gn[0:RB, 0:1]).then_inc(std_ready, 1)

            def evict_u(n, t, i, odd):
                r0, r1 = rows_of(i)
                m, j = t // HALVES, t % HALVES
                g, q = m // 3, m % 3
                if q == 0 and j == 0:
                    act.wait_ge(halo_ready, n * G + (g + 1))
                act.wait_ge(u_ready, n * U_TILES + (t + 1))
                A(ubuf[:, m, 2 + ROWS_T * j:2 + ROWS_T * (j + 1), 1:W + 1],
                  ps[:, t % 3, :].rearrange("p (r w) -> p r w", w=W),
                  ACT.Identity, bias=bias_u[:, m:m + 1]).then_inc(u_evicted, 1)
                if j < HALVES - 1:
                    return
                act.wait_ge(u_evicted, n * U_TILES + (t + 1) + 3)
                if q == 2:
                    act.wait_ge(v_stored[g], n * 16 + 16)
                    dst = accv[:, g]
                else:
                    dst = accs[:, odd, 2 * g + q]
                A(dst[:, r0 * W:r1 * W].rearrange("p (r w) -> p r w", w=W), ubuf[:, m, r0 + 1:r1 + 1, 1:W + 1],
                  ACT.Copy, scale=dw[:, m, 4:5]).then_inc(centre_ready, 1)

            def square(n, i, odd, idx, c):
                r0, r1 = rows_of(i)
                if c == 0:
                    act.wait_ge(tap_done, n * (G * OPS) + G * OPS)
                g, q = c // 2, c % 2
                col = norms[:, q, g, bass.ds(idx, 1)] if i is None else norms[:, q, g, i:i + 1]
                act.wait_ge(sq_done, n * (2 * G) + (c + 1))
                act.sem_inc(passed, 1)
                A(junk[:, c % 2, r0 * W:r1 * W], accs[:, odd, c, r0 * W:r1 * W], ACT.Square, bias=zero1[:, 0:1],
                  accum_out=col).then_inc(sq_done, 1)

            def evict_turned(n, i, r):
                r0, r1 = rows_of(i)
                if not r0 <= r < r1:
                    return
                act.wait_ge(qkT_ready, n * RB + r)
                act.wait_ge(gram_done, n * RB + r)
                A(qkT[:, r % 2, 0], ps[:, 5, 0:C], ACT.Copy)
                A(qkT[:, r % 2, 1], ps[:, 6, 0:C], ACT.Copy).then_inc(qkT_evicted, 1)

            with act.Fori(0, B) as b:
                act.wait_ge(cur_set, b + 1)
                make_y(b * NB, 0, b * (NB // 2))
                mean_squared(b * NB)
                root(b * NB)

                def first(n, i, odd, seen, prev, idx):
                    more = i != NB - 1
                    for t in range(U_TILES):
                        evict_u(n, t, i, odd)
                        if t < 2 * G and more:
                            make_y(n + 1, 1 - odd, seen + odd, [t])
                        if t == STATS_AT and more:
                            mean_squared(n + 1)
                        if t == ROOT_AT and more:
                            root(n + 1)
                        if i != 0 and SQUARES_AT <= t < SQUARES_AT + 2 * G:
                            square(n - 1, prev, 1 - odd, idx - 1, t - SQUARES_AT)
                        if i != 0 and t >= GRAM_AT:
                            evict_turned(n - 1, prev, t - GRAM_AT)

                first(b * NB, 0, 0, b * (NB // 2), None, 0)
                first(b * NB + 1, None, 1, b * (NB // 2), 0, 1)
                with act.Fori(0, (NB - 4) // 2) as k:
                    first(b * NB + k * 2 + 2, None, 0, b * (NB // 2) + k + 1, None, k * 2 + 2)
                    first(b * NB + k * 2 + 3, None, 1, b * (NB // 2) + k + 1, None, k * 2 + 3)
                first(b * NB + (NB - 2), None, 0, b * (NB // 2) + (NB // 2 - 1), None, NB - 2)
                first(b * NB + (NB - 1), NB - 1, 1, b * (NB // 2) + (NB // 2 - 1), None, NB - 1)
                for c in range(2 * G):
                    square(b * NB + (NB - 1), NB - 1, 1, NB - 1, c)
                for r in range(RB + 2):
                    evict_turned(b * NB + (NB - 1), NB - 1, r)

                act.wait_ge(nsum_ready, b + 1)
                A(norm[:], norm[:], ACT.Sqrt, bias=zero1[:, 0:1]).then_inc(nroot_ready, 1)
                act.wait_ge(rk_ready, b + 1)
                A(rk_row, ps[:, 0, 0:C], ACT.Copy).then_inc(rk_copied, 1)
                act.wait_ge(smx_ready, b + 1)
                for a in range(G):
                    cols = slice(WOFF[a], WOFF[a] + WIN[a][1] - WIN[a][0])
                    A(scores[:, cols], scores[:, cols], ACT.Exp, bias=smx[:, a:a + 1], accum_out=ssum[:, a:a + 1]
                      ).then_inc(exp_done, 1)
                act.wait_ge(at_ready, b + 1)
                A(at, ps[:, 2:5, 0:C], ACT.Copy).then_inc(at_copied, 1)

                with act.Fori(0, T2 // 4) as k:
                    for j in range(4):
                        T = b * T2 + k * 4 + j
                        s = 3 * (j % 2)
                        act.wait_ge(o_ready, T + 1)
                        A(osq[:, j % 2], ps[:, s:s + 3, :], ACT.Square, bias=zero1[:, 0:1]).then_inc(osq_ready, 1)
                        act.wait_ge(on_done, T + 1)
                        for a in range(G):
                            ins = A(ow[:, j, a], ps[:, s + a, :], ACT.Copy, scale=par["ln2_w"][:, a:a + 1])
                        ins.then_inc(o_evicted, 1)
                        act.wait_ge(ostat_ready, T + 1)
                        A(std2[:, j], ps[0:ROWS_T, 6, 0:W], ACT.Sqrt, bias=eps_gn[0:ROWS_T, 0:1]).then_inc(ostd_ready, 1)
                act.wait_ge(batch_done, b + 1)

            group_root(2)
            act.wait_ge(l1_in, 16 * 6)
            for g in range(G):
                ins = A(wsq[:, g], wmx[:, g], ACT.Square, bias=zero1[:, 0:1], accum_out=l1s[:, 0, g:g + 1])
            ins.then_inc(wnorm_done, 1)
            act.wait_ge(halo_ready, G * (B * NB + 1))
            act.wait_ge(gate_in, 1)
            A(l1v[:, 4], l1v[:, 3], ACT.Gelu, bias=zero1[:, 0:1]).then_inc(gelu_done, 1)
            act.wait_ge(gx2_ready, 1)
            A(l1v[:, 6], l1v[:, 5], ACT.Sqrt, bias=zero1[:, 0:1]).then_inc(gx_ready, 1)
            act.wait_ge(sig_ready, 1)
            A(sig, ps[:, 4, 0:C], ACT.Copy).then_inc(sig_set, 1)
            for t in range(4 * G):
                act.wait_ge(chb_ready, t + 1)
                v, g = t // G, t % G
                A(chb[:, v, P * g:P * (g + 1), :], ps[:, 6 + t % 2, :].rearrange("p (c b) -> p c b", b=B), ACT.Copy
                  ).then_inc(chb_set, 1)
            for r in range(K7):
                for q in range(6):
                    t = r * 6 + q
                    act.wait_ge(wf_ready, t + 1)
                    A(wfold[:, 64 * q:64 * (q + 1), 0:K7, r], ps[:, t % 4, 0:64 * K7].rearrange("p (c k) -> p c k", k=K7),
                      ACT.Copy).then_inc(wf_copied, 1)
            act.wait_ge(chb_set, 4 * G + 2)
            act.wait_ge(wf_copied, 6 * K7)
            act.sem_inc(l1_ready, 1)
            act.wait_ge(pads_zero, 3)
            with act.Fori(0, NCG // 2) as k:
                for s in range(2):
                    for c in range(CG):
                        K = k * (2 * CG) + (CG * s + c)
                        if c == 0:
                            act.wait_ge(xg_in[s], k * (16 * B) + 16 * B)
                        act.wait_ge(box_ready, K + 1)
                        act.wait_ge(conv_ready, K + 1)
                        act.sem_inc(passed, 1)
                        for b in range(B):
                            ins = A(zfull[:, c % 2, b], xg[:, s, b, c, :], ACT.Identity,
                                    bias=chb[:, 3, bass.ds(K, 1), b], scale=chb[:, 2, bass.ds(K, 1), b])
                        ins.then_inc(zfull_ready, 1)
                        for b in range(B):
                            A(ypad[:, c % 2, b, PAD:PAD + W], xg[:, s, b, c, :], ACT.Identity,
                              bias=chb[:, 1, bass.ds(K, 1), b], scale=chb[:, 0, bass.ds(K, 1), b])
                        act.wait_ge(zfull_ready, K + 1)
                        A(zhi[:, c % 2, :, PAD:PAD + W], zfull[:, c % 2], ACT.Copy).then_inc(yz_ready, 1)

        @block.tensor
        def _(pe):
            mm = pe.matmul
            pe.wait_ge(const_set, 5)
            pe.wait_ge(wraw_scaled, 1)
            for m in range(G):
                for k in range(G):
                    mm(ps[:, m, 0:C], mean_c[:], wc[:, k, C * m:C * (m + 1)], start=(k == 0), stop=(k == G - 1))
            for m in range(M9):
                for k in range(G):
                    ins = mm(ps[:, 3, m:m + 1], wraw[:, k, P * m:P * (m + 1)], par["ln1_b"][:, k:k + 1],
                             start=(k == 0), stop=(k == G - 1), skip_group_check=True)
            ins.then_inc(wmean_ready, 1)

            def group_sums(step):
                pe.wait_ge(gst_ready, step)
                for m in range(G):
                    for k in range(G):
                        ins = mm(ps[:, 4, 8 * m:8 * m + 8], member[:, k, P * m:P * (m + 1)],
                                 gn_st[:, k].rearrange("p b s -> p (b s)"), start=(k == 0), stop=(k == G - 1),
                                 skip_group_check=True)
                ins.then_inc(gsum_ready, 1)

            group_sums(1)

            def stats(n, odd):
                pe.wait_ge(y_ready, n + 1)
                pe.wait_ge(xn_ready, n * 2 + 2)
                for v, src in enumerate((xin[:, odd], ysq)):
                    for r in range(RB):
                        for k in range(G):
                            ins = mm(ps[0:RB, 3, W * v:W * (v + 1)], to_row[:, r, :], src[:, k, W * r:W * (r + 1)],
                                     start=(r == 0 and k == 0), stop=(r == RB - 1 and k == G - 1), skip_group_check=True)
                ins.then_inc(stat_ready, 1)

            def spread(n):
                pe.wait_ge(rstd_ready, n + 1)
                for j in range(HALVES):
                    for r in range(ROWS_T):
                        c = ROWS_T * j + r
                        ins = mm(ps[:, 3 + j, W * r:W * (r + 1)], from_row[:, c, :], rstd[:], start=True, stop=True)
                    ins.then_inc(bc_ready, 1)

            def u_tile(n, t, odd):
                m, j = t // HALVES, t % HALVES
                pe.wait_ge(u_evicted, n * U_TILES + (t + 1))
                for k in range(G):
                    ins = mm(ps[:, t % 3, :], wc[:, k, P * m:P * (m + 1)], xin[:, odd, k, TILE * j:TILE * (j + 1)],
                             start=(k == 0), stop=(k == G - 1))
                ins.then_inc(u_ready, 1)

            def turn(n, r, odd):
                pe.wait_ge(qkT_evicted, n * RB + r)
                for q in range(2):
                    for g in range(G):
                        ins = pe.transpose(ps[:, 5 + q, P * g:P * (g + 1)], accs[:, odd, 2 * g + q, W * r:W * (r + 1)], ident[:])
                ins.then_inc(qkT_ready, 1)

            def gram_row(n, r, start, stop):
                pe.wait_ge(qkT_evicted, n * RB + r + 1)
                for a in range(G):
                    lo, hi = WIN[a]
                    ins = mm(ps[:, 7, WOFF[a]:WOFF[a] + hi - lo], qkT[:, r % 2, 0, P * a:P * (a + 1)],
                             qkT[:, r % 2, 1, lo:hi], start=(start and a == 0), stop=stop, skip_group_check=True)
                ins.then_inc(gram_done, 1)

            def gram_step(n, i, odd, r):
                r0, r1 = rows_of(i)
                if r == r0:
                    pe.wait_ge(tap_done, n * (G * OPS) + G * OPS)
                if r0 < r <= r1:
                    gram_row(n, r - 1, i == 0 and r - 1 == r0, i == NB - 1 and r == r1)
                if r0 <= r < r1:
                    turn(n, r, odd)

            with pe.Fori(0, B) as b:
                pe.wait_ge(cur_set, b + 1)
                stats(b * NB, 0)
                spread(b * NB)

                def first(n, i, odd, prev):
                    more = i != NB - 1
                    pe.wait_ge(xn_ready, n * 2 + 4)
                    for t in range(U_TILES):
                        u_tile(n, t, odd)
                        if t == STATS_AT and more:
                            stats(n + 1, 1 - odd)
                        if t == SPREAD_AT and more:
                            spread(n + 1)
                        if i != 0 and t >= GRAM_AT:
                            gram_step(n - 1, prev, 1 - odd, t - GRAM_AT)

                first(b * NB, 0, 0, None)
                first(b * NB + 1, None, 1, 0)
                with pe.Fori(0, (NB - 4) // 2) as k:
                    first(b * NB + k * 2 + 2, None, 0, None)
                    first(b * NB + k * 2 + 3, None, 1, None)
                first(b * NB + (NB - 2), None, 0, None)
                first(b * NB + (NB - 1), NB - 1, 1, None)
                for r in range(RB + 2):
                    gram_step(b * NB + (NB - 1), NB - 1, 1, r)

                pe.wait_ge(diag_ready, b + 1)
                mm(ps[:, 0, 0:C], ones[:], diag[:].rearrange("p g c -> p (g c)"), start=True, stop=True).then_inc(rk_ready, 1)
                pe.wait_ge(a_ready, b + 1)
                for a in range(G):
                    ins = mm(ps[:, 1, 0:C], mean_c[:], a_full[:, a], start=(a == 0), stop=(a == G - 1))
                ins.then_inc(cm_ready, 1)
                pe.wait_ge(ac_ready, b + 1)
                for k in range(G):
                    for a in range(G):
                        ins = pe.transpose(ps[:, 2 + k, P * a:P * (a + 1)], a_cent[:, a, P * k:P * (k + 1)], ident[:])
                ins.then_inc(at_ready, 1)
                pe.wait_ge(at_copied, b + 1)

                def make_o(T, j, loaded, chunks):
                    s = 3 * (j % 2)
                    if chunks[0] == 0:
                        pe.wait_ge(v2_in[j], loaded)
                        pe.wait_ge(o_evicted, T + 1)
                    for a in chunks:
                        for k in range(G):
                            ins = mm(ps[:, s + a, :], at[:, k, P * a:P * (a + 1)],
                                     vin[:, j, k], start=(k == 0), stop=(k == G - 1))
                    if chunks[-1] == G - 1:
                        ins.then_inc(o_ready, 1)

                def mean_of_squares(T, j):
                    pe.wait_ge(osq_ready, T + 1)
                    pe.wait_ge(ostd_ready, T + 1)
                    for r in range(ROWS_T):
                        for k in range(G):
                            ins = mm(ps[0:ROWS_T, 6, 0:W], to_row[:, r, 0:ROWS_T], osq[:, j % 2, k, W * r:W * (r + 1)],
                                     start=(r == 0 and k == 0), stop=(r == ROWS_T - 1 and k == G - 1))
                    ins.then_inc(ostat_ready, 1)

                def spread_o(T, j):
                    pe.wait_ge(orstd_ready, T + 1)
                    pe.wait_ge(on_done, T + 4)
                    for r in range(ROWS_T):
                        ins = mm(ps[:, 7, W * r:W * (r + 1)], from_row[0:ROWS_T, r, :], rstd2[:, j], start=True, stop=True)
                    ins.then_inc(obc_ready, 1)

                def second(k, last):
                    for j in range(4):
                        T = b * T2 + k * 4 + j
                        if not (last and j == 3):
                            make_o(T + 1, (j + 1) % 4, None, range(1, G))
                        mean_of_squares(T, j)
                        if not (last and j >= 2):
                            nxt = (j + 2) % 4
                            make_o(T + 2, nxt, b * (4 * T2) + k * 16 + (16 if nxt >= 2 else 32), [0])
                        spread_o(T, j)

                make_o(b * T2, 0, b * (4 * T2) + 16, range(G))
                make_o(b * T2 + 1, 1, b * (4 * T2) + 16, [0])
                with pe.Fori(0, T2 // 4 - 1) as k:
                    second(k, False)
                second(T2 // 4 - 1, True)

            group_sums(2)
            pe.wait_ge(l1_in, 16 * 6)
            pe.wait_ge(batch_done, B)
            pe.wait_ge(diag_ready, B + 1)
            mm(ps[:, 0, 0:C], ones[:], diag[:].rearrange("p g c -> p (g c)"), start=True, stop=True).then_inc(wdiv_ready, 1)
            pe.wait_ge(pool_ready, 1)
            for m in range(G):
                for k in range(G):
                    for v in range(2):
                        ins = mm(ps[:, 3, B * m:B * (m + 1)], wT[:, v, k, P * m:P * (m + 1)], pooled[v][:, k, :],
                                 start=(k == 0 and v == 0), stop=(k == G - 1 and v == 1), skip_group_check=True)
            ins.then_inc(gate_ready, 1)
            pe.wait_ge(gx_ready, 1)
            for k in range(G):
                ins = mm(ps[:, 5, 0:B], mean_c[:], gxv[:, k, :], start=(k == 0), stop=(k == G - 1))
            ins.then_inc(gxm_ready, 1)
            pe.wait_ge(diag_ready, B + 2)
            mm(ps[:, 4, 0:C], ones[:], diag[:].rearrange("p g c -> p (g c)"), start=True, stop=True).then_inc(sig_ready, 1)
            for t in range(4 * G):
                pe.wait_ge(d4_ready, t + 1)
                pe.wait_ge(chb_set, t + 1)
                mm(ps[:, 6 + t % 2, :], ones[:], d4[:, t % 2].rearrange("p c b -> p (c b)"), start=True, stop=True
                   ).then_inc(chb_ready, 1)
            pe.wait_ge(wky_scaled, 1)
            for r in range(K7):
                for q in range(6):
                    t = r * 6 + q
                    pe.wait_ge(wf_lo, t + 1)
                    mm(ps[:, t % 4, 0:64 * K7], selk[0:K7, r, :], wky[0:K7, 64 * K7 * q:64 * K7 * (q + 1)],
                       start=True, stop=True).then_inc(wf_ready, 1)
            pe.sem_inc(conv_ready, 2)
            with pe.Fori(0, NCG // 2) as k:
                for s in range(2):
                    for c in range(CG):
                        K = k * (2 * CG) + (CG * s + c)
                        pe.wait_ge(yz_ready, K + 1)
                        pe.wait_ge(toep_ready, K + 1)
                        pe.wait_ge(og_ready, K + 1)
                        res = ps[:, c % 2, :].rearrange("p (b w) -> p b w", b=B)
                        for plane in range(2 * K7):
                            kx = plane % K7
                            mm(res, toep[:, c % 2, plane, 0:P], zhi[:, c % 2, :, kx:kx + W], start=(plane == 0), stop=False)
                        pe.wait_ge(zlo_ready, K + 1)
                        for kx in range(K7):
                            mm(res, toep[:, c % 2, kx, 0:P], zlo[:, c % 2, :, kx:kx + W], start=False, stop=False)
                        pe.wait_ge(box_ready, K + 3)
                        mm(res, band[:, 0:P], box[:, c % 2], start=False, stop=True).then_inc(conv_ready, 1)

        @block.vector
        def _(dve):
            V = nc.vector
            count = [0]

            def then(ins):
                count[0] += 1
                ins.then_inc(chain, 1)
                dve.wait_ge(chain, count[0])

            dve.sem_inc(gn_used, 2)
            dve.sem_inc(xn_ready, 2)
            dve.sem_inc(gram_done, 2)
            dve.sem_inc(on_done, 4)
            for g in range(G):
                dve.sem_inc(v_stored[g], 16)
            dve.wait_ge(par_in, 16 * 8)
            for k in range(G):
                ins = V.tensor_scalar(wc[:, k], wraw[:, k], par["ln1_w"][:, k:k + 1], None, ALU.mult)
            ins.then_inc(wraw_scaled, 1)
            dve.wait_ge(wmean_ready, 1)
            dve.wait_ge(wraw_scaled, 1)
            for k in range(G):
                ins = V.tensor_tensor(wc[:, k].rearrange("p (a n) -> p a n", a=G), wc[:, k].rearrange("p (a n) -> p a n", a=G),
                                      ps[:, 0:3, 0:C], ALU.subtract)
            ins.then_inc(wc_ready, 1)
            V.tensor_copy(bias_u[:], ps[:, 3, 0:M9]).then_inc(wc_ready, 1)
            gnbn_n = gnbn.rearrange("p g b t s -> p (g b) t s")
            with dve.Fori(0, B) as b:
                for g in range(G):
                    for q in range(GN_LOADS):
                        dve.wait_ge(gn_in[q % 2], b * (8 * G * GN_LOADS) + 16 * ((g * GN_LOADS + q) // 2 + 1))
                        dve.sem_inc(passed, 1)
                        for t in range(GN_COLS // 512):
                            ins = V.bn_stats(gnbn[:, g, bass.ds(b, 1), q * (GN_COLS // 512) + t, :].rearrange("p a s -> p (a s)"),
                                             gnx[:, q % 2, 512 * t:512 * (t + 1)])
                        ins.then_inc(gn_used, 1)
            dve.wait_ge(gn_used, B * G * GN_LOADS + 2)
            for g in range(G):
                for b in range(B):
                    ins = V.bn_aggr(gn_st[:, g, b, :], gnbn[:, g, b].rearrange("p t s -> p (t s)"))
            then(ins)

            def group_norm(step, r, nb):
                dve.wait_ge(gsum_ready, step)
                gs = ps[:, 4, 0:8 * G].rearrange("p (g b s) -> p g b s", g=G, b=B)
                then(V.tensor_copy(gn_mean[:], gs[:, :, :, 0]))
                then(V.tensor_tensor(gn_tmp[:], gn_mean[:], gn_mean[:], ALU.mult))
                V.tensor_tensor(gn_tmp[:], gs[:, :, :, 1], gn_tmp[:], ALU.subtract).then_inc(gvar_ready, 1)
                dve.wait_ge(gstd_ready, step)
                then(V.reciprocal(r, gn_r[:]))
                then(V.scalar_tensor_tensor(out=nb, in0=gn_mean[:], scalar=-1.0, in1=r, op0=ALU.mult, op1=ALU.mult))

            then(V.tensor_tensor(gn_tmp[:], gn_st[:, :, :, 0], gn_st[:, :, :, 0], ALU.mult))
            V.tensor_tensor(gn_st[:, :, :, 1], gn_st[:, :, :, 1], gn_tmp[:], ALU.add).then_inc(gst_ready, 1)
            group_norm(1, gn_r[:], gn_nb[:])

            def variance(n):
                dve.wait_ge(mu2_ready, n + 1)
                V.tensor_tensor(var[:], ps[0:RB, 3, W:2 * W], mu2[:], ALU.subtract).then_inc(var_ready, 1)

            def invert(n):
                dve.wait_ge(std_ready, n + 1)
                V.reciprocal(rstd[:], std[:]).then_inc(rstd_ready, 1)

            def normalise(n, odd):
                for j in range(HALVES):
                    dve.wait_ge(bc_ready, n * 2 + (j + 1))
                    px = xin[:, odd, :, TILE * j:TILE * (j + 1)]
                    V.tensor_tensor(px, px, ps[:, 3 + j:4 + j, :].broadcast_to([P, G, TILE]), ALU.mult).then_inc(xn_ready, 1)

            def taps(n, g, i, odd, between=None):
                r0, r1 = rows_of(i)
                dve.wait_ge(centre_ready, n * M9 + 3 * (g + 1))
                base = n * (G * OPS) + OPS * g
                for t, (dy, dx) in enumerate(TAPS):
                    if t == 3 and between:
                        between()
                    for q in range(3):
                        m = 3 * g + q
                        acc = accv[:, g] if q == 2 else accs[:, odd, 2 * g + q]
                        acc = acc[:, r0 * W:r1 * W].rearrange("p (r w) -> p r w", w=W)
                        if t:
                            dve.wait_ge(tap_done, base + (3 * t + q - 2))
                        V.scalar_tensor_tensor(out=acc, in0=ubuf[:, m, r0 + dy:r1 + dy, dx:dx + W],
                                               scalar=dw[:, m, 3 * dy + dx:3 * dy + dx + 1], in1=acc,
                                               op0=ALU.mult, op1=ALU.add).then_inc(tap_done, 1)

            with dve.Fori(0, B) as b:
                V.tensor_copy(cur[:, 0], gn_r[:, :, bass.ds(b, 1)].rearrange("p g a -> p (g a)"))
                V.tensor_copy(cur[:, 1], gn_nb[:, :, bass.ds(b, 1)].rearrange("p g a -> p (g a)")).then_inc(cur_set, 1)
                variance(b * NB)
                invert(b * NB)
                normalise(b * NB, 0)

                def first(n, i, odd, seen, idx=None):
                    more = i != NB - 1
                    taps(n, 0, i, odd)
                    if more:
                        variance(n + 1)
                    taps(n, 1, i, odd, (lambda: invert(n + 1)) if more else None)
                    if more:
                        normalise(n + 1, 1 - odd)
                    taps(n, 2, i, odd)

                blocks(dve, b, first)

                step = [0]

                def thus(ins):
                    step[0] += 1
                    ins.then_inc(small, 1)
                    dve.wait_ge(small, b * SMALL + step[0])

                dve.wait_ge(sq_done, b * (2 * G * NB) + (2 * G * NB + 2))
                V.tensor_reduce(norm[:], norms[:], AX.X, ALU.add).then_inc(nsum_ready, 1)
                dve.wait_ge(gram_done, b * H + (H + 2))
                thus(V.memset(a_full, 0.0))
                dve.wait_ge(nroot_ready, b + 1)
                thus(V.tensor_scalar(norm[:], norm[:], EPS_NORM, None, ALU.max))
                thus(V.reciprocal(rnorm[:], norm[:]))
                V.tensor_tensor(rqs[:], rnorm[:, 0], par["scale"], ALU.mult)
                for g in range(G):
                    ins = V.tensor_scalar(diag[:, g], ident[:], rnorm[:, 1, g:g + 1], None, ALU.mult)
                ins.then_inc(diag_ready, 1)
                dve.wait_ge(diag_ready, b + 1)
                dve.wait_ge(rk_copied, b + 1)
                for a in range(G):
                    cols = slice(WOFF[a], WOFF[a] + WIN[a][1] - WIN[a][0])
                    ins = V.scalar_tensor_tensor(out=scores[:, cols], in0=ps[:, 7, cols], scalar=rqs[:, a:a + 1],
                                                 in1=rk_row[:, WIN[a][0]:WIN[a][1]], op0=ALU.mult, op1=ALU.mult)
                thus(ins)
                thus(V.tensor_tensor(scores[:], scores[:], hmask[:], ALU.add))
                for a in range(G):
                    cols = slice(WOFF[a], WOFF[a] + WIN[a][1] - WIN[a][0])
                    ins = V.tensor_reduce(smx[:, a:a + 1], scores[:, cols], AX.X, ALU.max)
                thus(ins)
                V.tensor_scalar(smx[:], smx[:], -1.0, None, ALU.mult).then_inc(smx_ready, 1)
                dve.wait_ge(exp_done, b * 3 + 3)
                thus(V.reciprocal(rsum[:], ssum[:]))
                for a in range(G):
                    cols = slice(WOFF[a], WOFF[a] + WIN[a][1] - WIN[a][0])
                    ins = V.tensor_scalar(a_full[:, a, WIN[a][0]:WIN[a][1]], scores[:, cols], rsum[:, a:a + 1], None, ALU.mult)
                ins.then_inc(a_ready, 1)
                dve.wait_ge(a_ready, b + 1)
                dve.wait_ge(cm_ready, b + 1)
                V.tensor_tensor(a_cent, a_full, ps[:, 1:2, 0:C].broadcast_to([P, G, C]), ALU.subtract).then_inc(ac_ready, 1)

                with dve.Fori(0, T2 // 4) as k:
                    for j in range(4):
                        T = b * T2 + k * 4 + j
                        dve.wait_ge(ostd_ready, T + 2)
                        V.reciprocal(rstd2[:, j], std2[:, j]).then_inc(orstd_ready, 1)
                        dve.wait_ge(obc_ready, T + 1)
                        dve.wait_ge(o_evicted, T + 3)
                        V.tensor_tensor(ow[:, j], ow[:, j], ps[:, 7:8, :].broadcast_to([P, G, TILE]), ALU.mult
                                        ).then_inc(on_done, 1)
                        dve.wait_ge(x2_in[j], b * (4 * T2) + k * 16 + 16)
                        dve.wait_ge(on_done, T + 5)
                        px = x2[:, j]
                        for a in range(G):
                            V.scalar_tensor_tensor(out=px[:, a], in0=px[:, a], scalar=par["ln2_b"][:, a:a + 1],
                                                   in1=ow[:, j, a], op0=ALU.add, op1=ALU.add).then_inc(x1_ready, 1)
                        dve.wait_ge(x1_ready, b * (3 * T2) + k * 12 + 3 * (j + 1))
                        dve.sem_inc(passed, 1)
                        for a in range(G):
                            V.bn_stats(bn2[:, a, bass.ds(k * 4 + j, 1), :].rearrange("p a s -> p (a s)"), px[:, a])
                        V.tensor_reduce(mx2[:, :, bass.ds(k * 4 + j, 1)], px, AX.X, ALU.max).then_inc(bn_done, 1)
                dve.wait_ge(bn_done, b * T2 + T2)
                dve.sem_inc(passed, 1)
                for a in range(G):
                    V.bn_aggr(aggr[:, a], bn2[:, a].rearrange("p t s -> p (t s)"))
                at_b = bass.ds(b, 1)
                thus(V.tensor_reduce(ch_max[:, :, at_b], mx2, AX.X, ALU.max))
                V.tensor_copy(ch_mean[:, :, at_b], aggr[:, :, 0:1])
                V.tensor_copy(gn_st[:, :, at_b, 0], aggr[:, :, 0:1])
                thus(V.tensor_tensor(gn_tmp[:, :, 0], aggr[:, :, 0], aggr[:, :, 0], ALU.mult))
                V.tensor_tensor(gn_st[:, :, at_b, 1], aggr[:, :, 1:2], gn_tmp[:, :, 0:1], ALU.add).then_inc(batch_done, 1)
                assert step[0] == SMALL, step[0]

            dve.wait_ge(batch_done, B)
            dve.sem_inc(gst_ready, 1)
            r2, nb2, zr, znb, yr, ynb = (l1v[:, i] for i in range(8, 14))
            wdiv, iwdiv, hi, lo, sigma, isigma, bsig = (l1s[:, i] for i in range(2, 9))
            dve.sem_inc(wf_lo, 4)
            group_norm(2, r2, nb2)
            then(V.tensor_tensor(pooled[0], ch_mean[:], r2, ALU.mult))
            then(V.tensor_tensor(pooled[0], pooled[0], nb2, ALU.add))
            then(V.tensor_tensor(pooled[1], ch_max[:], r2, ALU.mult))
            V.tensor_tensor(pooled[1], pooled[1], nb2, ALU.add).then_inc(pool_ready, 1)
            dve.wait_ge(l1_in, 16 * 6)
            V.tensor_reduce(hi, wmx, AX.X, ALU.max)
            then(V.tensor_reduce(lo, wmx, AX.X, ALU.min))
            then(V.scalar_tensor_tensor(out=wdiv, in0=lo, scalar=-1.0, in1=hi, op0=ALU.mult, op1=ALU.max))
            then(V.tensor_scalar(wdiv, wdiv, MIN_W, None, ALU.max))
            then(V.reciprocal(iwdiv, wdiv))
            for g in range(G):
                ins = V.tensor_scalar(diag[:, g], ident[:], iwdiv[:, g:g + 1], None, ALU.mult)
            ins.then_inc(diag_ready, 1)
            then(V.tensor_tensor(l1s[:, 1], par["b_avg"], par["b_max"], ALU.add))
            then(V.tensor_copy(band16, band))
            dve.wait_ge(wdiv_ready, 1)
            wky_c = wky[0:K7].rearrange("p (c k) -> p c k", k=K7)
            V.tensor_tensor(wky_c, wky_c, ps[0:K7, 0, 0:C].unsqueeze(2).broadcast_to([K7, C, K7]), ALU.mult).then_inc(wky_scaled, 1)
            dve.wait_ge(gate_ready, 1)
            V.tensor_tensor(l1v[:, 3], ps[:, 3, 0:B * G].rearrange("p (g b) -> p g b", b=B),
                            l1s[:, 1].unsqueeze(2).broadcast_to([P, G, B]), ALU.add).then_inc(gate_in, 1)
            dve.wait_ge(gelu_done, 1)
            dve.wait_ge(wnorm_done, 1)
            xw = l1v[:, 4]
            then(V.tensor_tensor(l1v[:, 7], xw, xw, ALU.mult))
            V.tensor_tensor(l1v[:, 5], l1v[:, 7], l1s[:, 0].unsqueeze(2).broadcast_to([P, G, B]), ALU.mult).then_inc(gx2_ready, 1)
            dve.wait_ge(gxm_ready, 1)
            then(V.tensor_scalar(mrow[:, 0], ps[:, 5, 0:B], EPS_NX, None, ALU.add))
            then(V.reciprocal(mrow[:, 1], mrow[:, 0]))
            then(V.tensor_tensor(l1v[:, 7], l1v[:, 6], mrow[:, 1:2].broadcast_to([P, G, B]), ALU.mult))
            then(V.tensor_tensor(l1v[:, 7], l1v[:, 7], xw, ALU.mult))
            then(V.tensor_tensor(l1v[:, 7], l1v[:, 7], par["gamma"].unsqueeze(2).broadcast_to([P, G, B]), ALU.mult))
            sv = l1v[:, 7]
            then(V.tensor_tensor(sv, sv, wdiv.unsqueeze(2).broadcast_to([P, G, B]), ALU.mult))
            V.tensor_reduce(hi, sv, AX.X, ALU.max)
            then(V.tensor_reduce(lo, sv, AX.X, ALU.min))
            then(V.scalar_tensor_tensor(out=sigma, in0=lo, scalar=-1.0, in1=hi, op0=ALU.mult, op1=ALU.max))
            then(V.tensor_scalar(sigma, sigma, MIN_S, None, ALU.max))
            for g in range(G):
                ins = V.tensor_scalar(diag[:, g], ident[:], sigma[:, g:g + 1], None, ALU.mult)
            ins.then_inc(diag_ready, 1)
            then(V.reciprocal(isigma, sigma))
            then(V.tensor_tensor(sv, sv, isigma.unsqueeze(2).broadcast_to([P, G, B]), ALU.mult))
            then(V.tensor_tensor(bsig, par["beta"], isigma, ALU.mult))
            V.tensor_tensor(zr, sv, r2, ALU.mult)
            V.tensor_tensor(znb, sv, nb2, ALU.mult)
            V.tensor_tensor(yr, r2, bsig.unsqueeze(2).broadcast_to([P, G, B]), ALU.mult)
            then(V.tensor_tensor(ynb, nb2, bsig.unsqueeze(2).broadcast_to([P, G, B]), ALU.mult))
            for t in range(4 * G):
                v, g = t // G, t % G
                if t >= 2:
                    dve.wait_ge(chb_ready, t - 1)
                V.tensor_tensor(d4[:, t % 2], ident[:].unsqueeze(2).broadcast_to([P, P, B]),
                                (yr, ynb, zr, znb)[v][:, g:g + 1, :].broadcast_to([P, P, B]), ALU.mult).then_inc(d4_ready, 1)
            for r in range(K7):
                for q in range(6):
                    t = r * 6 + q
                    dve.wait_ge(wf_copied, t + 1)
                    V.tensor_tensor(wfold[:, 64 * q:64 * (q + 1), K7:2 * K7, r],
                                    ps[:, t % 4, 0:64 * K7].rearrange("p (c k) -> p c k", k=K7),
                                    wfold[:, 64 * q:64 * (q + 1), 0:K7, r], ALU.subtract).then_inc(wf_lo, 1)
            dve.wait_ge(sig_set, 1)
            dve.wait_ge(chb_ready, 4 * G)
            dve.wait_ge(wnorm_done, 1)
            dve.wait_ge(wf_lo, 6 * K7 + 4)
            dve.sem_inc(l1_ready, 1)
            dve.sem_inc(box_ready, 2)
            dve.sem_inc(og_ready, 2)
            for s in range(2):
                dve.sem_inc(og_stored[s], 16 * B)

            def add_x1(K, s, c, first_of_group, k):
                dve.wait_ge(conv_ready, K + 3)
                if first_of_group:
                    dve.wait_ge(og_stored[s], k * (16 * B) + 16 * B)
                V.scalar_tensor_tensor(out=og[:, s, :, c, :], in0=ps[:, c % 2, :].rearrange("p (b w) -> p b w", b=B),
                                       scalar=sig[:, bass.ds(K, 1)], in1=xg[:, s, :, c, :], op0=ALU.mult, op1=ALU.add
                                       ).then_inc(og_ready, 1)

            def prepare(K, c):
                y = ypad[:, c % 2]
                dve.wait_ge(conv_ready, K + 1)
                V.tensor_tensor(toep[:, c % 2].rearrange("p k (q r) -> p k q r", r=K7),
                                wfold[:, bass.ds(K, 1)].rearrange("p a k r -> p (a k) r").unsqueeze(2).broadcast_to([P, 2 * K7, FOLD, K7]),
                                band16.rearrange("p (q r) -> p q r", r=K7).unsqueeze(1).broadcast_to([P, 2 * K7, FOLD, K7]),
                                ALU.mult).then_inc(toep_ready, 1)
                dve.wait_ge(yz_ready, K + 1)
                V.tensor_tensor(zlo[:, c % 2, :, PAD:PAD + W], zfull[:, c % 2], zhi[:, c % 2, :, PAD:PAD + W], ALU.subtract
                                ).then_inc(zlo_ready, 1)
                V.tensor_tensor(s2[:, :, 0:XP - 1], y[:, :, 0:XP - 1], y[:, :, 1:XP], ALU.add).then_inc(box_step, 1)
                dve.wait_ge(box_step, K * 3 + 1)
                V.tensor_tensor(s4[:, :, 0:XP - 3], s2[:, :, 0:XP - 3], s2[:, :, 2:XP - 1], ALU.add).then_inc(box_step, 1)
                dve.wait_ge(box_step, K * 3 + 2)
                V.tensor_tensor(s6, s4[:, :, 0:W], s2[:, :, 4:W + 4], ALU.add).then_inc(box_step, 1)
                dve.wait_ge(box_step, K * 3 + 3)
                V.tensor_tensor(box[:, c % 2], s6, y[:, :, 6:W + 6], ALU.add).then_inc(box_ready, 1)

            def channels(k, last):
                for s in range(2):
                    for c in range(CG):
                        K = k * (2 * CG) + (CG * s + c)
                        if not (last and s == 1 and c == CG - 1):
                            prepare(K + 1, c + 1)
                        add_x1(K, s, c, c == 0, k)

            prepare(0, 0)
            with dve.Fori(0, NCG // 2 - 1) as k:
                channels(k, False)
            channels(NCG // 2 - 1, True)


_IN = ["x", "w_qkv", "dw_qkv", "chans", "w_avg", "w_max", "w_mix_ch", "w_mix_ky",
       "ident", "member", "headmask", "band", "sel", "to_row", "from_row"]


def kernel(**inputs):
    import concourse.bacc as bacc
    from concourse.bass_utils import run_bass_kernel_spmd

    def split(a):
        a = np.asarray(a)
        return np.moveaxis(a.reshape((G, P) + a.shape[1:]), 0, 1)

    i = {k: np.asarray(v) for k, v in inputs.items()}
    w = np.stack([i[f"L0_conv_w{q}"].T.reshape(C, G, P) for q in "qkv"], axis=2)
    dwt = np.stack([i[f"L0_conv_dw{q}"].reshape(G, P, 9) for q in "qkv"], axis=1)
    vectors = [i["L0_conv_ln1_w"], i["L0_conv_ln1_b"], i["L0_conv_ln2_w"], i["L0_conv_ln2_b"],
               np.repeat(i["L0_conv_scale"].reshape(HEADS), HEAD), i["L1_conv_b_avg"], i["L1_conv_b_max"],
               i["L1_conv_gamma"].reshape(C), i["L1_conv_beta"].reshape(C)]
    w_mix = i["L1_conv_w_mix"]

    c = np.arange(C)
    member = np.where(c[:, None] // GN_SIZE == c[None, :] // GN_SIZE, 1.0 / GN_SIZE, 0.0)
    headmask = np.concatenate(
        [np.where((P * a + np.arange(P))[:, None] // HEAD == np.arange(*WIN[a])[None, :] // HEAD, 0.0, -1e30)
         for a in range(G)], axis=1)
    p, j, r = np.arange(P), np.arange(BAND), np.arange(K7)
    band = np.where(np.abs(p[:, None] - j[None, :]) <= PAD, 1.0, 0.0)
    sel = np.where(((p[None, :] - r[:, None] + PAD) % K7)[None] == r[:, None, None], 1.0, 0.0)

    arrays = {
        "x": i["x"], "w_qkv": split(w.reshape(C, M9 * P)),
        "dw_qkv": dwt.reshape(M9, P, 9).transpose(1, 0, 2),
        "chans": np.stack([split(v) for v in vectors], axis=1),
        "w_avg": split(i["L1_conv_w_avg"].T), "w_max": split(i["L1_conv_w_max"].T),
        "w_mix_ch": split(w_mix), "w_mix_ky": w_mix.reshape(C, K7, K7).transpose(1, 0, 2).reshape(K7, C * K7),
        "ident": np.eye(P), "member": split(member), "headmask": headmask, "band": band, "sel": sel,
        "to_row": np.broadcast_to(np.eye(RB) / C, (P, RB, RB)),
        "from_row": np.broadcast_to(np.eye(RB)[:, :, None], (RB, RB, P)),
    }
    nc = bacc.Bacc("TRN2", target_bir_lowering=False, num_devices=1)
    given, args = {}, []
    for name in _IN:
        a = arrays[name]
        if name in ("ident", "member", "headmask", "band", "sel", "to_row", "from_row"):
            a = a.astype(np.float32)
        a = np.ascontiguousarray(a)
        given[f"in_{name}"] = a
        args.append(nc.dram_tensor(f"in_{name}", a.shape, mybir.dt.from_np(a.dtype), kind="ExternalInput").ap())
    out = nc.dram_tensor("out_0", (B, C, H, W), F32, kind="ExternalOutput").ap()
    build(nc, *args, out)
    r = run_bass_kernel_spmd(nc, [given], core_ids=[0])
    return r.results[0]["out_0"]
```

```python
from contextlib import ExitStack

import numpy as np

import concourse.bass as bass
from concourse import mybir

F32 = mybir.dt.float32
F16 = mybir.dt.float16
ALU = mybir.AluOpType
ACT = mybir.ActivationFunctionType
AX = mybir.AxisListType

P = 128
B, C, H, W = 4, 384, 128, 128
HW = H * W
G = C // P
GN_SIZE = C // 32
HEADS = 8
HEAD = C // HEADS
EPS_GN = 1e-5
EPS_LN = 1e-5
EPS_NORM = 1e-12
EPS_NX = 1e-6

RB = 8
NB = H // RB
PX = RB * W
TILE = 512
HALVES = PX // TILE
ROWS_T = TILE // W
M9 = 3 * G
U_TILES = M9 * HALVES
TAPS = [(dy, dx) for dy in range(3) for dx in range(3) if (dy, dx) != (1, 1)]
NT = len(TAPS)
PE_M = 2
PE_TAPS = [(1, 1)] + TAPS[:4]
SKIP = len(PE_TAPS) - 1
OPS = 3 * NT
B_OPS = G * OPS - SKIP
PE_TAPS_AT = 3 * HALVES
STATS_AT = 6 * HALVES - 1
ROOT_AT = 7 * HALVES
SQUARES_AT = 4 * HALVES - 2
SPREAD_AT = 8 * HALVES
GRAM_AT = U_TILES - RB - 2
WIN = [((P * a) // HEAD * HEAD, -(-(P * (a + 1)) // HEAD) * HEAD) for a in range(G)]
WOFF = [sum(hi - lo for lo, hi in WIN[:a]) for a in range(G)]
WCOLS = sum(hi - lo for lo, hi in WIN)

T2 = HW // TILE

K7 = 7
PAD = K7 // 2
FOLD = -(-P // K7)
BAND = FOLD * K7
CG = 4
NCG = C // CG
XP = W + 2 * PAD
MIN_W = 1e-30
MIN_S = 1e-12
W_TOP = 1024.0
S_TOP = 64.0
assert S_TOP * (GN_SIZE * HW) ** 0.5 < 65504
GN_COLS = 4096
GN_LOADS = HW // GN_COLS

ARENA = 46720

CH_NAMES = ["ln1_w", "ln1_b", "ln2_w", "ln2_b", "scale", "b_avg", "b_max", "gamma", "beta"]


def build(nc, x, w_qkv, dw_qkv, chans, w_avg, w_max, w_mix_ch, w_mix_ky,
          ident_in, member_in, headmask_in, band_in, sel_in,
          to_row_in, from_row_in, out):
    ctx = ExitStack()
    with ctx:
        def sb(name, shape):
            return ctx.enter_context(nc.sbuf_tensor(name, shape, F32))

        def sem(name):
            return ctx.enter_context(nc.semaphore(name))

        v_dram = nc.dram_tensor("v_scratch", (B, C, HW), F32, kind="Internal").ap()
        x1_dram = nc.dram_tensor("x1_scratch", (B, C, HW), F32, kind="Internal").ap()

        ps = ctx.enter_context(nc.psum_tensor("ps", [P, 8, 512], F32))

        ident = sb("ident", [P, P])
        ones = sb("ones", [P, P])
        mean_c = sb("mean_c", [P, P])
        zero1 = sb("zero1", [P, 1])
        eps_gn = sb("eps_gn", [P, 1])
        member = sb("member", [P, G, C])
        ch = sb("ch", [P, len(CH_NAMES), G])
        par = {n: ch[:, i, :] for i, n in enumerate(CH_NAMES)}
        dw = sb("dw", [P, M9, 9])
        bias_u = sb("bias_u", [P, M9])
        gn_st = sb("gn_st", [P, G, B, 2])
        gn_tmp = sb("gn_tmp", [P, G, B])
        gn_mean = sb("gn_mean", [P, G, B])
        gn_r = sb("gn_r", [P, G, B])
        gn_nb = sb("gn_nb", [P, G, B])
        ch_mean = sb("ch_mean", [P, G, B])
        ch_max = sb("ch_max", [P, G, B])
        aggr = sb("aggr", [P, 2, G, 2])
        mu2 = sb("mu2", [RB, W])
        var = sb("var", [RB, W])
        std = sb("std", [RB, W])
        rstd = sb("rstd", [RB, W])
        norms = sb("norms", [P, 2, G, NB])
        norm = sb("norm", [P, 2, G])
        rnorm = sb("rnorm", [P, 2, G])
        rqs = sb("rqs", [P, G])
        smx = sb("smx", [P, G])
        ssum = sb("ssum", [P, G])
        rsum = sb("rsum", [P, G])
        std2 = sb("std2", [ROWS_T, 2, W])
        rstd2 = sb("rstd2", [ROWS_T, 2, W])
        to_row = sb("to_row", [P, RB, RB])
        from_row = sb("from_row", [RB, RB, P])
        diag = sb("diag", [P, G, P])
        tap_diag = sb("tap_diag", [P, len(PE_TAPS), P])
        scores = sb("scores", [P, WCOLS])
        hmask = sb("hmask", [P, WCOLS])
        cur = sb("cur", [P, 2, G])

        arena = sb("arena", [P, ARENA])

        def carve(start, *dims):
            n = int(np.prod(dims))
            v = arena[:, start:start + n]
            names = "abcd"[:len(dims)]
            if len(dims) > 1:
                v = v.rearrange(f"p ({' '.join(names)}) -> p {' '.join(names)}",
                                **{k: d for k, d in zip(names, dims)})
            return v, start + n

        def carve16(start, *dims):
            words = -(-int(np.prod(dims)) // 2)
            v = arena[:, start:start + words].bitcast(F16)[:, 0:int(np.prod(dims))]
            names = "abcd"[:len(dims)]
            if len(dims) > 1:
                v = v.rearrange(f"p ({' '.join(names)}) -> p {' '.join(names)}",
                                **{k: d for k, d in zip(names, dims)})
            return v, start + words

        o = 0
        xin, o = carve(o, 2, G, PX)
        o_ysq = o
        ysq, o = carve(o, G, PX)
        o_ubuf = o
        ubuf, o = carve(o, M9, RB + 3, W + 2)
        o_acc = o
        accs, o = carve(o, 2, 2 * G, (RB + 1) * W)
        accv, o = carve(o, G, (RB + 1) * W)
        o_end_acc = o
        wc, o = carve(o, G, M9 * P)
        o_qkT = o
        qkT, o = carve(o, 2, 2, C)
        junk, o = carve(o, 2, (RB + 1) * W)
        end_l0 = o
        assert o <= ARENA, o
        wraw, _ = carve(o_acc, G, M9 * P)
        gnx, o = carve(0, 2, GN_COLS)
        assert o <= o_ubuf
        a_full, o = carve(o_qkT, G, C)
        a_cent, o = carve(o, G, C)
        rk_row, o = carve(o, C)
        at, o = carve(o, G, C)
        assert o <= end_l0
        o = o_acc
        vin, o = carve(o, 4, G, TILE)
        x2, _ = carve(0, 4, G, TILE)
        ow, o = carve(o, 4, G, TILE)
        osq, o = carve(o, 2, G, TILE)
        bn2, o = carve(o, G, T2, 6)
        mx2, o = carve(o, G, T2)
        gnb, o = carve(o, G, T2, 6)
        assert o <= o_end_acc, (o, o_end_acc)
        gx, o = carve(o_ysq, 2, G, TILE)
        assert o <= o_ubuf
        o = 0
        wfold, o = carve16(o, C, 2 * K7, K7)
        chb, o = carve(o, 4, C, B)
        sig, o = carve(o, C)
        band, o = carve(o, BAND)
        band16, o = carve16(o, BAND)
        toep, o = carve16(o, 2, 2 * K7, BAND)
        o_tmp = o
        xg, o = carve(o, 2, B, CG, W)
        og, o = carve(o, 2, B, CG, W)
        ypad, o = carve(o, 2, B, XP)
        zfull, o = carve(o, 2, B, W)
        zhi, o = carve16(o, 2, B, XP)
        zlo, o = carve16(o, 2, B, XP)
        s2, o = carve(o, B, XP)
        s4, o = carve(o, B, XP)
        s6, o = carve(o, B, W)
        box, o = carve(o, 2, B, W)
        assert o <= ARENA, o
        wT, o_l1 = carve(o_tmp, 2, G, C)
        selk, o_l1 = carve(o_l1, K7, P)
        wky, o_l1 = carve(o_l1, C * K7)
        selk16, o_l1 = carve16(o_l1, K7, P)
        wky16, o_l1 = carve16(o_l1, 2, C * K7)
        d4, o_l1 = carve(o_l1, 2, P, B)
        wmx, o_l1 = carve(o_l1, G, K7 * K7)
        wsq, o_l1 = carve(o_l1, G, K7 * K7)
        assert o_l1 <= o, o_l1
        l1v = sb("l1v", [P, 16, G, B])
        l1s = sb("l1s", [P, 10, G])
        mrow = sb("mrow", [P, 2, B])

        par_in = sem("par_in")
        const_set = sem("const_set")
        passed = sem("passed")
        gn_in = [sem(f"gn_in{i}") for i in range(2)]
        gn_used = sem("gn_used")
        chain = sem("chain")
        wraw_scaled = sem("wraw_scaled")
        wmean_ready = sem("wmean_ready")
        wc_ready = sem("wc_ready")
        gx_in = [sem(f"gx_in{i}") for i in range(2)]
        gx_used = sem("gx_used")
        gst_ready = sem("gst_ready")
        gsum_ready = sem("gsum_ready")
        gvar_ready = sem("gvar_ready")
        gstd_ready = sem("gstd_ready")
        cur_set = sem("cur_set")
        x_in = [sem(f"x_in{i}") for i in range(2)]
        y_ready = sem("y_ready")
        stat_ready = sem("stat_ready")
        mu2_ready = sem("mu2_ready")
        var_ready = sem("var_ready")
        std_ready = sem("std_ready")
        rstd_ready = sem("rstd_ready")
        bc_ready = sem("bc_ready")
        xn_ready = sem("xn_ready")
        u_ready = sem("u_ready")
        u_evicted = sem("u_evicted")
        halo_ready = sem("halo_ready")
        centre_ready = sem("centre_ready")
        tap_done = sem("tap_done")
        tap_diag_ready = sem("tap_diag_ready")
        pe_taps_ready = sem("pe_taps_ready")
        pe_taps_evicted = sem("pe_taps_evicted")
        v_stored = [sem(f"v_stored{g}") for g in range(G)]
        qkT_ready = sem("qkT_ready")
        qkT_evicted = sem("qkT_evicted")
        gram_done = sem("gram_done")
        sq_done = sem("sq_done")
        nsum_ready = sem("nsum_ready")
        nroot_ready = sem("nroot_ready")
        diag_ready = sem("diag_ready")
        rk_ready = sem("rk_ready")
        rk_copied = sem("rk_copied")
        smx_ready = sem("smx_ready")
        exp_done = sem("exp_done")
        a_ready = sem("a_ready")
        cm_ready = sem("cm_ready")
        ac_ready = sem("ac_ready")
        at_ready = sem("at_ready")
        at_copied = sem("at_copied")
        small = sem("small")
        x2_in = [sem(f"x2_in{i}") for i in range(4)]
        v2_in = [sem(f"v2_in{i}") for i in range(4)]
        o_ready = sem("o_ready")
        osq_ready = sem("osq_ready")
        o_evicted = sem("o_evicted")
        ostat_ready = sem("ostat_ready")
        ostd_ready = sem("ostd_ready")
        orstd_ready = sem("orstd_ready")
        obc_ready = sem("obc_ready")
        on_done = sem("on_done")
        x1_ready = sem("x1_ready")
        bn_done = sem("bn_done")
        x1_stored = [sem(f"x1_stored{i}") for i in range(4)]
        batch_done = sem("batch_done")
        l1_in = sem("l1_in")
        wf_ready = sem("wf_ready")
        wf_even = sem("wf_even")
        wf_odd = sem("wf_odd")
        wky_hi = sem("wky_hi")
        wky_split = sem("wky_split")
        wdiv_ready = sem("wdiv_ready")
        wky_scaled = sem("wky_scaled")
        sig_ready = sem("sig_ready")
        sig_set = sem("sig_set")
        pool_ready = sem("pool_ready")
        gate_ready = sem("gate_ready")
        gate_in = sem("gate_in")
        gelu_done = sem("gelu_done")
        wnorm_done = sem("wnorm_done")
        gx2_ready = sem("gx2_ready")
        gx_ready = sem("gx_ready")
        gxm_ready = sem("gxm_ready")
        d4_ready = sem("d4_ready")
        chb_ready = sem("chb_ready")
        chb_set = sem("chb_set")
        l1_ready = sem("l1_ready")
        pads_zero = sem("pads_zero")
        xg_in = [sem(f"xg_in{i}") for i in range(2)]
        zfull_ready = sem("zfull_ready")
        yz_ready = sem("yz_ready")
        zlo_ready = sem("zlo_ready")
        toep_ready = sem("toep_ready")
        box_step = sem("box_step")
        box_ready = sem("box_ready")
        conv_ready = sem("conv_ready")
        og_ready = sem("og_ready")
        og_stored = [sem(f"og_stored{i}") for i in range(2)]

        wqk = wc.rearrange("p k (m c) -> p k m c", c=P)
        xr = x.rearrange("b (g p) h w -> b p g (h w)", p=P)
        xg_n = x.rearrange("b (g p) h w -> (b g) p (h w)", p=P)
        vr = v_dram.rearrange("b (g p) n -> b p g n", p=P)
        x1r = x1_dram.rearrange("b (g p) n -> b p g n", p=P)
        x1y = x1_dram.rearrange("b c (y w) -> y b c w", w=W)
        outy = out.rearrange("b c y w -> y b c w")

        def of_image(ap, b):
            return ap[bass.ds(b, 1)].rearrange("a p g n -> (a p) g n")

        def rows_of(i):
            return (1 if i == 0 else 0), (RB + 1 if i == NB - 1 else RB)

        def blocks(eng, b, body):
            body(b * NB, 0, 0, b * (NB // 2))
            with eng.Fori(0, (NB - 2) // 2) as k:
                body(b * NB + k * 2 + 1, None, 1, b * (NB // 2) + k, k * 2 + 1)
                body(b * NB + k * 2 + 2, None, 0, b * (NB // 2) + k + 1, k * 2 + 2)
            body(b * NB + (NB - 1), NB - 1, 1, b * (NB // 2) + (NB // 2 - 1))

        def v_taps(i, g):
            return (2 * NT * G + NT * (g + 1) if i == NB - 1 else OPS * (g + 1)) - SKIP

        def qk_taps(i):
            return 2 * NT * G if i == NB - 1 else B_OPS

        def pe_tap_tiles(i):
            r0, r1 = rows_of(i)
            return [(bank, max(r0, ROWS_T * j), min(r1, ROWS_T * (j + 1)))
                    for j, bank in enumerate((4, 3, 5)) if ROWS_T * j < r1]

        def wf_in(t):
            return ps[:, 2 * (t % 2):2 * (t % 2) + 2, 0:64 * K7].rearrange("p v (c k) -> p c v k", k=K7)

        def wf_out(t):
            r, q = t // 6, t % 6
            return wfold[:, 64 * q:64 * (q + 1), :, r].rearrange("p c (v k) -> p c v k", v=2)

        pooled = (l1v[:, 0], l1v[:, 1])
        gxv = l1v[:, 6]
        SMALL = 17

        def images(eng, body):
            with eng.Fori(0, B - 1) as b:
                body(b, False)
            body(B - 1, True)

        block = ctx.enter_context(nc.Block())

        @block.sync
        def _(sp):
            for dst, src in ((ident, ident_in), (member, member_in), (ch, chans), (dw, dw_qkv),
                             (wraw, w_qkv), (hmask, headmask_in),
                             (to_row, to_row_in), (from_row, from_row_in)):
                sp.dma_start(dst[:], src).then_inc(par_in, 16)
            with sp.Fori(0, G) as n:
                for q in range(GN_LOADS):
                    sp.wait_ge(gn_used, n * GN_LOADS + (q + 1))
                    sp.sem_inc(passed, 1)
                    sp.dma_start(gnx[:, q % 2, :],
                                 xg_n[bass.ds(n, 1), :, q * GN_COLS:(q + 1) * GN_COLS].rearrange("a p n -> (a p) n")
                                 ).then_inc(gn_in[q % 2], 16)
            sp.wait_ge(gn_used, G * GN_LOADS + 2)
            sp.wait_ge(wc_ready, 2)
            def load_xin(xb, i):
                sp.dma_start(xin[:, i], xb[:, :, i * PX:(i + 1) * PX]).then_inc(x_in[i], 16)

            for i in range(2):
                load_xin(of_image(xr, 0), i)

            def image(b, last_image):
                xb, vb, x1b = of_image(xr, b), of_image(vr, b), of_image(x1r, b)
                def first(n, i, odd, seen, idx=None):
                    r0, r1 = rows_of(i)
                    for g in range(G):
                        sp.wait_ge(tap_done, n * B_OPS + OPS * (g + 1))
                        sp.sem_inc(passed, 1)
                        if i is None:
                            dst = vb[:, g:g + 1, bass.ds(idx * PX - W, RB * W)]
                        else:
                            dst = vb[:, g:g + 1, i * PX - W + r0 * W:i * PX - W + r1 * W]
                        sp.dma_start(dst.rearrange("p a n -> p (a n)"), accv[:, g, r0 * W:r1 * W]
                                     ).then_inc(v_stored[g], 16)
                        if g == 0 and i is None:
                            load(n, odd, idx)
                        elif g == 0 and i == 0:
                            sp.wait_ge(u_ready, n * U_TILES + U_TILES)
                            sp.sem_inc(passed, 1)
                            sp.dma_start(xin[:, 0], xb[:, :, 2 * PX:3 * PX]).then_inc(x_in[0], 16)

                def load(n, odd, idx):
                    sp.wait_ge(u_ready, n * U_TILES + U_TILES)
                    sp.sem_inc(passed, 1)
                    sp.dma_start(xin[:, odd], xb[:, :, bass.ds(idx * PX + 2 * PX, PX)]).then_inc(x_in[odd], 16)

                def first_no_load(n, i, odd, seen, idx):
                    r0, r1 = rows_of(i)
                    for g in range(G):
                        sp.wait_ge(tap_done, n * B_OPS + v_taps(i, g))
                        sp.sem_inc(passed, 1)
                        sp.dma_start(vb[:, g:g + 1, idx * PX - W + r0 * W:idx * PX - W + r1 * W].rearrange("p a n -> p (a n)"),
                                     accv[:, g, r0 * W:r1 * W]).then_inc(v_stored[g], 16)

                first(b * NB, 0, 0, None)
                with sp.Fori(0, (NB - 4) // 2) as k:
                    first(b * NB + k * 2 + 1, None, 1, None, k * 2 + 1)
                    first(b * NB + k * 2 + 2, None, 0, None, k * 2 + 2)
                first(b * NB + (NB - 3), None, 1, None, NB - 3)
                first_no_load(b * NB + (NB - 2), None, 0, None, NB - 2)
                first_no_load(b * NB + (NB - 1), NB - 1, 1, None, NB - 1)

                def load_x2(slot, cols):
                    sp.dma_start(x2[:, slot], xb[:, :, cols]).then_inc(x2_in[slot], 16)

                def load_gx(slot, cols):
                    sp.dma_start(gx[:, slot], xnext[:, :, cols]).then_inc(gx_in[slot], 16)

                def load_v2(slot, cols):
                    sp.dma_start(vin[:, slot], vb[:, :, cols]).then_inc(v2_in[slot], 16)

                sp.wait_ge(u_ready, b * (NB * U_TILES) + NB * U_TILES)
                sp.sem_inc(passed, 1)
                for s in range(4):
                    load_x2(s, slice(s * TILE, (s + 1) * TILE))
                if not last_image:
                    xnext = of_image(xr, b + 1)
                    for s in range(2):
                        load_gx(s, slice(s * TILE, (s + 1) * TILE))
                sp.wait_ge(gram_done, b * H + (H + 2))
                sp.sem_inc(passed, 1)
                sp.wait_ge(sq_done, b * (2 * G * NB) + (2 * G * NB + 2))
                sp.sem_inc(passed, 1)
                for g in range(G):
                    sp.wait_ge(v_stored[g], b * (16 * NB) + 16 * (NB + 1))
                    sp.sem_inc(passed, 1)
                for s in range(4):
                    load_v2(s, slice(s * TILE, (s + 1) * TILE))

                def next_block(i):
                    sp.wait_ge(bn_done, b * T2 + (T2 - 2 + 2 * i))
                    sp.sem_inc(passed, 1)
                    for s in (2 * i, 2 * i + 1):
                        sp.wait_ge(x1_stored[s], b * (4 * T2) + 4 * T2)
                        sp.sem_inc(passed, 1)
                    load_xin(xnext, i)

                def second(k, last):
                    for s in range(4):
                        T = b * T2 + k * 4 + s
                        nxt = bass.ds(k * (4 * TILE) + (s + 4) * TILE, TILE)
                        if not last:
                            sp.wait_ge(o_ready, T + 1)
                            sp.sem_inc(passed, 1)
                            load_v2(s, nxt)
                        if last and s == 3 and not last_image:
                            next_block(0)
                        sp.wait_ge(x1_ready, T * 3 + 3)
                        sp.sem_inc(passed, 1)
                        sp.dma_start(x1b[:, :, bass.ds(k * (4 * TILE) + s * TILE, TILE)], x2[:, s]).then_inc(x1_stored[s], 16)
                        if not last_image and not (last and s >= 2):
                            sp.wait_ge(gx_used, T + 1)
                            sp.sem_inc(passed, 1)
                            load_gx(s % 2, bass.ds(k * (4 * TILE) + (s + 2) * TILE, TILE))
                        if last:
                            continue
                        sp.wait_ge(bn_done, T + 1)
                        sp.sem_inc(passed, 1)
                        sp.wait_ge(x1_stored[s], b * (4 * T2) + k * 16 + 16)
                        sp.sem_inc(passed, 1)
                        load_x2(s, nxt)

                with sp.Fori(0, T2 // 4 - 1) as k:
                    second(k, False)
                second(T2 // 4 - 1, True)
                if not last_image:
                    next_block(1)
                sp.wait_ge(batch_done, b + 1)
                sp.sem_inc(passed, 1)
                for s in range(4):
                    sp.wait_ge(x1_stored[s], b * (4 * T2) + 4 * T2)
                    sp.sem_inc(passed, 1)

            images(sp, image)

            for dst, src in ((wT[:, 0], w_avg), (wT[:, 1], w_max), (wmx, w_mix_ch), (band, band_in)):
                sp.dma_start(dst, src).then_inc(l1_in, 16)
            sp.dma_start(selk[0:K7], sel_in).then_inc(l1_in, 16)
            sp.dma_start(wky[0:K7], w_mix_ky).then_inc(l1_in, 16)
            sp.wait_ge(l1_ready, 2)

            def load_x1(s, cols):
                for b in range(B):
                    sp.dma_start(xg[:, s, b], x1y[:, b, cols, :]).then_inc(xg_in[s], 16)

            for s in range(2):
                load_x1(s, slice(s * CG, (s + 1) * CG))

            def groups(k, last):
                for s in range(2):
                    sp.wait_ge(og_ready, k * (2 * CG) + CG * (s + 1) + 2)
                    sp.sem_inc(passed, 1)
                    for b in range(B):
                        sp.dma_start(outy[:, b, bass.ds(k * (2 * CG) + s * CG, CG), :], og[:, s, b]).then_inc(og_stored[s], 16)
                    if not last:
                        load_x1(s, bass.ds(k * (2 * CG) + (s + 2) * CG, CG))

            with sp.Fori(0, NCG // 2 - 1) as k:
                groups(k, False)
            groups(NCG // 2 - 1, True)
            for s in range(2):
                sp.wait_ge(og_stored[s], 16 * B * (NCG // 2 + 1))

        @block.gpsimd
        def _(pool):
            nc.gpsimd.memset(ones[:], 1.0).then_inc(const_set, 1)
            nc.gpsimd.memset(mean_c[:], 1.0 / C).then_inc(const_set, 1)
            nc.gpsimd.memset(zero1[:], 0.0).then_inc(const_set, 1)
            nc.gpsimd.memset(eps_gn[:], EPS_GN).then_inc(const_set, 1)
            nc.gpsimd.memset(ubuf, 0.0).then_inc(const_set, 1)
            pool.wait_ge(const_set, 5)
            for g in range(G):
                pool.sem_inc(halo_ready, 1)

            def halo(n, i, odd, seen, idx=None):
                for g in range(G):
                    pool.wait_ge(tap_done, n * B_OPS + v_taps(i, g))
                    pool.sem_inc(passed, 1)
                    rows = ubuf[:, 3 * g:3 * g + 3]
                    if i == NB - 1:
                        nc.gpsimd.memset(rows[:, :, 0:2, 1:W + 1], 0.0).then_inc(halo_ready, 1)
                    else:
                        nc.gpsimd.tensor_copy(rows[:, :, 0:2, 1:W + 1], rows[:, :, RB:RB + 2, 1:W + 1]).then_inc(halo_ready, 1)

            with pool.Fori(0, B) as b:
                blocks(pool, b, halo)
            pool.wait_ge(l1_ready, 2)
            nc.gpsimd.memset(ypad, 0.0).then_inc(pads_zero, 1)
            nc.gpsimd.memset(zhi, 0.0).then_inc(pads_zero, 1)
            nc.gpsimd.memset(zlo, 0.0).then_inc(pads_zero, 1)

        @block.scalar
        def _(act):
            A = nc.scalar.activation
            act.sem_inc(u_evicted, 3)
            act.sem_inc(sq_done, 2)
            act.sem_inc(qkT_evicted, 1)
            act.sem_inc(o_evicted, 2)
            act.sem_inc(ostd_ready, 1)
            act.sem_inc(chb_set, 2)
            act.wait_ge(const_set, 5)

            def group_root(step):
                act.wait_ge(gvar_ready, step)
                A(gn_r[:], gn_tmp[:], ACT.Sqrt, bias=eps_gn[:, 0:1]).then_inc(gstd_ready, 1)

            group_root(1)

            def make_y(n, odd, seen, parts=range(2 * G)):
                for part in parts:
                    if part == 0:
                        act.wait_ge(x_in[odd], seen * 16 + 16)
                    g = part % G
                    ins = A(ysq[:, g] if part < G else xin[:, odd, g], xin[:, odd, g],
                            ACT.Square if part < G else ACT.Identity, bias=cur[:, 1, g:g + 1], scale=cur[:, 0, g:g + 1])
                    if part == 2 * G - 1:
                        ins.then_inc(y_ready, 1)

            def mean_squared(n):
                act.wait_ge(stat_ready, n + 1)
                A(mu2[:], ps[0:RB, 3, 0:W], ACT.Square, bias=zero1[0:RB, 0:1]).then_inc(mu2_ready, 1)

            def root(n):
                act.wait_ge(var_ready, n + 1)
                A(std[:], var[:], ACT.Sqrt, bias=eps_gn[0:RB, 0:1]).then_inc(std_ready, 1)

            def evict_u(n, t, i, odd):
                r0, r1 = rows_of(i)
                m, j = t // HALVES, t % HALVES
                g, q = m // 3, m % 3
                if q == 0 and j == 0:
                    act.wait_ge(halo_ready, n * G + (g + 1))
                act.wait_ge(u_ready, n * U_TILES + (t + 1))
                A(ubuf[:, m, 2 + ROWS_T * j:2 + ROWS_T * (j + 1), 1:W + 1],
                  ps[:, t % 3, :].rearrange("p (r w) -> p r w", w=W),
                  ACT.Identity, bias=bias_u[:, m:m + 1]).then_inc(u_evicted, 1)
                if j < HALVES - 1:
                    return
                act.wait_ge(u_evicted, n * U_TILES + (t + 1) + 3)
                if m == PE_M:
                    return
                if q == 2:
                    act.wait_ge(v_stored[g], n * 16 + 16)
                    dst = accv[:, g]
                else:
                    dst = accs[:, odd, 2 * g + q]
                A(dst[:, r0 * W:r1 * W].rearrange("p (r w) -> p r w", w=W), ubuf[:, m, r0 + 1:r1 + 1, 1:W + 1],
                  ACT.Copy, scale=dw[:, m, 4:5]).then_inc(centre_ready, 1)

            def evict_pe_taps(n, i):
                act.wait_ge(pe_taps_ready, n + 1)
                act.wait_ge(v_stored[PE_M // 3], n * 16 + 16)
                tiles = pe_tap_tiles(i)
                for z, (bank, ra, rb) in enumerate(tiles):
                    ins = A(accv[:, PE_M // 3, ra * W:rb * W], ps[:, bank, 0:(rb - ra) * W], ACT.Copy)
                    if z == len(tiles) - 1:
                        ins.then_inc(centre_ready, 1)
                act.wait_ge(centre_ready, n * M9 + 3)
                act.sem_inc(pe_taps_evicted, 1)

            def square(n, i, odd, idx, c):
                r0, r1 = rows_of(i)
                if c == 0:
                    act.wait_ge(tap_done, n * B_OPS + qk_taps(i))
                g, q = c // 2, c % 2
                col = norms[:, q, g, bass.ds(idx, 1)] if i is None else norms[:, q, g, i:i + 1]
                act.wait_ge(sq_done, n * (2 * G) + (c + 1))
                act.sem_inc(passed, 1)
                A(junk[:, c % 2, r0 * W:r1 * W], accs[:, odd, c, r0 * W:r1 * W], ACT.Square, bias=zero1[:, 0:1],
                  accum_out=col).then_inc(sq_done, 1)

            def evict_turned(n, i, r):
                r0, r1 = rows_of(i)
                if not r0 <= r < r1:
                    return
                act.wait_ge(qkT_ready, n * RB + r)
                act.wait_ge(gram_done, n * RB + r)
                A(qkT[:, r % 2, 0], ps[:, 5, 0:C], ACT.Copy)
                A(qkT[:, r % 2, 1], ps[:, 6, 0:C], ACT.Copy).then_inc(qkT_evicted, 1)

            def image(b, last_image):
                act.wait_ge(cur_set, b + 1)
                make_y(b * NB, 0, b * (NB // 2))
                mean_squared(b * NB)
                root(b * NB)

                def first(n, i, odd, seen, prev, idx):
                    more = i != NB - 1
                    for t in range(U_TILES):
                        evict_u(n, t, i, odd)
                        if t == PE_TAPS_AT:
                            evict_pe_taps(n, i)
                        if t < 2 * G and more:
                            make_y(n + 1, 1 - odd, seen + odd, [t])
                        if t == STATS_AT and more:
                            mean_squared(n + 1)
                        if t == ROOT_AT and more:
                            root(n + 1)
                        if i != 0 and SQUARES_AT <= t < SQUARES_AT + 2 * G:
                            square(n - 1, prev, 1 - odd, idx - 1, t - SQUARES_AT)
                        if i != 0 and t >= GRAM_AT:
                            evict_turned(n - 1, prev, t - GRAM_AT)

                first(b * NB, 0, 0, b * (NB // 2), None, 0)
                first(b * NB + 1, None, 1, b * (NB // 2), 0, 1)
                with act.Fori(0, (NB - 4) // 2) as k:
                    first(b * NB + k * 2 + 2, None, 0, b * (NB // 2) + k + 1, None, k * 2 + 2)
                    first(b * NB + k * 2 + 3, None, 1, b * (NB // 2) + k + 1, None, k * 2 + 3)
                first(b * NB + (NB - 2), None, 0, b * (NB // 2) + (NB // 2 - 1), None, NB - 2)
                first(b * NB + (NB - 1), NB - 1, 1, b * (NB // 2) + (NB // 2 - 1), None, NB - 1)
                for r in range(RB + 2):
                    if r < 2 * G:
                        square(b * NB + (NB - 1), NB - 1, 1, NB - 1, r)
                    evict_turned(b * NB + (NB - 1), NB - 1, r)

                act.wait_ge(nsum_ready, b + 1)
                A(norm[:], norm[:], ACT.Sqrt, bias=zero1[:, 0:1]).then_inc(nroot_ready, 1)
                act.wait_ge(rk_ready, b + 1)
                A(rk_row, ps[:, 0, 0:C], ACT.Copy).then_inc(rk_copied, 1)
                act.wait_ge(smx_ready, b + 1)
                for a in range(G):
                    cols = slice(WOFF[a], WOFF[a] + WIN[a][1] - WIN[a][0])
                    A(scores[:, cols], scores[:, cols], ACT.Exp, bias=smx[:, a:a + 1], accum_out=ssum[:, a:a + 1]
                      ).then_inc(exp_done, 1)
                act.wait_ge(at_ready, b + 1)
                A(at, ps[:, 2:5, 0:C], ACT.Copy).then_inc(at_copied, 1)

                with act.Fori(0, T2 // 4) as k:
                    for j in range(4):
                        T = b * T2 + k * 4 + j
                        s = 3 * (j % 2)
                        act.wait_ge(o_ready, T + 1)
                        A(osq[:, j % 2], ps[:, s:s + 3, :], ACT.Square, bias=zero1[:, 0:1]).then_inc(osq_ready, 1)
                        act.wait_ge(on_done, T + 1)
                        for a in range(G):
                            ins = A(ow[:, j, a], ps[:, s + a, :], ACT.Copy, scale=par["ln2_w"][:, a:a + 1])
                        ins.then_inc(o_evicted, 1)
                        act.wait_ge(ostat_ready, T + 1)
                        A(std2[:, j % 2], ps[0:ROWS_T, 6, 0:W], ACT.Sqrt, bias=eps_gn[0:ROWS_T, 0:1]).then_inc(ostd_ready, 1)
                if not last_image:
                    group_root(b + 2)
                act.wait_ge(batch_done, b + 1)

            images(act, image)

            group_root(B + 1)
            act.wait_ge(l1_in, 16 * 6)
            for g in range(G):
                ins = A(wsq[:, g], wmx[:, g], ACT.Square, bias=zero1[:, 0:1], accum_out=l1s[:, 0, g:g + 1])
            ins.then_inc(wnorm_done, 1)
            act.sem_inc(wf_even, 1)
            act.wait_ge(wky_scaled, 1)
            A(wky16[0:K7, 0], wky[0:K7], ACT.Copy).then_inc(wky_hi, 1)
            act.wait_ge(halo_ready, G * (B * NB + 1))
            act.wait_ge(gate_in, 1)
            A(l1v[:, 4], l1v[:, 3], ACT.Gelu, bias=zero1[:, 0:1]).then_inc(gelu_done, 1)
            act.wait_ge(gx2_ready, 1)
            A(l1v[:, 6], l1v[:, 5], ACT.Sqrt, bias=zero1[:, 0:1]).then_inc(gx_ready, 1)
            act.wait_ge(sig_ready, 1)
            A(sig, ps[:, 4, 0:C], ACT.Copy).then_inc(sig_set, 1)
            for t in range(4 * G):
                act.wait_ge(chb_ready, t + 1)
                v, g = t // G, t % G
                A(chb[:, v, P * g:P * (g + 1), :], ps[:, 6 + t % 2, :].rearrange("p (c b) -> p c b", b=B), ACT.Copy
                  ).then_inc(chb_set, 1)
            for t in range(0, 6 * K7, 2):
                act.wait_ge(wf_ready, t + 1)
                A(wf_out(t), wf_in(t), ACT.Copy).then_inc(wf_even, 1)
            act.wait_ge(chb_set, 4 * G + 2)
            act.wait_ge(wf_even, 3 * K7 + 1)
            act.sem_inc(l1_ready, 1)
            act.wait_ge(pads_zero, 3)
            with act.Fori(0, NCG // 2) as k:
                for s in range(2):
                    for c in range(CG):
                        K = k * (2 * CG) + (CG * s + c)
                        if c == 0:
                            act.wait_ge(xg_in[s], k * (16 * B) + 16 * B)
                        act.wait_ge(box_ready, K + 1)
                        act.wait_ge(conv_ready, K + 1)
                        act.sem_inc(passed, 1)
                        for b in range(B):
                            ins = A(zfull[:, c % 2, b], xg[:, s, b, c, :], ACT.Identity,
                                    bias=chb[:, 3, bass.ds(K, 1), b], scale=chb[:, 2, bass.ds(K, 1), b])
                        ins.then_inc(zfull_ready, 1)
                        for b in range(B):
                            A(ypad[:, c % 2, b, PAD:PAD + W], xg[:, s, b, c, :], ACT.Identity,
                              bias=chb[:, 1, bass.ds(K, 1), b], scale=chb[:, 0, bass.ds(K, 1), b])
                        act.wait_ge(zfull_ready, K + 1)
                        A(zhi[:, c % 2, :, PAD:PAD + W], zfull[:, c % 2], ACT.Copy).then_inc(yz_ready, 1)

        @block.tensor
        def _(pe):
            mm = pe.matmul
            pe.wait_ge(const_set, 5)
            pe.wait_ge(wraw_scaled, 1)
            for m in range(G):
                for k in range(G):
                    mm(ps[:, m, 0:C], mean_c[:], wc[:, k, C * m:C * (m + 1)], start=(k == 0), stop=(k == G - 1))
            for m in range(M9):
                for k in range(G):
                    ins = mm(ps[:, 3, m:m + 1], wraw[:, k, P * m:P * (m + 1)], par["ln1_b"][:, k:k + 1],
                             start=(k == 0), stop=(k == G - 1), skip_group_check=True)
            ins.then_inc(wmean_ready, 1)

            def group_sums(step):
                pe.wait_ge(gst_ready, step)
                for m in range(G):
                    for k in range(G):
                        ins = mm(ps[:, 4, 8 * m:8 * m + 8], member[:, k, P * m:P * (m + 1)],
                                 gn_st[:, k].rearrange("p b s -> p (b s)"), start=(k == 0), stop=(k == G - 1),
                                 skip_group_check=True)
                ins.then_inc(gsum_ready, 1)

            group_sums(1)

            def stats(n, odd):
                pe.wait_ge(y_ready, n + 1)
                pe.wait_ge(xn_ready, n * 2 + 2)
                for v, src in enumerate((xin[:, odd], ysq)):
                    for r in range(RB):
                        for k in range(G):
                            ins = mm(ps[0:RB, 3, W * v:W * (v + 1)], to_row[:, r, :], src[:, k, W * r:W * (r + 1)],
                                     start=(r == 0 and k == 0), stop=(r == RB - 1 and k == G - 1), skip_group_check=True)
                ins.then_inc(stat_ready, 1)

            def spread(n):
                pe.wait_ge(rstd_ready, n + 1)
                for j in range(HALVES):
                    for r in range(ROWS_T):
                        c = ROWS_T * j + r
                        ins = mm(ps[:, 3 + j, W * r:W * (r + 1)], from_row[:, c, :], rstd[:], start=True, stop=True)
                    ins.then_inc(bc_ready, 1)

            def u_tile(n, t, odd):
                m, j = t // HALVES, t % HALVES
                pe.wait_ge(u_evicted, n * U_TILES + (t + 1))
                for k in range(G):
                    ins = mm(ps[:, t % 3, :], wc[:, k, P * m:P * (m + 1)], xin[:, odd, k, TILE * j:TILE * (j + 1)],
                             start=(k == 0), stop=(k == G - 1))
                ins.then_inc(u_ready, 1)

            def pe_taps(n, i):
                pe.wait_ge(u_evicted, n * U_TILES + HALVES * (PE_M + 1) + 3)
                for bank, ra, rb in pe_tap_tiles(i):
                    for z, (dy, dx) in enumerate(PE_TAPS):
                        ins = mm(ps[:, bank, 0:(rb - ra) * W].rearrange("p (r w) -> p r w", w=W), tap_diag[:, z],
                                 ubuf[:, PE_M, ra + dy:rb + dy, dx:dx + W], start=(z == 0), stop=(z == len(PE_TAPS) - 1))
                ins.then_inc(pe_taps_ready, 1)

            def turn(n, r, odd):
                pe.wait_ge(qkT_evicted, n * RB + r)
                for q in range(2):
                    for g in range(G):
                        ins = pe.transpose(ps[:, 5 + q, P * g:P * (g + 1)], accs[:, odd, 2 * g + q, W * r:W * (r + 1)], ident[:])
                ins.then_inc(qkT_ready, 1)

            def gram_row(n, r, start, stop):
                pe.wait_ge(qkT_evicted, n * RB + r + 1)
                for a in range(G):
                    lo, hi = WIN[a]
                    ins = mm(ps[:, 7, WOFF[a]:WOFF[a] + hi - lo], qkT[:, r % 2, 0, P * a:P * (a + 1)],
                             qkT[:, r % 2, 1, lo:hi], start=(start and a == 0), stop=stop, skip_group_check=True)
                ins.then_inc(gram_done, 1)

            def gram_step(n, i, odd, r):
                r0, r1 = rows_of(i)
                if r == r0:
                    pe.wait_ge(tap_done, n * B_OPS + qk_taps(i))
                if r0 < r <= r1:
                    gram_row(n, r - 1, i == 0 and r - 1 == r0, i == NB - 1 and r == r1)
                if r0 <= r < r1:
                    turn(n, r, odd)

            pe.wait_ge(tap_diag_ready, 1)
            def image(b, last_image):
                pe.wait_ge(cur_set, b + 1)
                stats(b * NB, 0)
                spread(b * NB)

                def first(n, i, odd, prev):
                    more = i != NB - 1
                    pe.wait_ge(xn_ready, n * 2 + 4)
                    for t in range(U_TILES):
                        u_tile(n, t, odd)
                        if t == PE_TAPS_AT:
                            pe_taps(n, i)
                        if t == PE_TAPS_AT + 1:
                            pe.wait_ge(pe_taps_evicted, n + 1)
                        if t == STATS_AT and more:
                            stats(n + 1, 1 - odd)
                        if t == SPREAD_AT and more:
                            spread(n + 1)
                        if i != 0 and t >= GRAM_AT:
                            gram_step(n - 1, prev, 1 - odd, t - GRAM_AT)

                first(b * NB, 0, 0, None)
                first(b * NB + 1, None, 1, 0)
                with pe.Fori(0, (NB - 4) // 2) as k:
                    first(b * NB + k * 2 + 2, None, 0, None)
                    first(b * NB + k * 2 + 3, None, 1, None)
                first(b * NB + (NB - 2), None, 0, None)
                first(b * NB + (NB - 1), NB - 1, 1, None)
                for r in range(RB + 2):
                    gram_step(b * NB + (NB - 1), NB - 1, 1, r)

                pe.wait_ge(diag_ready, b + 1)
                mm(ps[:, 0, 0:C], ones[:], diag[:].rearrange("p g c -> p (g c)"), start=True, stop=True).then_inc(rk_ready, 1)
                pe.wait_ge(a_ready, b + 1)
                for a in range(G):
                    ins = mm(ps[:, 1, 0:C], mean_c[:], a_full[:, a], start=(a == 0), stop=(a == G - 1))
                ins.then_inc(cm_ready, 1)
                pe.wait_ge(ac_ready, b + 1)
                for k in range(G):
                    for a in range(G):
                        ins = pe.transpose(ps[:, 2 + k, P * a:P * (a + 1)], a_cent[:, a, P * k:P * (k + 1)], ident[:])
                ins.then_inc(at_ready, 1)
                pe.wait_ge(at_copied, b + 1)

                def make_o(T, j, loaded, chunks):
                    s = 3 * (j % 2)
                    if chunks[0] == 0:
                        pe.wait_ge(v2_in[j], loaded)
                        pe.wait_ge(o_evicted, T + 1)
                    for a in chunks:
                        for k in range(G):
                            ins = mm(ps[:, s + a, :], at[:, k, P * a:P * (a + 1)],
                                     vin[:, j, k], start=(k == 0), stop=(k == G - 1))
                    if chunks[-1] == G - 1:
                        ins.then_inc(o_ready, 1)

                def mean_of_squares(T, j):
                    pe.wait_ge(osq_ready, T + 1)
                    pe.wait_ge(ostd_ready, T + 1)
                    for r in range(ROWS_T):
                        for k in range(G):
                            ins = mm(ps[0:ROWS_T, 6, 0:W], to_row[:, r, 0:ROWS_T], osq[:, j % 2, k, W * r:W * (r + 1)],
                                     start=(r == 0 and k == 0), stop=(r == ROWS_T - 1 and k == G - 1))
                    ins.then_inc(ostat_ready, 1)

                def spread_o(T, j):
                    pe.wait_ge(orstd_ready, T + 1)
                    pe.wait_ge(on_done, T + 4)
                    for r in range(ROWS_T):
                        ins = mm(ps[:, 7, W * r:W * (r + 1)], from_row[0:ROWS_T, r, :], rstd2[:, j % 2], start=True, stop=True)
                    ins.then_inc(obc_ready, 1)

                def second(k, last):
                    for j in range(4):
                        T = b * T2 + k * 4 + j
                        if not (last and j == 3):
                            make_o(T + 1, (j + 1) % 4, None, range(1, G))
                        mean_of_squares(T, j)
                        if not (last and j >= 2):
                            nxt = (j + 2) % 4
                            make_o(T + 2, nxt, b * (4 * T2) + k * 16 + (16 if nxt >= 2 else 32), [0])
                        spread_o(T, j)

                make_o(b * T2, 0, b * (4 * T2) + 16, range(G))
                make_o(b * T2 + 1, 1, b * (4 * T2) + 16, [0])
                with pe.Fori(0, T2 // 4 - 1) as k:
                    second(k, False)
                second(T2 // 4 - 1, True)
                if not last_image:
                    pe.wait_ge(o_evicted, b * T2 + T2 + 2)
                    pe.sem_inc(passed, 1)
                    group_sums(b + 2)

            images(pe, image)

            group_sums(B + 1)
            pe.wait_ge(l1_in, 16 * 6)
            pe.wait_ge(batch_done, B)
            pe.wait_ge(diag_ready, B + 1)
            mm(ps[:, 0, 0:C], ones[:], diag[:].rearrange("p g c -> p (g c)"), start=True, stop=True).then_inc(wdiv_ready, 1)
            pe.wait_ge(pool_ready, 1)
            for m in range(G):
                for k in range(G):
                    for v in range(2):
                        ins = mm(ps[:, 3, B * m:B * (m + 1)], wT[:, v, k, P * m:P * (m + 1)], pooled[v][:, k, :],
                                 start=(k == 0 and v == 0), stop=(k == G - 1 and v == 1), skip_group_check=True)
            ins.then_inc(gate_ready, 1)
            pe.wait_ge(gx_ready, 1)
            for k in range(G):
                ins = mm(ps[:, 5, 0:B], mean_c[:], gxv[:, k, :], start=(k == 0), stop=(k == G - 1))
            ins.then_inc(gxm_ready, 1)
            pe.wait_ge(diag_ready, B + 2)
            mm(ps[:, 4, 0:C], ones[:], diag[:].rearrange("p g c -> p (g c)"), start=True, stop=True).then_inc(sig_ready, 1)
            for t in range(4 * G):
                pe.wait_ge(d4_ready, t + 1)
                pe.wait_ge(chb_set, t + 1)
                mm(ps[:, 6 + t % 2, :], ones[:], d4[:, t % 2].rearrange("p c b -> p (c b)"), start=True, stop=True
                   ).then_inc(chb_ready, 1)
            pe.wait_ge(wky_split, 1)
            for t in range(6 * K7):
                r, q = t // 6, t % 6
                pe.wait_ge(wf_odd if t % 2 else wf_even, t // 2 + 1)
                for v in range(2):
                    ins = mm(ps[:, 2 * (t % 2) + v, 0:64 * K7], selk16[0:K7, r, :],
                             wky16[0:K7, v, 64 * K7 * q:64 * K7 * (q + 1)], start=True, stop=True)
                ins.then_inc(wf_ready, 1)
            pe.sem_inc(conv_ready, 2)
            with pe.Fori(0, NCG // 2) as k:
                for s in range(2):
                    for c in range(CG):
                        K = k * (2 * CG) + (CG * s + c)
                        pe.wait_ge(yz_ready, K + 1)
                        pe.wait_ge(toep_ready, K + 1)
                        pe.wait_ge(og_ready, K + 1)
                        res = ps[:, c % 2, :].rearrange("p (b w) -> p b w", b=B)
                        for plane in range(2 * K7):
                            kx = plane % K7
                            mm(res, toep[:, c % 2, plane, 0:P], zhi[:, c % 2, :, kx:kx + W], start=(plane == 0), stop=False)
                        pe.wait_ge(zlo_ready, K + 1)
                        for kx in range(K7):
                            mm(res, toep[:, c % 2, kx, 0:P], zlo[:, c % 2, :, kx:kx + W], start=False, stop=False)
                        pe.wait_ge(box_ready, K + 3)
                        mm(res, band[:, 0:P], box[:, c % 2], start=False, stop=True).then_inc(conv_ready, 1)

        @block.vector
        def _(dve):
            V = nc.vector
            count = [0]

            def then(ins):
                count[0] += 1
                ins.then_inc(chain, 1)
                dve.wait_ge(chain, count[0])

            dve.sem_inc(gn_used, 2)
            dve.sem_inc(xn_ready, 2)
            dve.sem_inc(gram_done, 2)
            dve.sem_inc(on_done, 4)
            for g in range(G):
                dve.sem_inc(v_stored[g], 16)
            dve.wait_ge(par_in, 16 * 8)
            for k in range(G):
                ins = V.tensor_scalar(wc[:, k], wraw[:, k], par["ln1_w"][:, k:k + 1], None, ALU.mult)
            ins.then_inc(wraw_scaled, 1)
            dve.wait_ge(wmean_ready, 1)
            dve.wait_ge(wraw_scaled, 1)
            for k in range(G):
                ins = V.tensor_tensor(wc[:, k].rearrange("p (a n) -> p a n", a=G), wc[:, k].rearrange("p (a n) -> p a n", a=G),
                                      ps[:, 0:3, 0:C], ALU.subtract)
            ins.then_inc(wc_ready, 1)
            V.tensor_copy(bias_u[:], ps[:, 3, 0:M9]).then_inc(wc_ready, 1)
            then(V.memset(gn_st[:], 0.0))
            with dve.Fori(0, G) as g:
                for q in range(GN_LOADS):
                    dve.wait_ge(gn_in[q % 2], g * (8 * GN_LOADS) + 16 * (q // 2 + 1))
                    dve.sem_inc(passed, 1)
                    for t in range(GN_COLS // 512):
                        ins = V.bn_stats(gnb[:, bass.ds(g, 1), q * (GN_COLS // 512) + t, :].rearrange("p a s -> p (a s)"),
                                         gnx[:, q % 2, 512 * t:512 * (t + 1)])
                    ins.then_inc(gn_used, 1)
            dve.wait_ge(gn_used, G * GN_LOADS + 2)
            for g in range(G):
                ins = V.bn_aggr(gn_st[:, g, 0, :], gnb[:, g].rearrange("p t s -> p (t s)"))
            then(ins)

            def group_norm(step, r, nb, then):
                dve.wait_ge(gsum_ready, step)
                gs = ps[:, 4, 0:8 * G].rearrange("p (g b s) -> p g b s", g=G, b=B)
                then(V.tensor_copy(gn_mean[:], gs[:, :, :, 0]))
                then(V.tensor_tensor(gn_tmp[:], gn_mean[:], gn_mean[:], ALU.mult))
                V.tensor_tensor(gn_tmp[:], gs[:, :, :, 1], gn_tmp[:], ALU.subtract).then_inc(gvar_ready, 1)
                dve.wait_ge(gstd_ready, step)
                then(V.reciprocal(r, gn_r[:]))
                then(V.scalar_tensor_tensor(out=nb, in0=gn_mean[:], scalar=-1.0, in1=r, op0=ALU.mult, op1=ALU.mult))

            then(V.tensor_tensor(gn_tmp[:, :, 0], gn_st[:, :, 0, 0], gn_st[:, :, 0, 0], ALU.mult))
            V.tensor_tensor(gn_st[:, :, 0, 1], gn_st[:, :, 0, 1], gn_tmp[:, :, 0], ALU.add).then_inc(gst_ready, 1)
            group_norm(1, gn_r[:], gn_nb[:], then)

            for z, (dy, dx) in enumerate(PE_TAPS):
                ins = V.tensor_scalar(tap_diag[:, z], ident[:], dw[:, PE_M, 3 * dy + dx:3 * dy + dx + 1], None, ALU.mult)
            ins.then_inc(tap_diag_ready, 1)

            def variance(n):
                dve.wait_ge(mu2_ready, n + 1)
                V.tensor_tensor(var[:], ps[0:RB, 3, W:2 * W], mu2[:], ALU.subtract).then_inc(var_ready, 1)

            def invert(n):
                dve.wait_ge(std_ready, n + 1)
                V.reciprocal(rstd[:], std[:]).then_inc(rstd_ready, 1)

            def normalise(n, odd):
                for j in range(HALVES):
                    dve.wait_ge(bc_ready, n * 2 + (j + 1))
                    px = xin[:, odd, :, TILE * j:TILE * (j + 1)]
                    V.tensor_tensor(px, px, ps[:, 3 + j:4 + j, :].broadcast_to([P, G, TILE]), ALU.mult).then_inc(xn_ready, 1)

            def taps(n, chunks, i, odd, before, between={}):
                r0, r1 = rows_of(i)
                dve.wait_ge(centre_ready, n * M9 + (PE_M if PE_M in chunks[1:] else 3 * (chunks[-1] // 3 + 1)))
                done, last = n * B_OPS, {}
                for t, (dy, dx) in enumerate(TAPS):
                    if t in between:
                        between[t]()
                    if t == SKIP and PE_M in chunks[1:]:
                        dve.wait_ge(centre_ready, n * M9 + PE_M + 1)
                    for m in chunks:
                        if m == PE_M and (dy, dx) in PE_TAPS:
                            continue
                        g, q = m // 3, m % 3
                        acc = accv[:, g] if q == 2 else accs[:, odd, 2 * g + q]
                        acc = acc[:, r0 * W:r1 * W].rearrange("p (r w) -> p r w", w=W)
                        if m in last:
                            dve.wait_ge(tap_done, done + last[m])
                        V.scalar_tensor_tensor(out=acc, in0=ubuf[:, m, r0 + dy:r1 + dy, dx:dx + W],
                                               scalar=dw[:, m, 3 * dy + dx:3 * dy + dx + 1], in1=acc,
                                               op0=ALU.mult, op1=ALU.add).then_inc(tap_done, 1)
                        before += 1
                        last[m] = before
                return before

            def image(b, last_image):
                V.tensor_copy(cur[:, 0], gn_r[:, :, bass.ds(b, 1)].rearrange("p g a -> p (g a)"))
                V.tensor_copy(cur[:, 1], gn_nb[:, :, bass.ds(b, 1)].rearrange("p g a -> p (g a)")).then_inc(cur_set, 1)
                variance(b * NB)
                invert(b * NB)
                normalise(b * NB, 0)

                def first(n, i, odd, seen, idx=None):
                    if i == NB - 1:
                        ops = 0
                        for g in range(G):
                            ops = taps(n, (3 * g, 3 * g + 1), i, odd, ops)
                        for g in range(G):
                            ops = taps(n, (3 * g + 2,), i, odd, ops)
                        assert ops == B_OPS
                        return
                    ops = taps(n, (0, 1, 2), i, odd, 0)
                    ops = taps(n, (3, 4, 5), i, odd, ops, {3: lambda: variance(n + 1), 5: lambda: invert(n + 1)})
                    normalise(n + 1, 1 - odd)
                    ops = taps(n, (6, 7, 8), i, odd, ops)
                    assert ops == B_OPS

                blocks(dve, b, first)

                step = [0]

                def thus(ins):
                    step[0] += 1
                    ins.then_inc(small, 1)
                    dve.wait_ge(small, b * SMALL + step[0])

                dve.wait_ge(sq_done, b * (2 * G * NB) + (2 * G * NB + 2))
                V.tensor_reduce(norm[:], norms[:], AX.X, ALU.add).then_inc(nsum_ready, 1)
                dve.wait_ge(gram_done, b * H + (H + 2))
                thus(V.memset(a_full, 0.0))
                dve.wait_ge(nroot_ready, b + 1)
                thus(V.tensor_scalar(norm[:], norm[:], EPS_NORM, None, ALU.max))
                thus(V.reciprocal(rnorm[:], norm[:]))
                V.tensor_tensor(rqs[:], rnorm[:, 0], par["scale"], ALU.mult)
                for g in range(G):
                    ins = V.tensor_scalar(diag[:, g], ident[:], rnorm[:, 1, g:g + 1], None, ALU.mult)
                ins.then_inc(diag_ready, 1)
                dve.wait_ge(diag_ready, b + 1)
                dve.wait_ge(rk_copied, b + 1)
                for a in range(G):
                    cols = slice(WOFF[a], WOFF[a] + WIN[a][1] - WIN[a][0])
                    ins = V.scalar_tensor_tensor(out=scores[:, cols], in0=ps[:, 7, cols], scalar=rqs[:, a:a + 1],
                                                 in1=rk_row[:, WIN[a][0]:WIN[a][1]], op0=ALU.mult, op1=ALU.mult)
                thus(ins)
                thus(V.tensor_tensor(scores[:], scores[:], hmask[:], ALU.add))
                for a in range(G):
                    cols = slice(WOFF[a], WOFF[a] + WIN[a][1] - WIN[a][0])
                    ins = V.tensor_reduce(smx[:, a:a + 1], scores[:, cols], AX.X, ALU.max)
                thus(ins)
                V.tensor_scalar(smx[:], smx[:], -1.0, None, ALU.mult).then_inc(smx_ready, 1)
                dve.wait_ge(exp_done, b * 3 + 3)
                thus(V.reciprocal(rsum[:], ssum[:]))
                for a in range(G):
                    cols = slice(WOFF[a], WOFF[a] + WIN[a][1] - WIN[a][0])
                    ins = V.tensor_scalar(a_full[:, a, WIN[a][0]:WIN[a][1]], scores[:, cols], rsum[:, a:a + 1], None, ALU.mult)
                ins.then_inc(a_ready, 1)
                dve.wait_ge(a_ready, b + 1)
                dve.wait_ge(cm_ready, b + 1)
                V.tensor_tensor(a_cent, a_full, ps[:, 1:2, 0:C].broadcast_to([P, G, C]), ALU.subtract).then_inc(ac_ready, 1)

                def channel_moments(v, src, n):
                    dve.sem_inc(passed, 1)
                    for a in range(G):
                        ins = V.bn_aggr(aggr[:, v, a], src[:, a].rearrange("p t s -> p (t s)"))
                    thus(ins)
                    V.tensor_copy(gn_st[:, :, bass.ds(n, 1), 0], aggr[:, v, :, 0:1])
                    thus(V.tensor_tensor(gn_tmp[:, :, v], aggr[:, v, :, 0], aggr[:, v, :, 0], ALU.mult))
                    return V.tensor_tensor(gn_st[:, :, bass.ds(n, 1), 1], aggr[:, v, :, 1:2], gn_tmp[:, :, v:v + 1], ALU.add)

                def second(k, last):
                    for j in range(4):
                        T = b * T2 + k * 4 + j
                        dve.wait_ge(ostd_ready, T + 2)
                        V.reciprocal(rstd2[:, j % 2], std2[:, j % 2]).then_inc(orstd_ready, 1)
                        if not last_image:
                            dve.wait_ge(gx_in[j % 2], b * (8 * T2) + k * 32 + 16 * (j // 2 + 1))
                            dve.sem_inc(passed, 1)
                            for a in range(G):
                                ins = V.bn_stats(gnb[:, a, bass.ds(k * 4 + j, 1), :].rearrange("p a s -> p (a s)"),
                                                 gx[:, j % 2, a])
                            ins.then_inc(gx_used, 1)
                        if last and j == 3 and not last_image:
                            dve.wait_ge(gx_used, b * T2 + T2)
                            dve.sem_inc(passed, 1)
                            channel_moments(1, gnb, b + 1).then_inc(gst_ready, 1)
                        dve.wait_ge(obc_ready, T + 1)
                        dve.wait_ge(o_evicted, T + 3)
                        V.tensor_tensor(ow[:, j], ow[:, j], ps[:, 7:8, :].broadcast_to([P, G, TILE]), ALU.mult
                                        ).then_inc(on_done, 1)
                        dve.wait_ge(x2_in[j], b * (4 * T2) + k * 16 + 16)
                        dve.wait_ge(on_done, T + 5)
                        px = x2[:, j]
                        for a in range(G):
                            V.scalar_tensor_tensor(out=px[:, a], in0=px[:, a], scalar=par["ln2_b"][:, a:a + 1],
                                                   in1=ow[:, j, a], op0=ALU.add, op1=ALU.add).then_inc(x1_ready, 1)
                        if last and j == 3 and not last_image:
                            group_norm(b + 2, gn_r[:], gn_nb[:], thus)
                        dve.wait_ge(x1_ready, b * (3 * T2) + k * 12 + 3 * (j + 1))
                        dve.sem_inc(passed, 1)
                        for a in range(G):
                            V.bn_stats(bn2[:, a, bass.ds(k * 4 + j, 1), :].rearrange("p a s -> p (a s)"), px[:, a])
                        V.tensor_reduce(mx2[:, :, bass.ds(k * 4 + j, 1)], px, AX.X, ALU.max).then_inc(bn_done, 1)

                with dve.Fori(0, T2 // 4 - 1) as k:
                    second(k, False)
                second(T2 // 4 - 1, True)
                dve.wait_ge(bn_done, b * T2 + T2)
                dve.sem_inc(passed, 1)
                thus(V.tensor_reduce(ch_max[:, :, bass.ds(b, 1)], mx2, AX.X, ALU.max))
                ins = channel_moments(0, bn2, b)
                thus(ins)
                V.tensor_copy(ch_mean[:, :, bass.ds(b, 1)], aggr[:, 0, :, 0:1]).then_inc(batch_done, 1)
                if not last_image:
                    assert step[0] == SMALL, step[0]

            images(dve, image)

            dve.wait_ge(batch_done, B)
            dve.sem_inc(gst_ready, 1)
            r2, nb2, zr, znb, yr, ynb = (l1v[:, i] for i in range(8, 14))
            wdiv, iwdiv, hi, lo, sigma, isigma, bsig = (l1s[:, i] for i in range(2, 9))
            dve.sem_inc(wf_odd, 1)
            group_norm(B + 1, r2, nb2, then)
            then(V.tensor_tensor(pooled[0], ch_mean[:], r2, ALU.mult))
            then(V.tensor_tensor(pooled[0], pooled[0], nb2, ALU.add))
            then(V.tensor_tensor(pooled[1], ch_max[:], r2, ALU.mult))
            V.tensor_tensor(pooled[1], pooled[1], nb2, ALU.add).then_inc(pool_ready, 1)
            dve.wait_ge(l1_in, 16 * 6)
            V.tensor_reduce(hi, wmx, AX.X, ALU.max)
            then(V.tensor_reduce(lo, wmx, AX.X, ALU.min))
            then(V.scalar_tensor_tensor(out=wdiv, in0=lo, scalar=-1.0, in1=hi, op0=ALU.mult, op1=ALU.max))
            then(V.tensor_scalar(wdiv, wdiv, MIN_W, 1 / W_TOP, ALU.max, ALU.mult))
            then(V.reciprocal(iwdiv, wdiv))
            for g in range(G):
                ins = V.tensor_scalar(diag[:, g], ident[:], iwdiv[:, g:g + 1], None, ALU.mult)
            ins.then_inc(diag_ready, 1)
            then(V.tensor_tensor(l1s[:, 1], par["b_avg"], par["b_max"], ALU.add))
            then(V.tensor_copy(band16, band))
            dve.wait_ge(wdiv_ready, 1)
            wky_c = wky[0:K7].rearrange("p (c k) -> p c k", k=K7)
            V.tensor_tensor(wky_c, wky_c, ps[0:K7, 0, 0:C].unsqueeze(2).broadcast_to([K7, C, K7]), ALU.mult).then_inc(wky_scaled, 1)
            V.tensor_copy(selk16[0:K7], selk[0:K7])
            dve.wait_ge(wky_scaled, 1)
            dve.wait_ge(wky_hi, 1)
            V.tensor_tensor(wky16[0:K7, 1], wky[0:K7], wky16[0:K7, 0], ALU.subtract).then_inc(wky_split, 1)
            dve.wait_ge(gate_ready, 1)
            V.tensor_tensor(l1v[:, 3], ps[:, 3, 0:B * G].rearrange("p (g b) -> p g b", b=B),
                            l1s[:, 1].unsqueeze(2).broadcast_to([P, G, B]), ALU.add).then_inc(gate_in, 1)
            dve.wait_ge(gelu_done, 1)
            dve.wait_ge(wnorm_done, 1)
            xw = l1v[:, 4]
            then(V.tensor_tensor(l1v[:, 7], xw, xw, ALU.mult))
            V.tensor_tensor(l1v[:, 5], l1v[:, 7], l1s[:, 0].unsqueeze(2).broadcast_to([P, G, B]), ALU.mult).then_inc(gx2_ready, 1)
            dve.wait_ge(gxm_ready, 1)
            then(V.tensor_scalar(mrow[:, 0], ps[:, 5, 0:B], EPS_NX, None, ALU.add))
            then(V.reciprocal(mrow[:, 1], mrow[:, 0]))
            then(V.tensor_tensor(l1v[:, 7], l1v[:, 6], mrow[:, 1:2].broadcast_to([P, G, B]), ALU.mult))
            then(V.tensor_tensor(l1v[:, 7], l1v[:, 7], xw, ALU.mult))
            then(V.tensor_tensor(l1v[:, 7], l1v[:, 7], par["gamma"].unsqueeze(2).broadcast_to([P, G, B]), ALU.mult))
            sv = l1v[:, 7]
            then(V.tensor_tensor(sv, sv, wdiv.unsqueeze(2).broadcast_to([P, G, B]), ALU.mult))
            V.tensor_reduce(hi, sv, AX.X, ALU.max)
            then(V.tensor_reduce(lo, sv, AX.X, ALU.min))
            then(V.scalar_tensor_tensor(out=sigma, in0=lo, scalar=-1.0, in1=hi, op0=ALU.mult, op1=ALU.max))
            then(V.tensor_scalar(sigma, sigma, MIN_S, 1 / S_TOP, ALU.max, ALU.mult))
            for g in range(G):
                ins = V.tensor_scalar(diag[:, g], ident[:], sigma[:, g:g + 1], None, ALU.mult)
            ins.then_inc(diag_ready, 1)
            then(V.reciprocal(isigma, sigma))
            then(V.tensor_tensor(sv, sv, isigma.unsqueeze(2).broadcast_to([P, G, B]), ALU.mult))
            then(V.tensor_tensor(bsig, par["beta"], isigma, ALU.mult))
            V.tensor_tensor(zr, sv, r2, ALU.mult)
            V.tensor_tensor(znb, sv, nb2, ALU.mult)
            V.tensor_tensor(yr, r2, bsig.unsqueeze(2).broadcast_to([P, G, B]), ALU.mult)
            then(V.tensor_tensor(ynb, nb2, bsig.unsqueeze(2).broadcast_to([P, G, B]), ALU.mult))
            for t in range(4 * G):
                v, g = t // G, t % G
                if t >= 2:
                    dve.wait_ge(chb_ready, t - 1)
                V.tensor_tensor(d4[:, t % 2], ident[:].unsqueeze(2).broadcast_to([P, P, B]),
                                (yr, ynb, zr, znb)[v][:, g:g + 1, :].broadcast_to([P, P, B]), ALU.mult).then_inc(d4_ready, 1)
            for t in range(1, 6 * K7, 2):
                dve.wait_ge(wf_ready, t + 1)
                V.tensor_copy(wf_out(t), wf_in(t)).then_inc(wf_odd, 1)
            dve.wait_ge(sig_set, 1)
            dve.wait_ge(chb_ready, 4 * G)
            dve.wait_ge(wnorm_done, 1)
            dve.wait_ge(wf_odd, 3 * K7 + 1)
            dve.wait_ge(wf_even, 3 * K7 + 1)
            dve.sem_inc(l1_ready, 1)
            dve.sem_inc(box_ready, 2)
            dve.sem_inc(og_ready, 2)
            for s in range(2):
                dve.sem_inc(og_stored[s], 16 * B)

            def add_x1(K, s, c, first_of_group, k):
                dve.wait_ge(conv_ready, K + 3)
                if first_of_group:
                    dve.wait_ge(og_stored[s], k * (16 * B) + 16 * B)
                V.scalar_tensor_tensor(out=og[:, s, :, c, :], in0=ps[:, c % 2, :].rearrange("p (b w) -> p b w", b=B),
                                       scalar=sig[:, bass.ds(K, 1)], in1=xg[:, s, :, c, :], op0=ALU.mult, op1=ALU.add
                                       ).then_inc(og_ready, 1)

            def prepare(K, c):
                y = ypad[:, c % 2]
                dve.wait_ge(conv_ready, K + 1)
                V.tensor_tensor(toep[:, c % 2].rearrange("p k (q r) -> p k q r", r=K7),
                                wfold[:, bass.ds(K, 1)].rearrange("p a k r -> p (a k) r").unsqueeze(2).broadcast_to([P, 2 * K7, FOLD, K7]),
                                band16.rearrange("p (q r) -> p q r", r=K7).unsqueeze(1).broadcast_to([P, 2 * K7, FOLD, K7]),
                                ALU.mult).then_inc(toep_ready, 1)
                dve.wait_ge(yz_ready, K + 1)
                V.tensor_tensor(zlo[:, c % 2, :, PAD:PAD + W], zfull[:, c % 2], zhi[:, c % 2, :, PAD:PAD + W], ALU.subtract
                                ).then_inc(zlo_ready, 1)
                V.tensor_tensor(s2[:, :, 0:XP - 1], y[:, :, 0:XP - 1], y[:, :, 1:XP], ALU.add).then_inc(box_step, 1)
                dve.wait_ge(box_step, K * 3 + 1)
                V.tensor_tensor(s4[:, :, 0:XP - 3], s2[:, :, 0:XP - 3], s2[:, :, 2:XP - 1], ALU.add).then_inc(box_step, 1)
                dve.wait_ge(box_step, K * 3 + 2)
                V.tensor_tensor(s6, s4[:, :, 0:W], s2[:, :, 4:W + 4], ALU.add).then_inc(box_step, 1)
                dve.wait_ge(box_step, K * 3 + 3)
                V.tensor_tensor(box[:, c % 2], s6, y[:, :, 6:W + 6], ALU.add).then_inc(box_ready, 1)

            def channels(k, last):
                for s in range(2):
                    for c in range(CG):
                        K = k * (2 * CG) + (CG * s + c)
                        if not (last and s == 1 and c == CG - 1):
                            prepare(K + 1, c + 1)
                        add_x1(K, s, c, c == 0, k)

            prepare(0, 0)
            with dve.Fori(0, NCG // 2 - 1) as k:
                channels(k, False)
            channels(NCG // 2 - 1, True)


_IN = ["x", "w_qkv", "dw_qkv", "chans", "w_avg", "w_max", "w_mix_ch", "w_mix_ky",
       "ident", "member", "headmask", "band", "sel", "to_row", "from_row"]


def kernel(**inputs):
    import concourse.bacc as bacc
    from concourse.bass_utils import run_bass_kernel_spmd

    def split(a):
        a = np.asarray(a)
        return np.moveaxis(a.reshape((G, P) + a.shape[1:]), 0, 1)

    i = {k: np.asarray(v) for k, v in inputs.items()}
    w = np.stack([i[f"L0_conv_w{q}"].T.reshape(C, G, P) for q in "qkv"], axis=2)
    dwt = np.stack([i[f"L0_conv_dw{q}"].reshape(G, P, 9) for q in "qkv"], axis=1)
    vectors = [i["L0_conv_ln1_w"], i["L0_conv_ln1_b"], i["L0_conv_ln2_w"], i["L0_conv_ln2_b"],
               np.repeat(i["L0_conv_scale"].reshape(HEADS), HEAD), i["L1_conv_b_avg"], i["L1_conv_b_max"],
               i["L1_conv_gamma"].reshape(C), i["L1_conv_beta"].reshape(C)]
    w_mix = i["L1_conv_w_mix"]

    c = np.arange(C)
    member = np.where(c[:, None] // GN_SIZE == c[None, :] // GN_SIZE, 1.0 / GN_SIZE, 0.0)
    headmask = np.concatenate(
        [np.where((P * a + np.arange(P))[:, None] // HEAD == np.arange(*WIN[a])[None, :] // HEAD, 0.0, -1e30)
         for a in range(G)], axis=1)
    p, j, r = np.arange(P), np.arange(BAND), np.arange(K7)
    band = np.where(np.abs(p[:, None] - j[None, :]) <= PAD, 1.0, 0.0)
    sel = np.where(((p[None, :] - r[:, None] + PAD) % K7)[None] == r[:, None, None], 1.0, 0.0)

    arrays = {
        "x": i["x"], "w_qkv": split(w.reshape(C, M9 * P)),
        "dw_qkv": dwt.reshape(M9, P, 9).transpose(1, 0, 2),
        "chans": np.stack([split(v) for v in vectors], axis=1),
        "w_avg": split(i["L1_conv_w_avg"].T), "w_max": split(i["L1_conv_w_max"].T),
        "w_mix_ch": split(w_mix), "w_mix_ky": w_mix.reshape(C, K7, K7).transpose(1, 0, 2).reshape(K7, C * K7),
        "ident": np.eye(P), "member": split(member), "headmask": headmask, "band": band, "sel": sel,
        "to_row": np.broadcast_to(np.eye(RB) / C, (P, RB, RB)),
        "from_row": np.broadcast_to(np.eye(RB)[:, :, None], (RB, RB, P)),
    }
    nc = bacc.Bacc("TRN2", target_bir_lowering=False, num_devices=1)
    given, args = {}, []
    for name in _IN:
        a = arrays[name]
        if name in ("ident", "member", "headmask", "band", "sel", "to_row", "from_row"):
            a = a.astype(np.float32)
        a = np.ascontiguousarray(a)
        given[f"in_{name}"] = a
        args.append(nc.dram_tensor(f"in_{name}", a.shape, mybir.dt.from_np(a.dtype), kind="ExternalInput").ap())
    out = nc.dram_tensor("out_0", (B, C, H, W), F32, kind="ExternalOutput").ap()
    build(nc, *args, out)
    r = run_bass_kernel_spmd(nc, [given], core_ids=[0])
    return r.results[0]["out_0"]
```
